# Optimizing a Trainium2 kernel written in Bass

```python
import numpy as np
import jax
import jax.numpy as jnp

def _softmax(x, axis=-1):
    return jax.nn.softmax(x, axis=axis)

def _gelu(x):
    return jax.nn.gelu(x, approximate=True)

def _silu(x):
    return jax.nn.silu(x)

def _sigmoid(x):
    return jax.nn.sigmoid(x)

def _layernorm(x, axis=-1, eps=1e-05):
    m = jnp.mean(x, axis=axis, keepdims=True)
    v = jnp.var(x, axis=axis, keepdims=True)
    return (x - m) / jnp.sqrt(v + eps)

def _scatter_add(tgt, idx, src, axis=0):
    return tgt.at[idx].add(src)

def _segment_sum(src, seg, n):
    return jax.ops.segment_sum(src, seg, n)
kernel_name = 'mk_adj_ffn_d2_adj_r2_cd8fbc'

def setup_inputs(seed: int=0):
    np.random.seed(seed)
    _w = jnp.asarray

    def _rec_inputs():
        import jax
        import jax.numpy as jnp
        _gk = jax.random.key(seed)
        x = 7.22e-05 + 1 * jax.random.normal(jax.random.fold_in(_gk, 1), (64, 128, 128), jnp.float32)
        _w = (1.0 + jnp.arange(128, dtype=jnp.float32)) ** (-0.5)
        _w = _w / _w.mean()
        _pij = jnp.clip(0.015625 * _w[:, None] * _w[None, :], 0.0, 1.0)
        _a = jax.random.uniform(jax.random.fold_in(_gk, 2), (64, 128, 128)) < _pij
        _a = jnp.logical_or(_a, jnp.swapaxes(_a, -1, -2))
        _a = jnp.logical_or(_a, jnp.eye(128, dtype=bool))
        _af = _a.astype(jnp.float32)
        adj = _af
        return (x, adj)
    x, adj = _rec_inputs()

    def _L0_gnn_setup():
        import jax, jax.numpy as jnp
        import numpy as np
        from jax import lax
        DIM = 128
        EPS = 1e-05

        def _bn(h, g, b, m, v):
            scale = g / jnp.sqrt(v + EPS)
            return h * scale[None, :, None] + (b - m * scale)[None, :, None]

        def _conv1d(h, w, pad):
            return lax.conv_general_dilated(h, w, window_strides=(1,), padding=[(pad, pad)], dimension_numbers=('NCH', 'OIH', 'NCH'))
        key = jax.random.key(seed)
        ks = jax.random.split(key, 16)
        bs, n, d = (16, 1024, DIM)
        s = 0.05
        return {'x': jax.random.normal(ks[0], (bs, n, d), jnp.float32), 'mask': jnp.ones((bs, n, n), jnp.float32), 'w_se': jax.random.normal(ks[1], (3, d), jnp.float32) * s, 'b_se': jnp.zeros((3,), jnp.float32), 'conv1_w': jax.random.normal(ks[2], (d, d, 1), jnp.float32) * s, 'bn1_g': jnp.ones((d,), jnp.float32), 'bn1_b': jnp.zeros((d,), jnp.float32), 'bn1_m': jnp.zeros((d,), jnp.float32), 'bn1_v': jnp.ones((d,), jnp.float32), 'conv2_w': jax.random.normal(ks[3], (d, d, 17), jnp.float32) * s, 'bn2_g': jnp.ones((d,), jnp.float32), 'bn2_b': jnp.zeros((d,), jnp.float32), 'bn2_m': jnp.zeros((d,), jnp.float32), 'bn2_v': jnp.ones((d,), jnp.float32), 'w_msg': jax.random.normal(ks[4], (d, d), jnp.float32) * s, 'b_msg': jnp.zeros((d,), jnp.float32), 'w_ih': jax.random.normal(ks[5], (3 * d, 2 * d), jnp.float32) * s, 'b_ih': jnp.zeros((3 * d,), jnp.float32), 'w_hh': jax.random.normal(ks[6], (3 * d, d), jnp.float32) * s, 'b_hh': jnp.zeros((3 * d,), jnp.float32)}
    _L0_gnn_all = _L0_gnn_setup()
    _L0_gnn_in = {k: v for k, v in _L0_gnn_all.items() if k in ('w_se', 'b_se', 'conv1_w', 'bn1_g', 'bn1_b', 'bn1_m', 'bn1_v', 'conv2_w', 'bn2_g', 'bn2_b', 'bn2_m', 'bn2_v', 'w_msg', 'b_msg', 'w_ih', 'b_ih', 'w_hh', 'b_hh')}
    del _L0_gnn_all

    def _L0_ffn_setup():
        import jax, jax.numpy as jnp
        import numpy as np
        E = 8
        K = 2
        D = 128
        H = 256
        DOUT = 128
        EPS = 1e-05
        key = jax.random.key(seed)
        ks = jax.random.split(key, 9)
        s = 0.02
        return {'x': jax.random.normal(ks[0], (4, 4096, D), jnp.float32), 'gamma': 1.0 + 0.05 * jax.random.normal(ks[1], (D,), jnp.float32), 'beta': 0.05 * jax.random.normal(ks[2], (D,), jnp.float32), 'Wr': 0.01 * jax.random.normal(ks[3], (D, E), jnp.float32), 'br': jnp.zeros((E,), jnp.float32), 'W1': s * jax.random.normal(ks[4], (E, D, H), jnp.float32), 'b1': s * jax.random.normal(ks[5], (E, H), jnp.float32), 'W2': s * jax.random.normal(ks[6], (E, H, DOUT), jnp.float32), 'b2': s * jax.random.normal(ks[7], (E, DOUT), jnp.float32)}
    _L0_ffn_all = _L0_ffn_setup()
    _L0_ffn_in = {k: v for k, v in _L0_ffn_all.items() if k in ('gamma', 'beta', 'Wr', 'br', 'W1', 'b1', 'W2', 'b2')}
    del _L0_ffn_all

    def _L1_gnn_setup():
        import math
        import jax, jax.numpy as jnp
        import numpy as np
        B, N, D, H = (32, 256, 128, 8)
        HD = D // H
        key = jax.random.key(seed)
        ks = jax.random.split(key, 9)
        h = jax.random.normal(ks[0], (B, N, D), dtype=jnp.float32)
        edge = jax.random.normal(ks[1], (B, N, N), dtype=jnp.float32)
        adj = jax.random.uniform(ks[2], (B, N, N)) < 0.5
        adj_mask = adj | jnp.eye(N, dtype=bool)[None]
        s = 1.0 / math.sqrt(D)
        W_q = jax.random.normal(ks[3], (D, D), dtype=jnp.float32) * s
        W_k = jax.random.normal(ks[4], (D, D), dtype=jnp.float32) * s
        W_v = jax.random.normal(ks[5], (D, D), dtype=jnp.float32) * s
        W_e = jax.random.normal(ks[6], (H, 1), dtype=jnp.float32)
        W_o = jax.random.normal(ks[7], (D, D), dtype=jnp.float32) * s
        return {'h': h, 'edge': edge, 'adj_mask': adj_mask, 'W_q': W_q, 'W_k': W_k, 'W_v': W_v, 'W_e': W_e, 'W_o': W_o}
    _L1_gnn_all = _L1_gnn_setup()
    _L1_gnn_in = {k: v for k, v in _L1_gnn_all.items() if k in ('W_q', 'W_k', 'W_v', 'W_e', 'W_o')}
    del _L1_gnn_all

    def _L1_ffn_setup():
        import jax, jax.numpy as jnp
        import numpy as np
        B, T, C = (64, 192, 128)
        NH, NKV = (4, 2)
        HD = C // NH
        NREP = NH // NKV
        NE, TOPK = (8, 2)
        HID = int(8 / 3 * C)
        EPS_RMS = 1e-06

        def _rope_tables(t_len):
            inv_freq = 1.0 / 10000.0 ** (np.arange(0, HD, 2, dtype=np.float32) / HD)
            t = np.arange(t_len, dtype=np.float32)
            freqs = np.outer(t, inv_freq)
            emb = np.concatenate([freqs, freqs], axis=-1)
            return (jnp.asarray(np.cos(emb)), jnp.asarray(np.sin(emb)))

        def _rotate_half(x):
            h = x.shape[-1] // 2
            return jnp.concatenate([-x[..., h:], x[..., :h]], axis=-1)

        def _rmsnorm(v, w):
            return v * jax.lax.rsqrt(jnp.mean(v * v, axis=-1, keepdims=True) + EPS_RMS) * w
        key = jax.random.key(seed)
        ks = jax.random.split(key, 10)
        s = lambda k, shape: jax.random.normal(k, shape, jnp.float32) * 0.02
        return {'x': jax.random.normal(ks[0], (B, T, C), jnp.float32), 'ln1_w': jnp.ones((C,), jnp.float32), 'ln2_w': jnp.ones((C,), jnp.float32), 'wq': s(ks[1], (NH * HD, C)), 'wk': s(ks[2], (NKV * HD, C)), 'wv': s(ks[3], (NKV * HD, C)), 'wo': s(ks[4], (C, C)), 'router_w': s(ks[5], (NE, C)), 'w1': s(ks[6], (NE, HID, C)), 'w2': s(ks[7], (NE, C, HID)), 'w3': s(ks[8], (NE, HID, C))}
    _L1_ffn_all = _L1_ffn_setup()
    _L1_ffn_in = {k: v for k, v in _L1_ffn_all.items() if k in ('ln1_w', 'ln2_w', 'wq', 'wk', 'wv', 'wo', 'router_w', 'w1', 'w2', 'w3')}
    del _L1_ffn_all
    return {'x': x, 'adj': adj, 'L0_gnn_w_se': _L0_gnn_in['w_se'], 'L0_gnn_b_se': _L0_gnn_in['b_se'], 'L0_gnn_conv1_w': _L0_gnn_in['conv1_w'], 'L0_gnn_bn1_g': _L0_gnn_in['bn1_g'], 'L0_gnn_bn1_b': _L0_gnn_in['bn1_b'], 'L0_gnn_bn1_m': _L0_gnn_in['bn1_m'], 'L0_gnn_bn1_v': _L0_gnn_in['bn1_v'], 'L0_gnn_conv2_w': _L0_gnn_in['conv2_w'], 'L0_gnn_bn2_g': _L0_gnn_in['bn2_g'], 'L0_gnn_bn2_b': _L0_gnn_in['bn2_b'], 'L0_gnn_bn2_m': _L0_gnn_in['bn2_m'], 'L0_gnn_bn2_v': _L0_gnn_in['bn2_v'], 'L0_gnn_w_msg': _L0_gnn_in['w_msg'], 'L0_gnn_b_msg': _L0_gnn_in['b_msg'], 'L0_gnn_w_ih': _L0_gnn_in['w_ih'], 'L0_gnn_b_ih': _L0_gnn_in['b_ih'], 'L0_gnn_w_hh': _L0_gnn_in['w_hh'], 'L0_gnn_b_hh': _L0_gnn_in['b_hh'], 'L0_ffn_gamma': _L0_ffn_in['gamma'], 'L0_ffn_beta': _L0_ffn_in['beta'], 'L0_ffn_Wr': _L0_ffn_in['Wr'], 'L0_ffn_br': _L0_ffn_in['br'], 'L0_ffn_W1': _L0_ffn_in['W1'], 'L0_ffn_b1': _L0_ffn_in['b1'], 'L0_ffn_W2': _L0_ffn_in['W2'], 'L0_ffn_b2': _L0_ffn_in['b2'], 'L1_gnn_W_q': _L1_gnn_in['W_q'], 'L1_gnn_W_k': _L1_gnn_in['W_k'], 'L1_gnn_W_v': _L1_gnn_in['W_v'], 'L1_gnn_W_e': _L1_gnn_in['W_e'], 'L1_gnn_W_o': _L1_gnn_in['W_o'], 'L1_ffn_ln1_w': _L1_ffn_in['ln1_w'], 'L1_ffn_ln2_w': _L1_ffn_in['ln2_w'], 'L1_ffn_wq': _L1_ffn_in['wq'], 'L1_ffn_wk': _L1_ffn_in['wk'], 'L1_ffn_wv': _L1_ffn_in['wv'], 'L1_ffn_wo': _L1_ffn_in['wo'], 'L1_ffn_router_w': _L1_ffn_in['router_w'], 'L1_ffn_w1': _L1_ffn_in['w1'], 'L1_ffn_w2': _L1_ffn_in['w2'], 'L1_ffn_w3': _L1_ffn_in['w3']}

def reference(x, adj, L0_gnn_w_se, L0_gnn_b_se, L0_gnn_conv1_w, L0_gnn_bn1_g, L0_gnn_bn1_b, L0_gnn_bn1_m, L0_gnn_bn1_v, L0_gnn_conv2_w, L0_gnn_bn2_g, L0_gnn_bn2_b, L0_gnn_bn2_m, L0_gnn_bn2_v, L0_gnn_w_msg, L0_gnn_b_msg, L0_gnn_w_ih, L0_gnn_b_ih, L0_gnn_w_hh, L0_gnn_b_hh, L0_ffn_gamma, L0_ffn_beta, L0_ffn_Wr, L0_ffn_br, L0_ffn_W1, L0_ffn_b1, L0_ffn_W2, L0_ffn_b2, L1_gnn_W_q, L1_gnn_W_k, L1_gnn_W_v, L1_gnn_W_e, L1_gnn_W_o, L1_ffn_ln1_w, L1_ffn_ln2_w, L1_ffn_wq, L1_ffn_wk, L1_ffn_wv, L1_ffn_wo, L1_ffn_router_w, L1_ffn_w1, L1_ffn_w2, L1_ffn_w3):
    import jax
    import jax.numpy as jnp

    def _L0_gnn_ref(x, mask, w_se, b_se, conv1_w, bn1_g, bn1_b, bn1_m, bn1_v, conv2_w, bn2_g, bn2_b, bn2_m, bn2_v, w_msg, b_msg, w_ih, b_ih, w_hh, b_hh):
        import jax, jax.numpy as jnp
        import numpy as np
        from jax import lax
        DIM = 128
        EPS = 1e-05

        def _bn(h, g, b, m, v):
            scale = g / jnp.sqrt(v + EPS)
            return h * scale[None, :, None] + (b - m * scale)[None, :, None]

        def _conv1d(h, w, pad):
            return lax.conv_general_dilated(h, w, window_strides=(1,), padding=[(pad, pad)], dimension_numbers=('NCH', 'OIH', 'NCH'))
        d = x.shape[-1]
        xc = jnp.transpose(x, (0, 2, 1))
        h = _bn(_conv1d(xc, conv1_w, 0), bn1_g, bn1_b, bn1_m, bn1_v)
        h = jax.nn.relu(h)
        h = _bn(_conv1d(h, conv2_w, 8), bn2_g, bn2_b, bn2_m, bn2_v)
        x_conv = jnp.transpose(jax.nn.relu(h + xc), (0, 2, 1))
        s = x @ w_se.T + b_se
        sq = jnp.sum(s * s, axis=-1)
        dist = sq[:, :, None] + sq[:, None, :] - 2.0 * jnp.einsum('bnd,bmd->bnm', s, s)
        A = jnp.exp(-dist) * mask
        msg = jax.nn.relu(x @ w_msg.T + b_msg)
        x_nmp = jnp.einsum('bnm,bmd->bnd', A, msg)
        x_in = jnp.concatenate([x_conv, x_nmp], axis=-1)
        gi = x_in @ w_ih.T + b_ih
        gh = x @ w_hh.T + b_hh
        gi_r, gi_z, gi_n = (gi[..., :d], gi[..., d:2 * d], gi[..., 2 * d:])
        gh_r, gh_z, gh_n = (gh[..., :d], gh[..., d:2 * d], gh[..., 2 * d:])
        r = jax.nn.sigmoid(gi_r + gh_r)
        z = jax.nn.sigmoid(gi_z + gh_z)
        nn_ = jnp.tanh(gi_n + r * gh_n)
        return (1.0 - z) * nn_ + z * x

    def _L0_ffn_ref(x, gamma, beta, Wr, br, W1, b1, W2, b2):
        import jax, jax.numpy as jnp
        import numpy as np
        E = 8
        K = 2
        D = 128
        H = 256
        DOUT = 128
        EPS = 1e-05
        mu = jnp.mean(x, axis=-1, keepdims=True)
        var = jnp.mean(jnp.square(x - mu), axis=-1, keepdims=True)
        xn = (x - mu) * jax.lax.rsqrt(var + EPS) * gamma + beta
        logits = jnp.einsum('bsd,de->bse', xn, Wr) + br
        top_vals, top_idx = jax.lax.top_k(logits, K)
        w = jax.nn.softmax(top_vals, axis=-1)
        w_full = jnp.einsum('bsk,bske->bse', w, jax.nn.one_hot(top_idx, E, dtype=w.dtype))
        y = jnp.zeros(x.shape[:-1] + (DOUT,), x.dtype)
        for e in range(E):
            h = jax.nn.gelu(jnp.einsum('bsd,dh->bsh', xn, W1[e]) + b1[e], approximate=False)
            y_e = jnp.einsum('bsh,hd->bsd', h, W2[e]) + b2[e]
            y = y + y_e * w_full[..., e, None]
        return y

    def _L1_gnn_ref(h, edge, adj_mask, W_q, W_k, W_v, W_e, W_o):
        import math
        import jax, jax.numpy as jnp
        import numpy as np
        B, N, D, H = (32, 256, 128, 8)
        HD = D // H
        b, n, _ = h.shape
        q = (h @ W_q.T).reshape(b, n, H, HD).transpose(0, 2, 1, 3)
        k = (h @ W_k.T).reshape(b, n, H, HD).transpose(0, 2, 1, 3)
        v = (h @ W_v.T).reshape(b, n, H, HD).transpose(0, 2, 1, 3)
        edge_bias = jnp.einsum('bij,h->bhij', edge, W_e[:, 0])
        scores = jnp.einsum('bhid,bhjd->bhij', q, k) / math.sqrt(HD) + edge_bias
        scores = jnp.where(adj_mask[:, None], scores, -jnp.inf)
        attn = jax.nn.softmax(scores, axis=-1)
        out = jnp.einsum('bhij,bhjd->bhid', attn, v)
        out = out.transpose(0, 2, 1, 3).reshape(b, n, D)
        return out @ W_o.T

    def _L1_ffn_ref(x, ln1_w, ln2_w, wq, wk, wv, wo, router_w, w1, w2, w3):
        import jax, jax.numpy as jnp
        import numpy as np
        B, T, C = (64, 192, 128)
        NH, NKV = (4, 2)
        HD = C // NH
        NREP = NH // NKV
        NE, TOPK = (8, 2)
        HID = int(8 / 3 * C)
        EPS_RMS = 1e-06

        def _rope_tables(t_len):
            inv_freq = 1.0 / 10000.0 ** (np.arange(0, HD, 2, dtype=np.float32) / HD)
            t = np.arange(t_len, dtype=np.float32)
            freqs = np.outer(t, inv_freq)
            emb = np.concatenate([freqs, freqs], axis=-1)
            return (jnp.asarray(np.cos(emb)), jnp.asarray(np.sin(emb)))

        def _rotate_half(x):
            h = x.shape[-1] // 2
            return jnp.concatenate([-x[..., h:], x[..., :h]], axis=-1)

        def _rmsnorm(v, w):
            return v * jax.lax.rsqrt(jnp.mean(v * v, axis=-1, keepdims=True) + EPS_RMS) * w
        Bx, Tx, Cx = x.shape
        h = _rmsnorm(x, ln1_w)
        q = (h @ wq.T).reshape(Bx, Tx, NH, HD).transpose(0, 2, 1, 3)
        k = (h @ wk.T).reshape(Bx, Tx, NKV, HD).transpose(0, 2, 1, 3)
        v = (h @ wv.T).reshape(Bx, Tx, NKV, HD).transpose(0, 2, 1, 3)
        cos, sin = _rope_tables(Tx)
        cos, sin = (cos[None, None], sin[None, None])
        q = q * cos + _rotate_half(q) * sin
        k = k * cos + _rotate_half(k) * sin
        k = jnp.repeat(k, NREP, axis=1)
        v = jnp.repeat(v, NREP, axis=1)
        scores = jnp.einsum('bhtd,bhsd->bhts', q, k) / jnp.sqrt(jnp.float32(HD))
        causal = jnp.tril(jnp.ones((Tx, Tx), dtype=bool))
        scores = jnp.where(causal[None, None], scores, jnp.float32(-1e+30))
        att = jax.nn.softmax(scores, axis=-1)
        y = jnp.einsum('bhts,bhsd->bhtd', att, v).transpose(0, 2, 1, 3).reshape(Bx, Tx, Cx)
        x = x + y @ wo.T
        flat = _rmsnorm(x, ln2_w).reshape(-1, Cx)
        probs = jax.nn.softmax(flat @ router_w.T, axis=-1)
        tp, ti = jax.lax.top_k(probs, TOPK)
        tp = tp / (jnp.sum(tp, axis=-1, keepdims=True) + 1e-09)
        weights = jnp.sum(tp[..., None] * jax.nn.one_hot(ti, NE, dtype=flat.dtype), axis=1)
        out = jnp.zeros_like(flat)
        for e in range(NE):
            hh = jax.nn.silu(flat @ w1[e].T) * (flat @ w3[e].T)
            out = out + weights[:, e:e + 1] * (hh @ w2[e].T)
        return x + out.reshape(Bx, Tx, Cx)
    x = x + _L0_gnn_ref(_layernorm(x, axis=-1), adj, L0_gnn_w_se, L0_gnn_b_se, L0_gnn_conv1_w, L0_gnn_bn1_g, L0_gnn_bn1_b, L0_gnn_bn1_m, L0_gnn_bn1_v, L0_gnn_conv2_w, L0_gnn_bn2_g, L0_gnn_bn2_b, L0_gnn_bn2_m, L0_gnn_bn2_v, L0_gnn_w_msg, L0_gnn_b_msg, L0_gnn_w_ih, L0_gnn_b_ih, L0_gnn_w_hh, L0_gnn_b_hh)
    x = x + _L0_ffn_ref(_layernorm(x, axis=-1), L0_ffn_gamma, L0_ffn_beta, L0_ffn_Wr, L0_ffn_br, L0_ffn_W1, L0_ffn_b1, L0_ffn_W2, L0_ffn_b2)
    x = x + _L1_gnn_ref(_layernorm(x, axis=-1), adj, adj, L1_gnn_W_q, L1_gnn_W_k, L1_gnn_W_v, L1_gnn_W_e, L1_gnn_W_o)
    x = x + _L1_ffn_ref(_layernorm(x, axis=-1), L1_ffn_ln1_w, L1_ffn_ln2_w, L1_ffn_wq, L1_ffn_wk, L1_ffn_wv, L1_ffn_wo, L1_ffn_router_w, L1_ffn_w1, L1_ffn_w2, L1_ffn_w3)
    return x

_drawn_inputs = setup_inputs


def setup_inputs(seed=0):
    import zlib

    import numpy as np

    out = dict(_drawn_inputs(seed))
    spreads = {'L0_gnn_b_se': (0.0, 0.8),
     'L0_gnn_bn1_g': (1.0, 0.6),
     'L0_gnn_bn1_b': (0.0, 0.425),
     'L0_gnn_bn1_m': (0.0, 0.392),
     'L0_gnn_bn1_v': (1.0, 0.6),
     'L0_gnn_bn2_g': (1.0, 0.562),
     'L0_gnn_bn2_b': (0.0, 0.635),
     'L0_gnn_bn2_m': (0.0, 0.599),
     'L0_gnn_bn2_v': (1.0, 0.6),
     'L0_gnn_b_msg': (0.0, 0.327),
     'L0_gnn_b_ih': (0.0, 0.1),
     'L0_gnn_b_hh': (0.0, 0.338),
     'L0_ffn_br': (0.0, 0.371),
     'L1_ffn_ln1_w': (1.0, 0.6),
     'L1_ffn_ln2_w': (1.0, 0.6)}
    factors = {'L0_ffn_gamma': 8.0,
     'L0_ffn_beta': 8.0,
     'L0_ffn_Wr': 4.874,
     'L0_ffn_W1': 3.193,
     'L0_ffn_b1': 8.0,
     'L0_ffn_W2': 3.133,
     'L0_ffn_b2': 5.604,
     'L1_gnn_W_e': 8.0,
     'L1_ffn_wq': 8.0,
     'L1_ffn_wk': 8.0,
     'L1_ffn_wv': 8.0,
     'L1_ffn_wo': 8.0,
     'L1_ffn_router_w': 8.0,
     'L1_ffn_w1': 8.0,
     'L1_ffn_w2': 8.0,
     'L1_ffn_w3': 8.0}
    for name, (base, spread) in spreads.items():
        noise = np.random.default_rng([zlib.crc32(name.encode()), seed]).standard_normal(out[name].shape)
        drawn = base * np.exp(spread * noise) if base else spread * noise
        out[name] = jnp.asarray(drawn.astype(out[name].dtype))
    for name, factor in factors.items():
        out[name] = (out[name] * factor).astype(out[name].dtype)
    return out
```

```python
from contextlib import ExitStack

import numpy as np

import concourse.bass as bass
from concourse import mybir

F32 = mybir.dt.float32
F32R = mybir.dt.float32r
BF16 = mybir.dt.bfloat16
ALU = mybir.AluOpType
ACT = mybir.ActivationFunctionType
AX = mybir.AxisListType

B, N, D = 64, 128, 128
GB = 4
NG = B // GB
W = GB * N
TAPS, PAD = 17, 8
E = 8
H0 = 256
HID = 341
HALL = E * HID
NT = (HALL + 127) // 128
NEG = -1e30
LN_EPS, RMS_EPS = 1e-5, 1e-6

COLS = ["bn1_g", "bn1_b", "bn1_m", "bn1_v", "bn2_g", "bn2_b", "bn2_m", "bn2_v",
        "bi_r", "bi_z", "bi_n", "bh_r", "bh_z", "bh_n", "gamma", "beta", "ln1", "ln2"]
COL = {n: i for i, n in enumerate(COLS)}
NCOL = len(COLS) + 2 * E


def over_groups(eng, step):
    step(0, 0)
    step(1, 1)
    with eng.Fori(2, NG - 3, 2) as g:
        step(g, 0)
        step(g + 1, 1)
    step(NG - 2, 0)
    step(NG - 1, 1)


def rise(g, k, per):
    return g * per + (k + 1)


def reached(g, k, per):
    return not isinstance(g, int) or g * per + k >= 0


def has(g):
    return not isinstance(g, int) or 0 <= g < NG


def clear_behind(nc, sg):
    def leave(failed, *_):
        if not failed:
            with nc.Block() as block:
                @block.gpsimd
                def _(p):
                    for sem in sg.values():
                        p.sem_clear(sem)

    return leave


def mm3(t, out, w_hi, w_lo, x_hi, x_lo, start=True, stop=True):
    t.matmul(out, w_hi, x_hi, start=start, stop=False)
    t.matmul(out, w_hi, x_lo, start=False, stop=False)
    return t.matmul(out, w_lo, x_hi, start=False, stop=stop)


def f(ap):
    return ap.bitcast(F32)


def four(ap):
    return ap.rearrange("p (b n) -> p b n", b=GB)


def along(ap, shape):
    return ap.unsqueeze(ap.ndim).to_broadcast(shape)


def layer_norm_stats(v, sg, x_sb, g, stats, mv):
    for b in range(GB):
        i = v.bn_stats(stats[:, b, 0:6], x_sb[:, bass.ds(GB * g + b, 1), :].rearrange("p a d -> p (a d)"))
    i.then_inc(sg["stats"], 1)
    m0, q0, m1, q1, msum, mdif, qsum = (stats[:, :, k] for k in (1, 2, 4, 5, 6, 7, 8))
    v.wait_ge(sg["stats"], g + 1)
    v.tensor_tensor(msum, m0, m1, ALU.add)
    v.tensor_tensor(mdif, m0, m1, ALU.subtract)
    v.tensor_tensor(qsum, q0, q1, ALU.add).then_inc(sg["pairs"], 1)
    v.wait_ge(sg["pairs"], g + 1)
    v.scalar_tensor_tensor(mdif, mdif, 0.25, mdif, ALU.mult, ALU.mult)
    v.tensor_scalar(mv[:, 0, :], msum, 0.5, None, ALU.mult).then_inc(sg["squared"], 1)
    v.wait_ge(sg["squared"], g + 1)
    v.scalar_tensor_tensor(mv[:, 1, :], qsum, 1.0 / D, mdif, ALU.mult, ALU.add).then_inc(sg["mean_var"], 1)


def normalise(v, x_sb, g, mv, rstd, xn):
    for b in range(GB):
        i = v.tensor_scalar(xn[:, b, :], x_sb[:, bass.ds(GB * g + b, 1), :].rearrange("p a d -> p (a d)"),
                            mv[:, 0, b:b + 1], rstd[:, b:b + 1], ALU.subtract, ALU.mult)
    return i


def layer0_gnn(nc, io, x_sb, c):
    with ExitStack() as ctx:
        def sb(name, shape, dt=F32):
            return ctx.enter_context(nc.sbuf_tensor("g0_" + name, shape, dt))

        bank = [ctx.enter_context(nc.psum_tensor(f"g0_bank{i}", [128, W], F32)) for i in range(8)]
        p_back, p_conv, p_s, p_adjT, p_msg, p_r, p_z, p_hn = bank
        p_front, p_dist = p_s, p_s
        p_nmp, p_in = p_adjT, p_msg

        adj = sb("adj", [128, 2, GB, N])
        conv2_raw = sb("conv2_raw", [128, TAPS * D])
        conv2_hi, conv2_lo = sb("conv2_hi", [128, TAPS * D], F32R), sb("conv2_lo", [128, TAPS * D], F32R)
        small_raw = sb("small_raw", [128, 10 * D])
        small_hi, small_lo = sb("small_hi", [128, 10 * D], F32R), sb("small_lo", [128, 10 * D], F32R)
        w_msg, b_msg = sb("w_msg", [128, D]), sb("b_msg", [128, D])
        w_se, b_se = sb("w_se", [128, 3]), sb("b_se", [3, 1])
        half3 = sb("half3", [3, W])
        affine = sb("affine", [128, 16])
        bn1_scale, bn1_shift, bn2_scale, bn2_shift = (affine[:, i:i + 1] for i in range(4))
        half_br, half_bz, half_bhn = (affine[:, i:i + 1] for i in range(4, 7))
        tmp = sb("tmp", [128, 2])
        stats, mv = sb("stats", [128, GB, 9]), sb("mv", [128, 2, GB])
        rstd = sb("rstd", [128, GB])
        xn = sb("xn", [128, GB, D])
        xc = sb("xc", [128, 2, W])
        xcb = sb("xcb", [128, 2, W])
        xc_hi, xc_lo = sb("xc_hi", [128, W], F32R), sb("xc_lo", [128, W], F32R)
        h1 = sb("h1", [128, W])
        h1_hi = sb("h1_hi", [128, GB, N + 2 * PAD], F32R)
        h1_lo = sb("h1_lo", [128, GB, N + 2 * PAD], F32R)
        s3, s3sq = sb("s3", [3, W]), sb("s3sq", [3, W])
        ex, am = sb("ex", [128, W]), sb("am", [128, W])
        msg_pre, msg = sb("msg_pre", [128, W]), sb("msg", [128, W])
        cv = sb("cv", [128, W])
        cv_hi, cv_lo = sb("cv_hi", [128, W], F32R), sb("cv_lo", [128, W], F32R)
        nmp_hi, nmp_lo = sb("nmp_hi", [128, W], F32R), sb("nmp_lo", [128, W], F32R)
        tr, tz = sb("tr", [128, W]), sb("tz", [128, W])
        hn, pre_n, nn = sb("hn", [128, W]), sb("pre_n", [128, W]), sb("nn", [128, W])
        dx, upd = sb("dx", [128, W]), sb("upd", [128, W])

        sg = {n: ctx.enter_context(nc.semaphore("g0_" + n)) for n in """weights input prep_pool prep_vec split stats pairs squared mean_var var_eps rstd xn
            xT xc xc_hi xc_lo xcb conv1 h1 h1_hi h1_lo s_out s3 s3sq msg_out msg_pre msg adjT am gates_x dist ex
            conv2 cv cv_hi cv_lo nmp nmp_hi nmp_lo gates tr tz hn rn pre_n nn dx zx upd upT added""".split()}
        ctx.push(clear_behind(nc, sg))
        block = ctx.enter_context(nc.Block())
        n_weights = 6

        @block.sync
        def _(q):
            q.dma_start(small_raw[:, :], io["small0"]).then_inc(sg["weights"], 16)
            q.dma_start(w_msg[:, :], io["w_msg"]).then_inc(sg["weights"], 16)
            q.dma_start(b_msg[:, :], io["b_msg"]).then_inc(sg["weights"], 16)
            q.dma_start(w_se[:, :], io["w_se"]).then_inc(sg["weights"], 16)
            q.dma_start(b_se[:, :], io["b_se"]).then_inc(sg["weights"], 16)
            q.dma_start(conv2_raw[:, :], io["conv2"]).then_inc(sg["weights"], 16)

            def step(g, par):
                if has(g - 2):
                    q.wait_ge(sg["adjT"], g - 1)
                if has(g - 1):
                    q.wait_ge(sg["input"], rise(g - 1, 31, 32))
                q.dma_start(x_sb[:, bass.ds(GB * g, GB), :],
                            io["x"][bass.ds(GB * g, GB), :, :].rearrange("b n d -> n b d")).then_inc(sg["input"], 16)
                q.dma_start(adj[:, par, :, :],
                            io["adj"][bass.ds(GB * g, GB), :, :].rearrange("b n m -> n b m")).then_inc(sg["input"], 16)

            over_groups(q, step)

        @block.tensor
        def _(t):
            def transpose_in(g):
                t.wait_ge(sg["xn"], g + 1)
                if has(g - 1):
                    t.wait_ge(sg["ex"], g)
                for b in range(GB):
                    i = t.transpose(p_front[:, bass.ts(b, N)], xn[:, b, :], c["ident"][:, :])
                i.then_inc(sg["xT"], 1)

            def transpose_back(g):
                t.wait_ge(sg["upd"], g + 1)
                if has(g - 1):
                    t.wait_ge(sg["added"], g)
                for b in range(GB):
                    i = t.transpose(p_back[:, bass.ts(b, N)], upd[:, bass.ts(b, N)], c["ident"][:, :])
                i.then_inc(sg["upT"], 1)

            def w(k):
                return small_hi[:, bass.ts(k, D)], small_lo[:, bass.ts(k, D)]

            def step(g, par):
                t.wait_ge(sg["xc_hi"], g + 1)
                t.wait_ge(sg["xc_lo"], g + 1)
                if has(g - 1):
                    t.wait_ge(sg["cv"], g)
                mm3(t, p_conv[:, :], *w(0), xc_hi[:, :], xc_lo[:, :]).then_inc(sg["conv1"], 1)
                t.matmul(p_s[0:3, :], w_se[:, :], xc[:, par, :], start=True, stop=True).then_inc(sg["s_out"], 1)
                if has(g - 1):
                    t.wait_ge(sg["nmp_lo"], g)
                t.wait_ge(sg["input"], rise(g, 31, 32))
                for b in range(GB):
                    i = t.transpose(p_adjT[:, bass.ts(b, N)], adj[:, par, b, :], c["ident"][:, :])
                i.then_inc(sg["adjT"], 1)
                if has(g - 1):
                    t.wait_ge(sg["pre_n"], g)
                if has(g - 1):
                    t.wait_ge(sg["hn"], g)
                if has(g - 1):
                    t.wait_ge(sg["tr"], g)
                if has(g - 1):
                    t.wait_ge(sg["tz"], g)
                for b in range(GB):
                    i = t.matmul(p_msg[:, bass.ts(b, N)], xc[:, par, bass.ts(b, N)], w_msg[:, :], start=True, stop=True)
                i.then_inc(sg["msg_out"], 1)
                mm3(t, p_r[:, :], *w(7), xc_hi[:, :], xc_lo[:, :], stop=False)
                mm3(t, p_z[:, :], *w(8), xc_hi[:, :], xc_lo[:, :], stop=False)
                mm3(t, p_hn[:, :], *w(9), xc_hi[:, :], xc_lo[:, :]).then_inc(sg["gates_x"], 1)
                t.wait_ge(sg["s3"], g + 1)
                t.wait_ge(sg["s3sq"], g + 1)
                for b in range(GB):
                    cols = bass.ts(b, N)
                    t.matmul(p_dist[:, cols], s3[:, cols], s3[:, cols], start=True, stop=False)
                    t.matmul(p_dist[:, cols], half3[:, cols], s3sq[:, cols], start=False, stop=False)
                    i = t.matmul(p_dist[:, cols], s3sq[:, cols], half3[:, cols], start=False, stop=True)
                i.then_inc(sg["dist"], 1)
                t.wait_ge(sg["h1_hi"], g + 1)
                t.wait_ge(sg["h1_lo"], g + 1)
                for k in range(TAPS):
                    i = mm3(t, four(p_conv[:, :]), conv2_hi[:, bass.ts(k, D)], conv2_lo[:, bass.ts(k, D)],
                            h1_hi[:, :, k:k + N], h1_lo[:, :, k:k + N], start=k == 0, stop=k == TAPS - 1)
                i.then_inc(sg["conv2"], 1)
                if has(g - 1):
                    transpose_back(g - 1)
                if has(g + 1):
                    transpose_in(g + 1)
                t.wait_ge(sg["msg"], g + 1)
                t.wait_ge(sg["am"], g + 1)
                for b in range(GB):
                    i = t.matmul(p_nmp[:, bass.ts(b, N)], msg[:, bass.ts(b, N)], am[:, bass.ts(b, N)],
                                 start=True, stop=True)
                i.then_inc(sg["nmp"], 1)
                t.wait_ge(sg["msg_pre"], g + 1)
                t.wait_ge(sg["cv_hi"], g + 1)
                t.wait_ge(sg["cv_lo"], g + 1)
                for k, out in enumerate((p_r, p_z, p_in)):
                    mm3(t, out[:, :], *w(1 + k), cv_hi[:, :], cv_lo[:, :], start=k == 2, stop=False)
                t.wait_ge(sg["nmp_hi"], g + 1)
                t.wait_ge(sg["nmp_lo"], g + 1)
                for k, out in enumerate((p_r, p_z, p_in)):
                    i = mm3(t, out[:, :], *w(4 + k), nmp_hi[:, :], nmp_lo[:, :], start=False)
                i.then_inc(sg["gates"], 1)

            t.wait_ge(sg["split"], 2)
            t.wait_ge(sg["weights"], 16 * n_weights)
            transpose_in(0)
            over_groups(t, step)
            transpose_back(NG - 1)

        @block.scalar
        def _(a):
            def evacuate_in(g, par):
                a.wait_ge(sg["xT"], g + 1)
                if has(g - 2):
                    a.wait_ge(sg["zx"], g - 1)
                if has(g - 2):
                    a.wait_ge(sg["dx"], g - 1)
                a.activation(xc[:, par, :], p_front[:, :], ACT.Copy).then_inc(sg["xc"], 1)
                if has(g - 1):
                    a.wait_ge(sg["gates_x"], g)
                a.activation(xc_hi[:, :], p_front[:, :], ACT.Copy).then_inc(sg["xc_hi"], 1)

            def gates(g):
                a.wait_ge(sg["gates"], g + 1)
                if has(g - 1):
                    a.wait_ge(sg["zx"], g)
                a.activation(tr[:, :], p_r[:, :], ACT.Tanh, bias=half_br, scale=0.5).then_inc(sg["tr"], 1)
                a.activation(tz[:, :], p_z[:, :], ACT.Tanh, bias=half_bz, scale=0.5).then_inc(sg["tz"], 1)

            def new(g):
                a.wait_ge(sg["pre_n"], g + 1)
                if has(g - 1):
                    a.wait_ge(sg["upd"], g)
                a.activation(nn[:, :], pre_n[:, :], ACT.Tanh, bias=c["col"]("bi_n")).then_inc(sg["nn"], 1)

            def step(g, par):
                if has(g - 1):
                    gates(g - 1)
                a.wait_ge(sg["conv1"], g + 1)
                if has(g - 1):
                    a.wait_ge(sg["h1_lo"], g)
                a.activation(h1[:, :], p_conv[:, :], ACT.Relu, bias=bn1_shift, scale=bn1_scale).then_inc(sg["h1"], 1)
                a.wait_ge(sg["h1"], g + 1)
                a.activation(h1_hi[:, :, PAD:PAD + N], four(h1[:, :]), ACT.Copy).then_inc(sg["h1_hi"], 1)
                a.wait_ge(sg["s_out"], g + 1)
                a.activation(s3[:, :], p_s[0:3, :], ACT.Identity, bias=b_se[:, :]).then_inc(sg["s3"], 1)
                a.activation(s3sq[:, :], p_s[0:3, :], ACT.Square, bias=b_se[:, :]).then_inc(sg["s3sq"], 1)
                if has(g - 1):
                    new(g - 1)
                a.wait_ge(sg["msg_pre"], g + 1)
                if has(g - 1):
                    a.wait_ge(sg["nmp"], g)
                a.activation(msg[:, :], msg_pre[:, :], ACT.Relu).then_inc(sg["msg"], 1)
                a.wait_ge(sg["dist"], g + 1)
                if has(g - 1):
                    a.wait_ge(sg["am"], g)
                a.activation(ex[:, :], p_dist[:, :], ACT.Exp, scale=2.0).then_inc(sg["ex"], 1)
                if has(g + 1):
                    evacuate_in(g + 1, 1 - par)
                a.wait_ge(sg["cv"], g + 1)
                a.activation(cv_hi[:, :], cv[:, :], ACT.Relu).then_inc(sg["cv_hi"], 1)
                a.wait_ge(sg["nmp"], g + 1)
                a.activation(nmp_hi[:, :], p_nmp[:, :], ACT.Copy).then_inc(sg["nmp_hi"], 1)

            a.wait_ge(sg["prep_vec"], 9)
            a.wait_ge(sg["weights"], 16 * n_weights)
            evacuate_in(0, 0)
            over_groups(a, step)
            gates(NG - 1)
            new(NG - 1)

        @block.vector
        def _(v):
            def split_in(g, par):
                v.wait_ge(sg["xc"], g + 1)
                v.wait_ge(sg["xc_hi"], g + 1)
                if has(g - 1):
                    v.wait_ge(sg["gates_x"], g)
                v.tensor_tensor(xc_lo[:, :], xc[:, par, :], f(xc_hi[:, :]), ALU.subtract).then_inc(sg["xc_lo"], 1)

            def front_stats(g):
                v.wait_ge(sg["input"], rise(g, 31, 32))
                layer_norm_stats(v, sg, x_sb, g, stats, mv)

            def front_norm(g):
                v.wait_ge(sg["mean_var"], g + 1)
                v.wait_ge(sg["rstd"], g + 1)
                if has(g - 1):
                    v.wait_ge(sg["xT"], g)
                normalise(v, x_sb, g, mv, rstd, xn).then_inc(sg["xn"], 1)

            def gru_gates(g):
                v.wait_ge(sg["gates"], g + 1)
                v.tensor_scalar(hn[:, :], p_hn[:, :], 0.5, half_bhn, ALU.mult, ALU.add).then_inc(sg["hn"], 1)
                v.wait_ge(sg["hn"], g + 1)
                v.wait_ge(sg["tr"], g + 1)
                v.scalar_tensor_tensor(pre_n[:, :], tr[:, :], 1.0, hn[:, :], ALU.add, ALU.mult).then_inc(sg["rn"], 1)
                v.wait_ge(sg["rn"], g + 1)
                v.tensor_tensor(pre_n[:, :], pre_n[:, :], p_in[:, :], ALU.add).then_inc(sg["pre_n"], 1)

            def gru_out(g):
                v.wait_ge(sg["dx"], g + 1)
                v.wait_ge(sg["tz"], g + 1)
                v.scalar_tensor_tensor(dx[:, :], tz[:, :], 1.0, dx[:, :], ALU.add, ALU.mult).then_inc(sg["zx"], 1)
                v.wait_ge(sg["zx"], g + 1)
                v.wait_ge(sg["nn"], g + 1)
                if has(g - 1):
                    v.wait_ge(sg["upT"], g)
                v.scalar_tensor_tensor(upd[:, :], dx[:, :], 0.5, nn[:, :], ALU.mult, ALU.add).then_inc(sg["upd"], 1)

            def add_back(g):
                v.wait_ge(sg["upT"], g + 1)
                xg = x_sb[:, bass.ds(GB * g, GB), :]
                v.tensor_tensor(xg, xg, four(p_back[:, :]), ALU.add).then_inc(sg["added"], 1)

            def step(g, par):
                if has(g - 1):
                    gru_gates(g - 1)
                v.wait_ge(sg["h1_hi"], g + 1)
                v.tensor_tensor(h1_lo[:, :, PAD:PAD + N], four(h1[:, :]), f(h1_hi[:, :, PAD:PAD + N]),
                                ALU.subtract).then_inc(sg["h1_lo"], 1)
                v.wait_ge(sg["msg_out"], g + 1)
                if has(g - 1):
                    v.wait_ge(sg["msg"], g)
                v.tensor_tensor(four(msg_pre[:, :]), four(p_msg[:, :]), b_msg[:, :].unsqueeze(1).to_broadcast([128, GB, D]),
                                ALU.add).then_inc(sg["msg_pre"], 1)
                if has(g - 1):
                    gru_out(g - 1)
                if has(g + 1):
                    front_stats(g + 1)
                v.wait_ge(sg["adjT"], g + 1)
                v.wait_ge(sg["ex"], g + 1)
                if has(g - 1):
                    v.wait_ge(sg["nmp"], g)
                v.tensor_tensor(am[:, :], ex[:, :], p_adjT[:, :], ALU.mult).then_inc(sg["am"], 1)
                if has(g + 1):
                    front_norm(g + 1)
                if has(g - 1):
                    add_back(g - 1)
                v.wait_ge(sg["conv2"], g + 1)
                v.wait_ge(sg["xcb"], g + 1)
                v.scalar_tensor_tensor(cv[:, :], p_conv[:, :], bn2_scale, xcb[:, par, :], ALU.mult,
                                       ALU.add).then_inc(sg["cv"], 1)
                v.wait_ge(sg["cv_hi"], g + 1)
                v.scalar_tensor_tensor(cv_lo[:, :], cv[:, :], 0.0, f(cv_hi[:, :]), ALU.max,
                                       ALU.subtract).then_inc(sg["cv_lo"], 1)
                v.wait_ge(sg["nmp_hi"], g + 1)
                v.tensor_tensor(nmp_lo[:, :], p_nmp[:, :], f(nmp_hi[:, :]), ALU.subtract).then_inc(sg["nmp_lo"], 1)
                if has(g + 1):
                    split_in(g + 1, 1 - par)

            v.memset(h1_hi[:, :, :].bitcast(F32), 0.0)
            v.memset(h1_lo[:, :, :].bitcast(F32), 0.0)
            v.memset(half3[:, :], -0.5).then_inc(sg["prep_vec"], 1)
            v.wait_ge(sg["weights"], 16 * n_weights)
            v.wait_ge(sg["prep_pool"], 2)
            v.tensor_tensor(bn1_scale, c["col"]("bn1_g"), tmp[:, 0:1], ALU.mult).then_inc(sg["prep_vec"], 1)
            v.tensor_tensor(bn2_scale, c["col"]("bn2_g"), tmp[:, 1:2], ALU.mult).then_inc(sg["prep_vec"], 1)
            v.wait_ge(sg["prep_vec"], 3)
            v.tensor_tensor(bn1_shift, c["col"]("bn1_m"), bn1_scale, ALU.mult)
            v.tensor_tensor(bn2_shift, c["col"]("bn2_m"), bn2_scale, ALU.mult).then_inc(sg["prep_vec"], 1)
            v.wait_ge(sg["prep_vec"], 4)
            v.tensor_tensor(bn1_shift, c["col"]("bn1_b"), bn1_shift, ALU.subtract)
            v.tensor_tensor(bn2_shift, c["col"]("bn2_b"), bn2_shift, ALU.subtract).then_inc(sg["prep_vec"], 1)
            v.tensor_tensor(half_br, c["col"]("bi_r"), c["col"]("bh_r"), ALU.add)
            v.tensor_tensor(half_bz, c["col"]("bi_z"), c["col"]("bh_z"), ALU.add).then_inc(sg["prep_vec"], 1)
            v.tensor_scalar(half_bhn, c["col"]("bh_n"), 0.5, None, ALU.mult).then_inc(sg["prep_vec"], 1)
            v.wait_ge(sg["prep_vec"], 7)
            v.tensor_scalar(half_br, half_br, 0.5, None, ALU.mult).then_inc(sg["prep_vec"], 1)
            v.tensor_scalar(half_bz, half_bz, 0.5, None, ALU.mult).then_inc(sg["prep_vec"], 1)
            v.tensor_copy(small_hi[:, :], small_raw[:, :])
            v.tensor_copy(conv2_hi[:, :], conv2_raw[:, :]).then_inc(sg["prep_vec"], 1)
            v.wait_ge(sg["prep_vec"], 10)
            v.tensor_tensor(small_lo[:, :], small_raw[:, :], f(small_hi[:, :]), ALU.subtract).then_inc(sg["split"], 1)
            v.tensor_tensor(conv2_lo[:, :], conv2_raw[:, :], f(conv2_hi[:, :]), ALU.subtract).then_inc(sg["split"], 1)
            front_stats(0)
            front_norm(0)
            split_in(0, 0)
            over_groups(v, step)
            gru_gates(NG - 1)
            gru_out(NG - 1)
            add_back(NG - 1)

        @block.gpsimd
        def _(p):
            def front(g):
                p.wait_ge(sg["mean_var"], g + 1)
                p.tensor_tensor(rstd[:, :], mv[:, 1, :], c["ln_eps"][:, 0:GB], ALU.add).then_inc(sg["var_eps"], 1)
                p.wait_ge(sg["var_eps"], g + 1)
                p.tensor_tensor(rstd[:, :], rstd[:, :], c["minus_half"][:, 0:GB], ALU.pow).then_inc(sg["rstd"], 1)

            def shifted(g, par):
                p.wait_ge(sg["xc"], g + 1)
                if has(g - 2):
                    p.wait_ge(sg["cv"], g - 1)
                p.tensor_tensor(xcb[:, par, :], xc[:, par, :], bn2_shift.to_broadcast([128, W]), ALU.add).then_inc(sg["xcb"], 1)

            def gru_diff(g, par):
                p.wait_ge(sg["nn"], g + 1)
                if has(g - 1):
                    p.wait_ge(sg["upd"], g)
                p.tensor_tensor(dx[:, :], xc[:, par, :], nn[:, :], ALU.subtract).then_inc(sg["dx"], 1)

            def step(g, par):
                if has(g - 1):
                    gru_diff(g - 1, 1 - par)
                if has(g + 1):
                    front(g + 1)
                    shifted(g + 1, 1 - par)

            p.tensor_scalar(tmp[:, 0:1], c["col"]("bn1_v"), LN_EPS, None, ALU.add)
            p.tensor_scalar(tmp[:, 1:2], c["col"]("bn2_v"), LN_EPS, None, ALU.add).then_inc(sg["prep_pool"], 1)
            p.wait_ge(sg["prep_pool"], 1)
            p.tensor_tensor(tmp[:, :], tmp[:, :], c["minus_half"][:, 0:2], ALU.pow).then_inc(sg["prep_pool"], 1)
            p.wait_ge(sg["prep_vec"], 5)
            front(0)
            shifted(0, 0)
            over_groups(p, step)
            gru_diff(NG - 1, 1)


def ranks(v, sem, g, base, per, logits, gt, eq, rank, tri):
    mine = logits.unsqueeze(3).to_broadcast([128, GB, E, E])
    other = logits.unsqueeze(2).to_broadcast([128, GB, E, E])
    v.tensor_tensor(gt, other, mine, ALU.is_gt)
    v.tensor_tensor(eq, other, mine, ALU.is_equal).then_inc(sem, 1)
    v.wait_ge(sem, rise(g, base, per))
    v.tensor_tensor(eq, eq, tri, ALU.mult).then_inc(sem, 1)
    v.wait_ge(sem, rise(g, base + 1, per))
    v.tensor_tensor(gt, gt, eq, ALU.add).then_inc(sem, 1)
    v.wait_ge(sem, rise(g, base + 2, per))
    v.tensor_reduce(rank, gt, AX.X, ALU.add).then_inc(sem, 1)


def layer0_ffn(nc, io, x_sb, c):
    with ExitStack() as ctx:
        def sb(name, shape, dt=F32):
            return ctx.enter_context(nc.sbuf_tensor("f0_" + name, shape, dt))

        bank = [ctx.enter_context(nc.psum_tensor(f"f0_bank{i}", [128, W], F32)) for i in range(8)]
        p_h, p_wb, p_y, p_front, p_back = bank[0:2], bank[2:4], bank[4:6], bank[6], bank[7]

        C = 2 * E
        LAG = 4
        RING = 8
        w1_raw, w2_raw = sb("w1_raw", [128, C * 128]), sb("w2_raw", [128, C * 128])
        w1_hi, w1_lo = sb("w1_hi", [128, C * 128], F32R), sb("w1_lo", [128, C * 128], F32R)
        w2_hi, w2_lo = sb("w2_hi", [128, C * 128], F32R), sb("w2_lo", [128, C * 128], F32R)
        b2_raw = sb("b2_raw", [2 * E, D])
        b2_hi, b2_lo = sb("b2_hi", [2 * E, D], F32R), sb("b2_lo", [2 * E, D], F32R)
        pick_raw, pick = sb("pick_raw", [2 * E, E * 128]), sb("pick", [2 * E, E * 128], F32R)
        w_route, b_route, tri = sb("w_route", [128, E]), sb("b_route", [128, E]), sb("tri", [128, E * E])
        stats, mv, rstd = sb("stats", [128, GB, 9]), sb("mv", [128, 2, GB]), sb("rstd", [128, 4, GB])
        xn = sb("xn", [128, GB, D])
        xc = sb("xc", [128, W])
        xc_hi, xc_lo = sb("xc_hi", [128, 2, W], F32R), sb("xc_lo", [128, 2, W], F32R)
        logits = sb("logits", [128, GB, E])
        gt, eq = sb("gt", [128, GB, E, E]), sb("eq", [128, GB, E, E])
        rank, first, second = sb("rank", [128, GB, E]), sb("first", [128, GB, E]), sb("second", [128, GB, E])
        dif, both, prod = sb("dif", [128, GB, E]), sb("both", [128, GB, E]), sb("prod", [128, GB, E])
        gap, tanh_gap = sb("gap", [128, GB]), sb("tanh_gap", [128, GB])
        w_cat = sb("w_cat", [128, GB, 2 * E], F32R)
        wT = sb("wT", [2 * E, 2, W], F32R)
        h, hw = sb("h", [128, 2, W]), sb("hw", [128, 4, W])
        h_hi, h_lo = sb("h_hi", [128, RING, W], F32R), sb("h_lo", [128, RING, W], F32R)
        y = sb("y", [128, W])

        sg = {n: ctx.enter_context(nc.semaphore("f0_" + n)) for n in """weights hi split stats pairs squared mean_var rstd_step xn xT xc xc_hi xc_lo
            logits_out logits route gap tanh_gap w_cat wT_out wT wb h_out h hw h_hi h_lo y_out y yT added""".split()}
        ctx.push(clear_behind(nc, sg))
        block = ctx.enter_context(nc.Block())
        RSTD = 7
        ROUTE = 10

        @block.sync
        def _(q):
            for dst, src in ((w1_raw, io["w1_0"]), (w2_raw, io["w2_0"]), (b2_raw, io["b2_0"]), (pick_raw, io["pick_0"]),
                             (w_route, io["w_route0"]), (b_route, io["b_route0"]), (tri, io["tri"])):
                q.dma_start(dst[:, :], src).then_inc(sg["weights"], 16)
            q.wait_ge(sg["weights"], 16 * 7)

        @block.tensor
        def _(t):
            def transpose_in(g):
                t.wait_ge(sg["xn"], g + 1)
                if has(g - 1):
                    t.wait_ge(sg["wT"], g)
                for b in range(GB):
                    i = t.transpose(p_front[:, bass.ts(b, N)], xn[:, b, :], c["ident"][:, :])
                i.then_inc(sg["xT"], 1)

            def route(g):
                t.wait_ge(sg["xc"], g + 1)
                t.wait_ge(sg["xc_hi"], g + 1)
                for b in range(GB):
                    i = t.matmul(p_front[:, b * E:(b + 1) * E], xc[:, bass.ts(b, N)], w_route[:, :], start=True, stop=True)
                i.then_inc(sg["logits_out"], 1)

            def weights_in(g):
                t.wait_ge(sg["w_cat"], g + 1)
                t.wait_ge(sg["logits"], g + 1)
                for b in range(GB):
                    i = t.transpose(p_front[0:2 * E, bass.ts(b, N)], f(w_cat[:, b, :]), c["ident"][:, :])
                i.then_inc(sg["wT_out"], 1)

            def transpose_back(g):
                t.wait_ge(sg["y"], g + 1)
                if has(g - 1):
                    t.wait_ge(sg["added"], g)
                for b in range(GB):
                    i = t.transpose(p_back[:, bass.ts(b, N)], y[:, bass.ts(b, N)], c["ident"][:, :])
                i.then_inc(sg["yT"], 1)

            def second(g, par, k):
                out = p_y[par][:, :]
                if k == 0:
                    if has(g - 2):
                        t.wait_ge(sg["y"], g - 1)
                    t.matmul(out, b2_hi[:, :], wT[:, par, :], start=True, stop=False)
                    t.matmul(out, b2_lo[:, :], wT[:, par, :], start=False, stop=False)
                t.wait_ge(sg["h_hi"], rise(g, k, C))
                t.wait_ge(sg["h_lo"], rise(g, k, C))
                i = mm3(t, out, w2_hi[:, bass.ts(k, 128)], w2_lo[:, bass.ts(k, 128)],
                        h_hi[:, k % RING, :], h_lo[:, k % RING, :], start=False, stop=k == C - 1)
                i.then_inc(sg["y_out"], 1)

            def step(g, par):
                for k in range(C):
                    if k == 0:
                        t.wait_ge(sg["xc_hi"], g + 1)
                        t.wait_ge(sg["xc_lo"], g + 1)
                        t.wait_ge(sg["wT"], g + 1)
                    if reached(g, k - 2, C):
                        t.wait_ge(sg["h"], rise(g, k - 2, C))
                    mm3(t, p_h[k % 2][:, :], w1_hi[:, bass.ts(k, 128)], w1_lo[:, bass.ts(k, 128)],
                        xc_hi[:, par, :], xc_lo[:, par, :]).then_inc(sg["h_out"], 1)
                    if k % 2 == 0:
                        e = k // 2
                        if reached(g, k - 3, C):
                            t.wait_ge(sg["hw"], rise(g, k - 3, C))
                        t.matmul(p_wb[e % 2][:, :], pick[:, bass.ts(e, 128)], wT[:, par, :],
                                 start=True, stop=True).then_inc(sg["wb"], 1)
                    if k >= LAG:
                        second(g, par, k - LAG)
                    elif has(g - 1):
                        second(g - 1, 1 - par, k - LAG + C)
                    if k == 5 and has(g + 1):
                        transpose_in(g + 1)
                    if k == 6 and has(g - 1):
                        transpose_back(g - 1)
                    if k == 8 and has(g + 1):
                        route(g + 1)
                    if k == 14 and has(g + 1):
                        weights_in(g + 1)

            t.wait_ge(sg["split"], 3)
            t.wait_ge(sg["weights"], 16 * 7)
            transpose_in(0)
            route(0)
            weights_in(0)
            over_groups(t, step)
            for k in range(C - LAG, C):
                second(NG - 1, 1, k)
            transpose_back(NG - 1)

        @block.scalar
        def _(a):
            def evacuate_in(g, par):
                a.wait_ge(sg["xT"], g + 1)
                if has(g - 1):
                    a.wait_ge(sg["logits_out"], g)
                a.activation(xc[:, :], p_front[:, :], ACT.Identity, bias=c["col"]("beta"), scale=c["col"]("gamma")).then_inc(sg["xc"], 1)
                if reached(g, -C - 1, C):
                    a.wait_ge(sg["h_out"], rise(g, -C - 1, C))
                a.activation(xc_hi[:, par, :], p_front[:, :], ACT.Identity, bias=c["col"]("beta"),
                             scale=c["col"]("gamma")).then_inc(sg["xc_hi"], 1)

            def share(g):
                a.wait_ge(sg["gap"], g + 1)
                a.activation(tanh_gap[:, :], gap[:, :], ACT.Tanh, scale=0.5).then_inc(sg["tanh_gap"], 1)

            def weights_in(g, par):
                a.wait_ge(sg["wT_out"], g + 1)
                if reached(g, -2 * C, C):
                    a.wait_ge(sg["y_out"], rise(g, -2 * C, C))
                if reached(g, -E - 1, E):
                    a.wait_ge(sg["wb"], rise(g, -E - 1, E))
                a.activation(wT[:, par, :], p_front[0:2 * E, :], ACT.Copy).then_inc(sg["wT"], 1)

            def evacuate_y(g, par):
                a.wait_ge(sg["y_out"], rise(g, C - 1, C))
                if has(g - 1):
                    a.wait_ge(sg["yT"], g)
                a.activation(y[:, :], p_y[par][:, :], ACT.Copy).then_inc(sg["y"], 1)

            def head(g, k):
                a.wait_ge(sg["hw"], rise(g, k, C))
                if reached(g, k - RING, C):
                    a.wait_ge(sg["y_out"], rise(g, k - RING, C))
                a.activation(h_hi[:, k % RING, :], hw[:, k % 4, :], ACT.Copy).then_inc(sg["h_hi"], 1)

            def step(g, par):
                for k in range(C):
                    a.wait_ge(sg["h_out"], rise(g, k, C))
                    if reached(g, k - 2, C):
                        a.wait_ge(sg["hw"], rise(g, k - 2, C))
                    a.activation(h[:, k % 2, :], p_h[k % 2][:, :], ACT.Gelu, bias=c["col"](k)).then_inc(sg["h"], 1)
                    if k > 0:
                        head(g, k - 1)
                    elif has(g - 1):
                        head(g - 1, C - 1)
                    if k == 4 and has(g - 1):
                        evacuate_y(g - 1, 1 - par)
                    if k == 6 and has(g + 1):
                        evacuate_in(g + 1, 1 - par)
                    if k == 10 and has(g + 1):
                        share(g + 1)
                    if k == 15 and has(g + 1):
                        weights_in(g + 1, 1 - par)

            evacuate_in(0, 0)
            share(0)
            weights_in(0, 0)
            over_groups(a, step)
            head(NG - 1, C - 1)
            evacuate_y(NG - 1, 1)

        @block.vector
        def _(v):
            def front_norm(g):
                v.wait_ge(sg["rstd_step"], rise(g, RSTD - 1, RSTD))
                if has(g - 1):
                    v.wait_ge(sg["xT"], g)
                normalise(v, x_sb, g, mv, rstd[:, 3, :], xn).then_inc(sg["xn"], 1)

            def split_in(g, par):
                v.wait_ge(sg["xc"], g + 1)
                v.wait_ge(sg["xc_hi"], g + 1)
                v.tensor_tensor(xc_lo[:, par, :], xc[:, :], f(xc_hi[:, par, :]), ALU.subtract).then_inc(sg["xc_lo"], 1)

            def rank_experts(g):
                v.wait_ge(sg["logits_out"], g + 1)
                v.tensor_tensor(logits[:, :, :], p_front[:, 0:GB * E].rearrange("p (b e) -> p b e", b=GB),
                                b_route[:, :].unsqueeze(1).to_broadcast([128, GB, E]), ALU.add).then_inc(sg["logits"], 1)
                v.wait_ge(sg["logits"], g + 1)
                ranks(v, sg["route"], g, 0, ROUTE, logits[:, :, :], gt[:, :, :, :], eq[:, :, :, :],
                      rank[:, :, :], tri[:, :].rearrange("p (e j) -> p e j", e=E).unsqueeze(1).to_broadcast([128, GB, E, E]))

            def pick_two(g):
                v.wait_ge(sg["route"], rise(g, 3, ROUTE))
                v.tensor_scalar(first[:, :, :], rank[:, :, :], 0.0, None, ALU.is_equal)
                v.tensor_scalar(second[:, :, :], rank[:, :, :], 1.0, None, ALU.is_equal).then_inc(sg["route"], 1)
                v.wait_ge(sg["route"], rise(g, 4, ROUTE))
                v.tensor_tensor(dif[:, :, :], first[:, :, :], second[:, :, :], ALU.subtract)
                v.tensor_tensor(both[:, :, :], first[:, :, :], second[:, :, :], ALU.add).then_inc(sg["route"], 1)
                v.wait_ge(sg["route"], rise(g, 5, ROUTE))
                v.tensor_tensor(prod[:, :, :], logits[:, :, :], dif[:, :, :], ALU.mult).then_inc(sg["route"], 1)
                v.wait_ge(sg["route"], rise(g, 6, ROUTE))
                v.tensor_reduce(gap[:, :], prod[:, :, :], AX.X, ALU.add).then_inc(sg["gap"], 1)

            def shares(g):
                v.wait_ge(sg["tanh_gap"], g + 1)
                v.tensor_tensor(prod[:, :, :], dif[:, :, :], tanh_gap[:, :].unsqueeze(2).to_broadcast([128, GB, E]),
                                ALU.mult).then_inc(sg["route"], 1)
                v.wait_ge(sg["route"], rise(g, 7, ROUTE))
                v.tensor_tensor(prod[:, :, :], prod[:, :, :], both[:, :, :], ALU.add).then_inc(sg["route"], 1)
                v.wait_ge(sg["route"], rise(g, 8, ROUTE))
                if has(g - 1):
                    v.wait_ge(sg["wT_out"], g)
                v.tensor_scalar(w_cat[:, :, 0:E], prod[:, :, :], 0.5, None, ALU.mult).then_inc(sg["route"], 1)
                v.wait_ge(sg["route"], rise(g, 9, ROUTE))
                v.scalar_tensor_tensor(w_cat[:, :, E:2 * E], prod[:, :, :], 0.5, f(w_cat[:, :, 0:E]), ALU.mult,
                                       ALU.subtract).then_inc(sg["w_cat"], 1)

            def add_back(g):
                v.wait_ge(sg["yT"], g + 1)
                xg = x_sb[:, bass.ds(GB * g, GB), :]
                v.tensor_tensor(xg, xg, four(p_back[:, :]), ALU.add).then_inc(sg["added"], 1)

            def step(g, par):
                for k in range(C):
                    v.wait_ge(sg["h"], rise(g, k, C))
                    v.wait_ge(sg["wb"], rise(g, k // 2, E))
                    if reached(g, k - 4, C):
                        v.wait_ge(sg["h_lo"], rise(g, k - 4, C))
                    v.tensor_tensor(hw[:, k % 4, :], h[:, k % 2, :], p_wb[k // 2 % 2][:, :], ALU.mult).then_inc(sg["hw"], 1)
                    if has(g + 1):
                        if k == 1:
                            layer_norm_stats(v, sg, x_sb, g + 1, stats, mv)
                        if k == 3:
                            front_norm(g + 1)
                        if k == 7:
                            split_in(g + 1, 1 - par)
                        if k == 9:
                            rank_experts(g + 1)
                        if k == 10:
                            pick_two(g + 1)
                        if k == 12:
                            shares(g + 1)
                    if k == 8 and has(g - 1):
                        add_back(g - 1)

            v.wait_ge(sg["weights"], 16 * 7)
            v.tensor_copy(w1_hi[:, :], w1_raw[:, :])
            v.tensor_copy(w2_hi[:, :], w2_raw[:, :])
            v.tensor_copy(pick[:, :], pick_raw[:, :])
            v.tensor_copy(b2_hi[:, :], b2_raw[:, :]).then_inc(sg["hi"], 1)
            v.wait_ge(sg["hi"], 1)
            v.tensor_tensor(w1_lo[:, :], w1_raw[:, :], f(w1_hi[:, :]), ALU.subtract).then_inc(sg["split"], 1)
            v.tensor_tensor(w2_lo[:, :], w2_raw[:, :], f(w2_hi[:, :]), ALU.subtract).then_inc(sg["split"], 1)
            v.tensor_tensor(b2_lo[:, :], b2_raw[:, :], f(b2_hi[:, :]), ALU.subtract).then_inc(sg["split"], 1)
            layer_norm_stats(v, sg, x_sb, 0, stats, mv)
            front_norm(0)
            split_in(0, 0)
            rank_experts(0)
            pick_two(0)
            shares(0)
            over_groups(v, step)
            add_back(NG - 1)

        @block.gpsimd
        def _(p):
            def front(g):
                double_norm_scale(p, sg, g, mv, rstd, c, RSTD, c["ln_eps"])

            def remainder(g, k):
                p.wait_ge(sg["h_hi"], rise(g, k, C))
                if reached(g, k - RING, C):
                    p.wait_ge(sg["y_out"], rise(g, k - RING, C))
                p.tensor_tensor(h_lo[:, k % RING, :], hw[:, k % 4, :], f(h_hi[:, k % RING, :]),
                                ALU.subtract).then_inc(sg["h_lo"], 1)

            def step(g, par):
                for k in range(C):
                    remainder(g, k)
                    if k == 1 and has(g + 1):
                        front(g + 1)

            front(0)
            over_groups(p, step)


def double_norm_scale(p, sg, g, mv, rstd, c, per, eps2):
    tt = p.tensor_tensor
    step = sg["rstd_step"]
    half = c["minus_half"][:, 0:GB]
    p.wait_ge(sg["mean_var"], g + 1)
    tt(rstd[:, 0, :], mv[:, 1, :], c["ln_eps"][:, 0:GB], ALU.add).then_inc(step, 1)
    p.wait_ge(step, rise(g, 0, per))
    tt(rstd[:, 0, :], rstd[:, 0, :], half, ALU.pow).then_inc(step, 1)
    p.wait_ge(step, rise(g, 1, per))
    tt(rstd[:, 1, :], rstd[:, 0, :], rstd[:, 0, :], ALU.mult).then_inc(step, 1)
    p.wait_ge(step, rise(g, 2, per))
    tt(rstd[:, 1, :], rstd[:, 1, :], mv[:, 1, :], ALU.mult).then_inc(step, 1)
    p.wait_ge(step, rise(g, 3, per))
    tt(rstd[:, 2, :], rstd[:, 1, :], eps2[:, 0:GB], ALU.add).then_inc(step, 1)
    p.wait_ge(step, rise(g, 4, per))
    tt(rstd[:, 2, :], rstd[:, 2, :], half, ALU.pow).then_inc(step, 1)
    p.wait_ge(step, rise(g, 5, per))
    tt(rstd[:, 3, :], rstd[:, 0, :], rstd[:, 2, :], ALU.mult).then_inc(step, 1)


def attention(nc, io, x_sb, x2_sb, c):
    rope = x2_sb is not None
    pre = "a1_" if rope else "a0_"
    H = 4 if rope else 8
    HD = D // H
    HALVES = H // 4
    U = GB * HALVES
    T_LAG, PV_LAG = (1, 2) if rope else (2, 3)
    EDGES = 4
    with ExitStack() as ctx:
        def sb(name, shape, dt=F32):
            return ctx.enter_context(nc.sbuf_tensor(pre + name, shape, dt))

        bank = [ctx.enter_context(nc.psum_tensor(f"{pre}bank{i}", [128, W], F32)) for i in range(8)]
        p_s, p_t, p_o, p_front, p_x = bank[0:2], bank[2:4], bank[4:6], bank[6], bank[7]

        NPROJ = 4 if rope else 2
        VH = 2 if rope else 8
        proj_raw = sb("proj_raw", [128, NPROJ * D])
        proj_hi, proj_lo = sb("proj_hi", [128, NPROJ * D], F32R), sb("proj_lo", [128, NPROJ * D], F32R)
        w_v, w_o = sb("w_v", [128, VH * HD]), sb("w_o", [128, D])
        ident_bf = sb("ident_bf", [128, 128], BF16)
        stats, mv, rstd = sb("stats", [128, GB, 9]), sb("mv", [128, 2, GB]), sb("rstd", [128, 4, GB])
        xn = sb("xn", [128, GB, D])
        xc = sb("xc", [128, 2, W])
        xc_hi, xc_lo = sb("xc_hi", [128, 2, W], F32R), sb("xc_lo", [128, 2, W], F32R)
        q_hi, q_lo = sb("q_hi", [128, 2, W], F32R), sb("q_lo", [128, 2, W], F32R)
        k_split = sb("k_split", [128, 2, W], F32R)
        k_hi, k_lo = k_split[:, 0, :], k_split[:, 1, :]
        k_blocks = sb("k_blocks", [128, 2, 2, H, GB, N], F32R)
        v_ones = sb("v_ones", [128, 2, GB, VH, HD + 1])
        top = sb("top", [128, 2, 4])
        probs, probsT = sb("probs", [128, 2, W]), sb("probsT", [128, 2, W])
        inv = sb("inv", [128, 2, 2 * H])
        yn, yT = sb("yn", [128, GB, D]), sb("yT", [128, W])
        if rope:
            cos, sin = sb("cos", [128, N]), sb("sin", [128, N])
            causal_raw, causal = sb("causal_raw", [128, N]), sb("causal", [128, N], BF16)
            rot_a, rot_b, rot = sb("rot_a", [128, 2, W]), sb("rot_b", [128, 2, W]), sb("rot", [128, 2, W])
        else:
            w_edge = sb("w_edge", [128, H])
            adj = sb("adj", [128, 2, GB, N])
            masked = sb("masked", [128, 2, GB, N], BF16)
            edge, scores = sb("edge", [128, EDGES, W]), sb("scores", [128, 2, W])

        sg = {n: ctx.enter_context(nc.semaphore(pre + n)) for n in """weights zeroed hi split input stats pairs squared mean_var rstd_step xn xT xc
            xc_hi xc_lo proj proj_a proj_b rot q_hi q_lo k_hi k_lo kb v_out v masked edge s_out scores top exp
            pT_out pT_v pT_a pv inv yn yT_out yT o_out added base""".split()}
        ctx.push(clear_behind(nc, sg))
        block = ctx.enter_context(nc.Block())
        loads = [(proj_raw, io["proj1"] if rope else io["proj0"]), (w_v, io["w_v1"] if rope else io["w_v0"]),
                 (w_o, io["w_o1"] if rope else io["w_o0"])]
        loads += [(cos, io["cos"]), (sin, io["sin"]), (causal_raw, io["causal"])] if rope else [(w_edge, io["w_edge"])]
        RSTD = 7 if rope else 2
        SCALE = float(np.float32(1.0 / np.sqrt(np.float32(HD))))
        if rope:
            PE_PLAN = [[("front", 0), ("front", 1)], [("front", 2), ("front", 3)], [("front", 4), ("back", 0)],
                       [("in", 0), ("back", 1)]]
            ACT_Q, ACT_K, ACT_V, ACT_Y, ACT_IN = 1, 2, 3, 3, 0
            DVE_Q, DVE_K, DVE_NORM, DVE_ADD = 0, 1, 2, 3
        else:
            PE_PLAN = [[("front", 0)], [], [("front", 1)], [], [("front", 2), ("back", 0)], [], [("in", 0), ("back", 1)], []]
            ACT_Q, ACT_K, ACT_V, ACT_Y, ACT_IN = 1, 3, 5, 5, 7
            DVE_Q, DVE_K, DVE_MASK, DVE_NORM, DVE_ADD = 1, 3, 6, 5, 7

        def on_act(u):
            return not rope and u % 2 == 1

        def turned(eng, g, u):
            if rope and reached(g, u, U):
                eng.wait_ge(sg["pT_v"], rise(g, u, U))
            if not rope and reached(g, u // 2, U // 2):
                eng.wait_ge(sg["pT_a"] if on_act(u) else sg["pT_v"], rise(g, u // 2, U // 2))

        KB = 16 * H

        @block.sync
        def _(s):
            for dst, src in loads:
                s.dma_start(dst[:, :], src).then_inc(sg["weights"], 16)

            def load(g, par):
                if not rope:
                    if has(g - 2):
                        s.wait_ge(sg["masked"], g - 1)
                    if reached(g, -U - 1, U):
                        s.wait_ge(sg["edge"], rise(g, -U - 1, U))
                    s.dma_start(adj[:, par, :, :],
                                io["adj"][bass.ds(GB * g, GB), :, :].rearrange("b n m -> n b m")).then_inc(sg["input"], 16)

            def blocks(g, par):
                s.wait_ge(sg["k_hi"], g + 1)
                s.wait_ge(sg["k_lo"], g + 1)
                if reached(g, -U - 1, U):
                    s.wait_ge(sg["s_out"], rise(g, -U - 1, U))
                if has(g - 1):
                    s.wait_ge(sg["kb"], rise(g - 1, KB - 1, KB))
                for h in range(H):
                    rows = slice(HD * h, HD * h + HD)
                    s.dma_start(f(k_blocks[rows, par, :, h, :, :]),
                                f(k_split[rows, :, :]).rearrange("p s (b n) -> p s b n", b=GB)).then_inc(sg["kb"], 16)

            def step(g, par):
                if has(g + 1):
                    if not rope:
                        s.wait_ge(sg["input"], rise(g, 15, 16))
                    load(g + 1, 1 - par)
                    blocks(g + 1, 1 - par)

            s.wait_ge(sg["zeroed"], 2)
            load(0, 0)
            blocks(0, 0)
            over_groups(s, step)

        @block.tensor
        def _(t):
            def transpose_in(g):
                t.wait_ge(sg["xn"], g + 1)
                if has(g - 1):
                    t.wait_ge(sg["v"], g)
                for b in range(GB):
                    i = t.transpose(p_front[:, bass.ts(b, N)], xn[:, b, :], c["ident"][:, :])
                i.then_inc(sg["xT"], 1)

            def project(g, par, n):
                if n == 0:
                    t.wait_ge(sg["xc_hi"], g + 1)
                    t.wait_ge(sg["xc_lo"], g + 1)
                elif not rope:
                    t.wait_ge(sg["q_lo"], g + 1)
                elif n == 1:
                    if has(g - 3):
                        t.wait_ge(sg["added"], g - 2)
                    if has(g - 1):
                        t.wait_ge(sg["proj_b"], rise(g - 1, 1, 2))
                elif n == 2:
                    t.wait_ge(sg["proj_a"], rise(g, 0, 2))
                else:
                    t.wait_ge(sg["proj_b"], rise(g, 0, 2))
                out = p_x if rope and n % 2 else p_front
                mm3(t, out[:, :], proj_hi[:, bass.ts(n, D)], proj_lo[:, bass.ts(n, D)],
                    xc_hi[:, par, :], xc_lo[:, par, :]).then_inc(sg["proj"], 1)

            def values(g, par):
                if rope:
                    t.wait_ge(sg["proj_a"], rise(g, 1, 2))
                else:
                    t.wait_ge(sg["k_lo"], g + 1)
                width = VH * HD
                for b in range(GB):
                    i = t.matmul(p_front[:, b * width:(b + 1) * width], xc[:, par, bass.ts(b, N)], w_v[:, :],
                                 start=True, stop=True)
                i.then_inc(sg["v_out"], 1)

            def score(g, par, u):
                b, half = divmod(u, HALVES)
                out = p_s[u % 2][:, :]
                if u == 0:
                    t.wait_ge(sg["q_hi"], g + 1)
                    t.wait_ge(sg["q_lo"], g + 1)
                    t.wait_ge(sg["kb"], rise(g, KB - 1, KB))
                    if not rope:
                        t.wait_ge(sg["masked"], g + 1)
                if reached(g, u - 2, U):
                    t.wait_ge(sg["exp"] if rope else sg["scores"], rise(g, u - 2, U))
                mask = causal[:, :] if rope else masked[:, par, b, :]
                t.matmul(four(out), ident_bf[:, :], mask.unsqueeze(1).to_broadcast([128, 4, N]), start=True, stop=False)
                heads, nodes = slice(4 * half, 4 * half + 4), bass.ts(b, N)
                mm3(t, four(out), q_hi[:, par, nodes], q_lo[:, par, nodes], k_blocks[:, par, 0, heads, b, :],
                    k_blocks[:, par, 1, heads, b, :], start=False).then_inc(sg["s_out"], 1)

            def turn(g, u):
                t.wait_ge(sg["exp"], rise(g, u, U))
                turned(t, g, u - 2)
                for h in range(4):
                    i = t.transpose(p_t[u % 2][:, bass.ts(h, N)], probs[:, u % 2, bass.ts(h, N)], c["ident"][:, :])
                i.then_inc(sg["pT_out"], 1)

            def weigh(g, par, u):
                b, half = divmod(u, HALVES)
                if u == 0:
                    t.wait_ge(sg["v"], g + 1)
                    if has(g - 1):
                        t.wait_ge(sg["yn"], g)
                turned(t, g, u)
                for h in range(4):
                    head = 4 * half + h
                    o = ((b % 2) * H + head) * (HD + 1)
                    i = t.matmul(p_o[b // 2][:, o:o + HD + 1], probsT[:, u % 2, bass.ts(h, N)],
                                 v_ones[:, par, b, head * VH // H, :], start=True, stop=True)
                i.then_inc(sg["pv"], 1)

            def turn_y(g):
                t.wait_ge(sg["yn"], g + 1)
                if has(g - 1):
                    t.wait_ge(sg["added"], g)
                if rope and has(g + 2):
                    t.wait_ge(sg["proj_b"], rise(g + 2, 1, 2))
                for b in range(GB):
                    i = t.transpose(p_x[:, bass.ts(b, N)], yn[:, b, :], c["ident"][:, :])
                i.then_inc(sg["yT_out"], 1)

            def out_product(g):
                t.wait_ge(sg["yT"], g + 1)
                for b in range(GB):
                    i = t.matmul(p_x[:, bass.ts(b, N)], yT[:, bass.ts(b, N)], w_o[:, :], start=True, stop=True)
                i.then_inc(sg["o_out"], 1)

            def front(g, par, n):
                if n < NPROJ:
                    project(g, par, n)
                else:
                    values(g, par)

            def step(g, par):
                for u in range(U):
                    score(g, par, u)
                    if u >= T_LAG:
                        turn(g, u - T_LAG)
                    elif has(g - 1):
                        turn(g - 1, u - T_LAG + U)
                    if u >= PV_LAG:
                        weigh(g, par, u - PV_LAG)
                    elif has(g - 1):
                        weigh(g - 1, 1 - par, u - PV_LAG + U)
                    for side, n in PE_PLAN[u]:
                        if side == "back" and has(g - 1):
                            (turn_y, out_product)[n](g - 1)
                        if side == "front" and has(g + 1):
                            front(g + 1, 1 - par, n)
                        if side == "in" and has(g + 2):
                            transpose_in(g + 2)

            t.wait_ge(sg["weights"], 16 * len(loads))
            t.wait_ge(sg["split"], 1)
            transpose_in(0)
            for n in range(NPROJ + 1):
                front(0, 0, n)
            transpose_in(1)
            over_groups(t, step)
            for j in range(PV_LAG):
                if j < T_LAG:
                    turn(NG - 1, U - T_LAG + j)
                weigh(NG - 1, 1, U - PV_LAG + j)
            turn_y(NG - 1)
            out_product(NG - 1)

        @block.scalar
        def _(a):
            def evacuate_in(g, par):
                a.wait_ge(sg["xT"], g + 1)
                if rope:
                    a.activation(xc[:, par, :], p_front[:, :], ACT.Copy, scale=c["col"]("ln1")).then_inc(sg["xc"], 1)
                    a.activation(xc_hi[:, par, :], p_front[:, :], ACT.Copy, scale=c["col"]("ln1")).then_inc(sg["xc_hi"], 1)
                else:
                    a.activation(xc[:, par, :], p_front[:, :], ACT.Copy).then_inc(sg["xc"], 1)
                    a.activation(xc_hi[:, par, :], p_front[:, :], ACT.Copy).then_inc(sg["xc_hi"], 1)

            def q_head(g, par):
                if reached(g, -U - 1, U):
                    a.wait_ge(sg["s_out"], rise(g, -U - 1, U))
                if rope:
                    a.wait_ge(sg["rot"], rise(g, 0, 2))
                    a.activation(q_hi[:, par, :], rot[:, 0, :], ACT.Copy).then_inc(sg["q_hi"], 1)
                else:
                    a.wait_ge(sg["proj"], rise(g, 0, 2))
                    a.activation(q_hi[:, par, :], p_front[:, :], ACT.Copy, scale=SCALE).then_inc(sg["q_hi"], 1)

            def k_head(g):
                if has(g - 1):
                    a.wait_ge(sg["kb"], rise(g - 1, KB - 1, KB))
                if rope:
                    a.wait_ge(sg["rot"], rise(g, 1, 2))
                    a.activation(k_hi, rot[:, 1, :], ACT.Copy).then_inc(sg["k_hi"], 1)
                else:
                    a.wait_ge(sg["proj"], rise(g, 1, 2))
                    a.activation(k_hi, p_front[:, :], ACT.Copy).then_inc(sg["k_hi"], 1)

            def values(g, par):
                a.wait_ge(sg["v_out"], g + 1)
                if reached(g, -U - 1, U):
                    a.wait_ge(sg["pv"], rise(g, -U - 1, U))
                a.activation(v_ones[:, par, :, :, 0:HD],
                             p_front[:, 0:GB * VH * HD].rearrange("p (b h d) -> p b h d", b=GB, h=VH),
                             ACT.Copy).then_inc(sg["v"], 1)

            def exponent(g, u):
                a.wait_ge(sg["top"], rise(g, u, U))
                if reached(g, u - 2, U):
                    a.wait_ge(sg["pT_out"], rise(g, u - 2, U))
                src = p_s[u % 2][:, :] if rope else scores[:, u % 2, :]
                for h in range(4):
                    i = a.activation(probs[:, u % 2, bass.ts(h, N)], src[:, bass.ts(h, N)], ACT.Exp,
                                     bias=top[:, u % 2, h:h + 1])
                i.then_inc(sg["exp"], 1)

            def evacuate_turned(g, u):
                a.wait_ge(sg["pT_out"], rise(g, u, U))
                if reached(g, u - 2, U):
                    a.wait_ge(sg["pv"], rise(g, u - 2, U))
                a.activation(probsT[:, u % 2, :], p_t[u % 2][:, :], ACT.Copy).then_inc(sg["pT_a"], 1)

            def y_in(g):
                a.wait_ge(sg["yT_out"], g + 1)
                if has(g - 1):
                    a.wait_ge(sg["o_out"], g)
                a.activation(yT[:, :], p_x[:, :], ACT.Copy).then_inc(sg["yT"], 1)

            def step(g, par):
                for u in range(U):
                    if on_act(u - T_LAG):
                        if u >= T_LAG:
                            evacuate_turned(g, u - T_LAG)
                        elif has(g - 1):
                            evacuate_turned(g - 1, u - T_LAG + U)
                    if has(g + 1):
                        if rope and u == ACT_IN:
                            evacuate_in(g + 1, 1 - par)
                        if u == ACT_Q:
                            q_head(g + 1, 1 - par)
                        if u == ACT_K:
                            k_head(g + 1)
                        if u == ACT_V:
                            values(g + 1, 1 - par)
                    if not rope and has(g + 2) and u == ACT_IN:
                        evacuate_in(g + 2, par)
                    if has(g - 1) and u == ACT_Y:
                        y_in(g - 1)
                    exponent(g, u)

            evacuate_in(0, 0)
            q_head(0, 0)
            k_head(0)
            values(0, 0)
            if not rope:
                evacuate_in(1, 1)
            over_groups(a, step)
            for u in range(U - T_LAG, U):
                if on_act(u):
                    evacuate_turned(NG - 1, u)
            y_in(NG - 1)

        @block.vector
        def _(v):
            def front_norm(g):
                v.wait_ge(sg["rstd_step"], rise(g, RSTD - 1, RSTD))
                if has(g - 1):
                    v.wait_ge(sg["xT"], g)
                if rope:
                    normalise(v, x_sb, g, mv, rstd[:, 0, :], x2_sb[:, bass.ds(GB * g, GB), :]).then_inc(sg["base"], 1)
                normalise(v, x_sb, g, mv, rstd[:, 3 if rope else 0, :], xn).then_inc(sg["xn"], 1)

            def front_q(g, par):
                if rope:
                    rotate(g, 0)
                else:
                    v.wait_ge(sg["q_hi"], g + 1)
                    v.scalar_tensor_tensor(q_lo[:, par, :], p_front[:, :], SCALE, f(q_hi[:, par, :]), ALU.mult,
                                           ALU.subtract).then_inc(sg["q_lo"], 1)

            def front_k(g):
                if rope:
                    rotate(g, 1)
                else:
                    v.wait_ge(sg["k_hi"], g + 1)
                    v.tensor_tensor(k_lo, p_front[:, :], f(k_hi), ALU.subtract).then_inc(sg["k_lo"], 1)

            def rotate(g, n):
                v.wait_ge(sg["proj"], rise(g, 2 * n, 4))
                if has(g - 1):
                    v.wait_ge(sg["rot"], rise(g - 1, 1, 2))
                scale = 1.0 if n else SCALE
                v.scalar_tensor_tensor(four(rot_a[:, n, :]), four(p_front[:, :]), scale,
                                       cos[:, :].unsqueeze(1).to_broadcast([128, GB, N]), ALU.mult, ALU.mult).then_inc(sg["proj_a"], 1)
                v.wait_ge(sg["proj"], rise(g, 2 * n + 1, 4))
                v.scalar_tensor_tensor(four(rot_b[:, n, :]), four(p_x[:, :]), scale,
                                       sin[:, :].unsqueeze(1).to_broadcast([128, GB, N]), ALU.mult, ALU.mult).then_inc(sg["proj_b"], 1)

            def mask(g, par):
                v.wait_ge(sg["input"], rise(g, 15, 16))
                if reached(g, -U - 1, U):
                    v.wait_ge(sg["s_out"], rise(g, -U - 1, U))
                v.tensor_scalar(masked[:, par, :, :], adj[:, par, :, :], 0.0, NEG, ALU.is_equal,
                                ALU.mult).then_inc(sg["masked"], 1)

            def unit(g, u):
                v.wait_ge(sg["s_out"], rise(g, u, U))
                if reached(g, u - 2, U):
                    v.wait_ge(sg["exp"], rise(g, u - 2, U))
                src = p_s[u % 2]
                if not rope:
                    v.wait_ge(sg["edge"], rise(g, u, U))
                    v.tensor_tensor(scores[:, u % 2, :], p_s[u % 2][:, :], edge[:, u % EDGES, :], ALU.add).then_inc(sg["scores"], 1)
                    v.wait_ge(sg["scores"], rise(g, u, U))
                    src = scores[:, u % 2, :]
                v.tensor_reduce(top[:, u % 2, :], four(src[:, :]), AX.X, ALU.max, negate=True).then_inc(sg["top"], 1)

            def evacuate_turned(g, u):
                v.wait_ge(sg["pT_out"], rise(g, u, U))
                if reached(g, u - 2, U):
                    v.wait_ge(sg["pv"], rise(g, u - 2, U))
                v.tensor_copy(probsT[:, u % 2, :], p_t[u % 2][:, :]).then_inc(sg["pT_v"], 1)

            def divide(g):
                v.wait_ge(sg["pv"], rise(g, U - 1, U))
                if has(g - 1):
                    v.wait_ge(sg["yT_out"], g)
                out = [p_o[n][:, 0:2 * H * (HD + 1)].rearrange("p (h d) -> p h d", d=HD + 1) for n in range(2)]
                for n in range(2):
                    i = v.reciprocal(inv[:, n, :], out[n][:, :, HD])
                i.then_inc(sg["inv"], 1)
                v.wait_ge(sg["inv"], g + 1)
                for n in range(2):
                    i = v.tensor_tensor(yn[:, 2 * n:2 * n + 2, :].rearrange("p b (h d) -> p (b h) d", h=H),
                                        out[n][:, :, 0:HD], inv[:, n, :].unsqueeze(2).to_broadcast([128, 2 * H, HD]), ALU.mult)
                i.then_inc(sg["yn"], 1)

            def add_back(g):
                v.wait_ge(sg["o_out"], g + 1)
                xg = (x2_sb if rope else x_sb)[:, bass.ds(GB * g, GB), :]
                if rope:
                    v.wait_ge(sg["base"], g + 1)
                v.tensor_tensor(xg, xg, four(p_x[:, :]), ALU.add).then_inc(sg["added"], 1)

            def step(g, par):
                for u in range(U):
                    unit(g, u)
                    if not on_act(u - T_LAG):
                        if u >= T_LAG:
                            evacuate_turned(g, u - T_LAG)
                        elif has(g - 1):
                            evacuate_turned(g - 1, u - T_LAG + U)
                    if has(g + 1):
                        if u == DVE_Q:
                            front_q(g + 1, 1 - par)
                        if u == DVE_K:
                            front_k(g + 1)
                        if not rope and u == DVE_MASK:
                            mask(g + 1, 1 - par)
                    if has(g - 1) and u == PV_LAG - 1:
                        divide(g - 1)
                    if has(g + 2):
                        if u == 0:
                            layer_norm_stats(v, sg, x_sb, g + 2, stats, mv)
                        if u == DVE_NORM:
                            front_norm(g + 2)
                    if has(g - 1) and u == DVE_ADD:
                        add_back(g - 1)

            v.memset(v_ones[:, :, :, :, HD:HD + 1], 1.0)
            v.memset(f(k_blocks[:, 0, :, :, :, :]), 0.0).then_inc(sg["zeroed"], 1)
            v.wait_ge(sg["weights"], 16 * len(loads))
            if rope:
                v.tensor_copy(causal[:, :], causal_raw[:, :])
            v.tensor_copy(ident_bf[:, :], c["ident"][:, :])
            v.tensor_copy(proj_hi[:, :], proj_raw[:, :]).then_inc(sg["hi"], 1)
            v.wait_ge(sg["hi"], 1)
            v.tensor_tensor(proj_lo[:, :], proj_raw[:, :], f(proj_hi[:, :]), ALU.subtract).then_inc(sg["split"], 1)
            layer_norm_stats(v, sg, x_sb, 0, stats, mv)
            front_norm(0)
            if not rope:
                mask(0, 0)
            front_q(0, 0)
            front_k(0)
            layer_norm_stats(v, sg, x_sb, 1, stats, mv)
            front_norm(1)
            over_groups(v, step)
            for u in range(U - T_LAG, U):
                if not on_act(u):
                    evacuate_turned(NG - 1, u)
            divide(NG - 1)
            add_back(NG - 1)

        @block.gpsimd
        def _(p):
            def scales(g):
                if rope:
                    double_norm_scale(p, sg, g, mv, rstd, c, RSTD, c["rms_eps"])
                else:
                    p.wait_ge(sg["mean_var"], g + 1)
                    p.tensor_tensor(rstd[:, 0, :], mv[:, 1, :], c["ln_eps"][:, 0:GB], ALU.add).then_inc(sg["rstd_step"], 1)
                    p.wait_ge(sg["rstd_step"], rise(g, 0, RSTD))
                    p.tensor_tensor(rstd[:, 0, :], rstd[:, 0, :], c["minus_half"][:, 0:GB], ALU.pow).then_inc(sg["rstd_step"], 1)

            def split_in(g, par):
                p.wait_ge(sg["xc"], g + 1)
                p.wait_ge(sg["xc_hi"], g + 1)
                p.tensor_tensor(xc_lo[:, par, :], xc[:, par, :], f(xc_hi[:, par, :]), ALU.subtract).then_inc(sg["xc_lo"], 1)

            def edge_bias(g, par, u):
                b, half = divmod(u, HALVES)
                if u == 0:
                    p.wait_ge(sg["input"], rise(g, 15, 16))
                if reached(g, u - EDGES, U):
                    p.wait_ge(sg["scores"], rise(g, u - EDGES, U))
                p.tensor_tensor(four(edge[:, u % EDGES, :]), adj[:, par, b, :].unsqueeze(1).to_broadcast([128, 4, N]),
                                w_edge[:, 4 * half:4 * half + 4].unsqueeze(2).to_broadcast([128, 4, N]),
                                ALU.mult).then_inc(sg["edge"], 1)

            def rotated(g, par, n):
                p.wait_ge(sg["proj_b"], rise(g, n, 2))
                if has(g - 1):
                    p.wait_ge(sg["k_lo"] if n else sg["q_lo"], g)
                if n:
                    if has(g - 1):
                        p.wait_ge(sg["k_hi"], g)
                else:
                    if has(g - 1):
                        p.wait_ge(sg["q_hi"], g)
                p.tensor_tensor(rot[:, n, :], rot_a[:, n, :], rot_b[:, n, :], ALU.add).then_inc(sg["rot"], 1)
                hi, lo, s_hi, s_lo = ((k_hi, k_lo, sg["k_hi"], sg["k_lo"]) if n else
                                      (q_hi[:, par, :], q_lo[:, par, :], sg["q_hi"], sg["q_lo"]))
                p.wait_ge(s_hi, g + 1)
                p.tensor_tensor(lo, rot[:, n, :], f(hi), ALU.subtract).then_inc(s_lo, 1)

            def step(g, par):
                for u in range(U):
                    if not rope:
                        edge_bias(g, par, u)
                    if has(g + 1) and u == 0:
                        split_in(g + 1, 1 - par)
                    if rope and has(g + 1) and u in (DVE_Q, DVE_K):
                        rotated(g + 1, 1 - par, int(u == DVE_K))
                    if has(g + 2) and u == (1 if rope else 3):
                        scales(g + 2)

            p.memset(f(k_blocks[:, 1, :, :, :, :]), 0.0).then_inc(sg["zeroed"], 1)
            if not rope:
                p.wait_ge(sg["weights"], 16 * len(loads))
            scales(0)
            split_in(0, 0)
            if rope:
                rotated(0, 0, 0)
                rotated(0, 0, 1)
            scales(1)
            over_groups(p, step)


def layer1_gnn(nc, io, x_sb, c):
    attention(nc, io, x_sb, None, c)


def layer1_attention(nc, io, x_sb, x2_sb, c):
    attention(nc, io, x_sb, x2_sb, c)


def layer1_ffn(nc, io, x_sb, x2_sb, c):
    with ExitStack() as ctx:
        def sb(name, shape, dt=F32):
            return ctx.enter_context(nc.sbuf_tensor("f1_" + name, shape, dt))

        bank = [ctx.enter_context(nc.psum_tensor(f"f1_bank{i}", [128, W], F32)) for i in range(8)]
        p_gate, p_up, p_wb, p_y, p_front = bank[0:2], bank[2:4], bank[4:6], bank[6], bank[7]

        LAG = 3
        RING = 4
        HALF = NT * 128 // 2
        raw = sb("raw", [128, 2, HALF])
        w1_hi, w1_lo = sb("w1_hi", [128, NT * 128], F32R), sb("w1_lo", [128, NT * 128], F32R)
        w3_hi, w3_lo = sb("w3_hi", [128, NT * 128], F32R), sb("w3_lo", [128, NT * 128], F32R)
        w2_hi, w2_lo = sb("w2_hi", [128, NT * 128], F32R), sb("w2_lo", [128, NT * 128], F32R)
        pick = sb("pick", [2 * E, NT * 128], F32R)
        w_route, tri = sb("w_route", [128, E]), sb("tri", [128, E * E])
        stats, mv, rstd = sb("stats", [128, GB, 9]), sb("mv", [128, 2, GB]), sb("rstd", [128, GB])
        xn, xc = sb("xn", [128, GB, D]), sb("xc", [128, W])
        xc_hi, xc_lo = sb("xc_hi", [128, 2, W], F32R), sb("xc_lo", [128, 2, W], F32R)
        logits = sb("logits", [128, GB, E])
        gt, eq = sb("gt", [128, GB, E, E]), sb("eq", [128, GB, E, E])
        rank, chosen = sb("rank", [128, GB, E]), sb("chosen", [128, GB, E])
        ex, share = sb("ex", [128, GB, E]), sb("share", [128, GB, E])
        top, total, kept = sb("top", [128, GB]), sb("total", [128, GB]), sb("kept", [128, GB])
        w_cat, wT = sb("w_cat", [128, GB, 2 * E], F32R), sb("wT", [2 * E, 2, W], F32R)
        act, h = sb("act", [128, 2, W]), sb("h", [128, 2, W])
        h_hi, h_lo = sb("h_hi", [128, RING, W], F32R), sb("h_lo", [128, RING, W], F32R)
        y, result = sb("y", [128, W]), sb("result", [128, 2, W])

        sg = {n: ctx.enter_context(nc.semaphore("f1_" + n)) for n in """small raw0 raw1 hi split stats pairs squared mean_var rstd_step xn xT xc xc_hi
            xc_lo logits_out logits route shifted ex w_head w_cat wT_out wT gate up wb act gated h h_hi h_lo y_out y yT
            result stored residual""".split()}
        block = ctx.enter_context(nc.Block())
        ROUTE = 11

        @block.sync
        def _(q):
            q.dma_start(w_route[:, :], io["w_route1"]).then_inc(sg["small"], 16)
            q.dma_start(tri[:, :], io["tri"]).then_inc(sg["small"], 16)
            for n in range(8):
                src = (io["w1_1"], io["w3_1"], io["w2_1"], io["pick_1"])[n // 2]
                if n >= 2:
                    q.wait_ge(sg["split"], n - 1)
                q.dma_start(raw[0:src.shape[0], n % 2, :], src[:, bass.ts(n % 2, HALF)]).then_inc(
                    (sg["raw0"], sg["raw1"])[n % 2], 16)

            def step(g, par):
                q.wait_ge(sg["result"], g + 1)
                if has(g - 1):
                    q.wait_ge(sg["stored"], rise(g - 1, 15, 16))
                q.dma_start(io["out"][bass.ds(GB * g, GB), :, :].rearrange("b n d -> n b d"),
                            four(result[:, par, :])).then_inc(sg["stored"], 16)

            over_groups(q, step)
            q.wait_ge(sg["stored"], 16 * NG)

        @block.tensor
        def _(t):
            def transpose_in(g):
                t.wait_ge(sg["xn"], g + 1)
                if has(g - 1):
                    t.wait_ge(sg["wT"], g)
                if has(g - 2):
                    t.wait_ge(sg["result"], g - 1)
                for b in range(GB):
                    i = t.transpose(p_front[:, bass.ts(b, N)], xn[:, b, :], c["ident"][:, :])
                i.then_inc(sg["xT"], 1)

            def route(g):
                t.wait_ge(sg["xc"], g + 1)
                t.wait_ge(sg["xc_hi"], g + 1)
                for b in range(GB):
                    i = t.matmul(p_front[:, b * E:(b + 1) * E], xc[:, bass.ts(b, N)], w_route[:, :], start=True, stop=True)
                i.then_inc(sg["logits_out"], 1)

            def weights_in(g):
                t.wait_ge(sg["w_cat"], g + 1)
                t.wait_ge(sg["logits"], g + 1)
                if has(g - 2):
                    t.wait_ge(sg["result"], g - 1)
                for b in range(GB):
                    i = t.transpose(p_front[0:2 * E, bass.ts(b, N)], f(w_cat[:, b, :]), c["ident"][:, :])
                i.then_inc(sg["wT_out"], 1)

            def transpose_back(g):
                t.wait_ge(sg["y"], g + 1)
                if has(g + 1):
                    t.wait_ge(sg["wT"], g + 2)
                for b in range(GB):
                    i = t.transpose(p_front[:, bass.ts(b, N)], y[:, bass.ts(b, N)], c["ident"][:, :])
                i.then_inc(sg["yT"], 1)

            def out_product(g, par, k):
                if k == 0:
                    if has(g - 1):
                        t.wait_ge(sg["y"], g)
                t.wait_ge(sg["h_hi"], rise(g, k, NT))
                t.wait_ge(sg["h_lo"], rise(g, k, NT))
                r = (par * NT + k) % RING
                mm3(t, p_y[:, :], w2_hi[:, bass.ts(k, 128)], w2_lo[:, bass.ts(k, 128)],
                    h_hi[:, r, :], h_lo[:, r, :], start=k == 0, stop=k == NT - 1).then_inc(sg["y_out"], 1)

            def step(g, par):
                for k in range(NT):
                    if k == 0:
                        t.wait_ge(sg["xc_hi"], g + 1)
                        t.wait_ge(sg["xc_lo"], g + 1)
                        t.wait_ge(sg["wT"], g + 1)
                    cols = bass.ts(k, 128)
                    if reached(g, k - 2, NT):
                        t.wait_ge(sg["act"], rise(g, k - 2, NT))
                    mm3(t, p_gate[k % 2][:, :], w1_hi[:, cols], w1_lo[:, cols],
                        xc_hi[:, par, :], xc_lo[:, par, :]).then_inc(sg["gate"], 1)
                    if reached(g, k - 2, NT):
                        t.wait_ge(sg["h"], rise(g, k - 2, NT))
                    mm3(t, p_up[k % 2][:, :], w3_hi[:, cols], w3_lo[:, cols],
                        xc_hi[:, par, :], xc_lo[:, par, :]).then_inc(sg["up"], 1)
                    t.matmul(p_wb[k % 2][:, :], pick[:, cols], wT[:, par, :], start=True, stop=True).then_inc(sg["wb"], 1)
                    if k >= LAG:
                        out_product(g, par, k - LAG)
                    elif has(g - 1):
                        out_product(g - 1, 1 - par, k - LAG + NT)
                    if k == 4 and has(g - 1):
                        transpose_back(g - 1)
                    if has(g + 1):
                        if k == 7:
                            transpose_in(g + 1)
                        if k == 10:
                            route(g + 1)
                        if k == 18:
                            weights_in(g + 1)

            t.wait_ge(sg["split"], 8)
            t.wait_ge(sg["small"], 32)
            transpose_in(0)
            route(0)
            weights_in(0)
            over_groups(t, step)
            for k in range(NT - LAG, NT):
                out_product(NG - 1, 1, k)
            transpose_back(NG - 1)

        @block.scalar
        def _(a):
            def evacuate_in(g, par):
                a.wait_ge(sg["xT"], g + 1)
                if has(g - 1):
                    a.wait_ge(sg["logits_out"], g)
                a.activation(xc[:, :], p_front[:, :], ACT.Copy, scale=c["col"]("ln2")).then_inc(sg["xc"], 1)
                if reached(g, -NT - 1, NT):
                    a.wait_ge(sg["up"], rise(g, -NT - 1, NT))
                a.activation(xc_hi[:, par, :], p_front[:, :], ACT.Copy, scale=c["col"]("ln2")).then_inc(sg["xc_hi"], 1)

            def exponent(g):
                a.wait_ge(sg["shifted"], rise(g, 0, 1))
                if has(g - 1):
                    a.wait_ge(sg["w_cat"], g)
                a.activation(ex[:, :, :], logits[:, :, :], ACT.Exp).then_inc(sg["ex"], 1)

            def weights_in(g, par):
                a.wait_ge(sg["wT_out"], g + 1)
                if reached(g, -NT - 1, NT):
                    a.wait_ge(sg["wb"], rise(g, -NT - 1, NT))
                a.activation(wT[:, par, :], p_front[0:2 * E, :], ACT.Copy).then_inc(sg["wT"], 1)

            def evacuate_y(g):
                a.wait_ge(sg["y_out"], rise(g, NT - 1, NT))
                if has(g - 1):
                    a.wait_ge(sg["yT"], g)
                a.activation(y[:, :], p_y[:, :], ACT.Copy).then_inc(sg["y"], 1)

            def head(g, par, k):
                a.wait_ge(sg["h"], rise(g, k, NT))
                if reached(g, k - RING, NT):
                    a.wait_ge(sg["y_out"], rise(g, k - RING, NT))
                a.activation(h_hi[:, (par * NT + k) % RING, :], h[:, k % 2, :], ACT.Copy).then_inc(sg["h_hi"], 1)

            def step(g, par):
                for k in range(NT):
                    a.wait_ge(sg["gate"], rise(g, k, NT))
                    if reached(g, k - 2, NT):
                        a.wait_ge(sg["h"], rise(g, k - 2, NT))
                    a.activation(act[:, k % 2, :], p_gate[k % 2][:, :], ACT.Silu).then_inc(sg["act"], 1)
                    if k > 0:
                        head(g, par, k - 1)
                    elif has(g - 1):
                        head(g - 1, 1 - par, NT - 1)
                    if k == 3 and has(g - 1):
                        evacuate_y(g - 1)
                    if has(g + 1):
                        if k == 8:
                            evacuate_in(g + 1, 1 - par)
                        if k == 14:
                            exponent(g + 1)
                        if k == 19:
                            weights_in(g + 1, 1 - par)

            evacuate_in(0, 0)
            exponent(0)
            weights_in(0, 0)
            over_groups(a, step)
            head(NG - 1, 1, NT - 1)
            evacuate_y(NG - 1)

        @block.vector
        def _(v):
            def front_norm(g):
                v.wait_ge(sg["rstd_step"], rise(g, 3, 4))
                if has(g - 1):
                    v.wait_ge(sg["xT"], g)
                for b in range(GB):
                    i = v.tensor_scalar(xn[:, b, :], x2_sb[:, bass.ds(GB * g + b, 1), :].rearrange("p a d -> p (a d)"),
                                        rstd[:, b:b + 1], None, ALU.mult)
                i.then_inc(sg["xn"], 1)

            def residual(g):
                xg = x2_sb[:, bass.ds(GB * g, GB), :]
                v.wait_ge(sg["xn"], g + 1)
                v.tensor_tensor(xg, xg, x_sb[:, bass.ds(GB * g, GB), :], ALU.add).then_inc(sg["residual"], 1)

            def split_in(g, par):
                v.wait_ge(sg["xc"], g + 1)
                v.wait_ge(sg["xc_hi"], g + 1)
                v.tensor_tensor(xc_lo[:, par, :], xc[:, :], f(xc_hi[:, par, :]), ALU.subtract).then_inc(sg["xc_lo"], 1)

            def rank_experts(g):
                v.wait_ge(sg["logits_out"], g + 1)
                v.tensor_copy(logits[:, :, :], p_front[:, 0:GB * E].rearrange("p (b e) -> p b e", b=GB)).then_inc(sg["logits"], 1)
                v.wait_ge(sg["logits"], g + 1)
                ranks(v, sg["route"], g, 0, ROUTE, logits[:, :, :], gt[:, :, :, :], eq[:, :, :, :],
                      rank[:, :, :], tri[:, :].rearrange("p (e j) -> p e j", e=E).unsqueeze(1).to_broadcast([128, GB, E, E]))

            def below_top(g):
                v.tensor_reduce(top[:, :], logits[:, :, :], AX.X, ALU.max, negate=True).then_inc(sg["route"], 1)
                v.wait_ge(sg["route"], rise(g, 4, ROUTE))
                v.tensor_tensor(logits[:, :, :], logits[:, :, :], along(top[:, :], [128, GB, E]), ALU.add).then_inc(sg["shifted"], 1)

            def shares(g):
                v.wait_ge(sg["ex"], g + 1)
                v.tensor_reduce(total[:, :], ex[:, :, :], AX.X, ALU.add)
                v.tensor_scalar(chosen[:, :, :], rank[:, :, :], 2.0, None, ALU.is_lt).then_inc(sg["route"], 1)
                v.wait_ge(sg["route"], rise(g, 5, ROUTE))
                v.tensor_tensor(share[:, :, :], ex[:, :, :], chosen[:, :, :], ALU.mult).then_inc(sg["route"], 1)
                v.wait_ge(sg["route"], rise(g, 6, ROUTE))
                v.tensor_reduce(kept[:, :], share[:, :, :], AX.X, ALU.add).then_inc(sg["route"], 1)
                v.wait_ge(sg["route"], rise(g, 7, ROUTE))
                v.scalar_tensor_tensor(kept[:, :], total[:, :], 1e-9, kept[:, :], ALU.mult, ALU.add).then_inc(sg["route"], 1)
                v.wait_ge(sg["route"], rise(g, 8, ROUTE))
                v.reciprocal(kept[:, :], kept[:, :]).then_inc(sg["route"], 1)
                v.wait_ge(sg["route"], rise(g, 9, ROUTE))
                v.tensor_tensor(share[:, :, :], share[:, :, :], along(kept[:, :], [128, GB, E]), ALU.mult).then_inc(sg["route"], 1)
                v.wait_ge(sg["route"], rise(g, 10, ROUTE))
                if has(g - 1):
                    v.wait_ge(sg["wT_out"], g)
                v.tensor_copy(w_cat[:, :, 0:E], share[:, :, :]).then_inc(sg["w_head"], 1)
                v.wait_ge(sg["w_head"], g + 1)
                v.tensor_tensor(w_cat[:, :, E:2 * E], share[:, :, :], f(w_cat[:, :, 0:E]), ALU.subtract).then_inc(sg["w_cat"], 1)

            def finish(g, par):
                v.wait_ge(sg["yT"], g + 1)
                if has(g - 2):
                    v.wait_ge(sg["stored"], rise(g - 2, 15, 16))
                v.wait_ge(sg["residual"], g + 1)
                v.tensor_tensor(four(result[:, par, :]), x2_sb[:, bass.ds(GB * g, GB), :], four(p_front[:, :]),
                                ALU.add).then_inc(sg["result"], 1)

            def step(g, par):
                for k in range(NT):
                    v.wait_ge(sg["act"], rise(g, k, NT))
                    v.wait_ge(sg["up"], rise(g, k, NT))
                    v.tensor_tensor(act[:, k % 2, :], act[:, k % 2, :], p_up[k % 2][:, :], ALU.mult).then_inc(sg["gated"], 1)
                    v.wait_ge(sg["gated"], rise(g, k, NT))
                    v.wait_ge(sg["wb"], rise(g, k, NT))
                    if reached(g, k - 2, NT):
                        v.wait_ge(sg["h_lo"], rise(g, k - 2, NT))
                    v.tensor_tensor(h[:, k % 2, :], act[:, k % 2, :], p_wb[k % 2][:, :], ALU.mult).then_inc(sg["h"], 1)
                    if k == 5 and has(g - 1):
                        finish(g - 1, 1 - par)
                    if has(g + 1):
                        if k == 1:
                            layer_norm_stats(v, sg, x2_sb, g + 1, stats, mv)
                        if k == 4:
                            front_norm(g + 1)
                        if k == 6:
                            residual(g + 1)
                        if k == 9:
                            split_in(g + 1, 1 - par)
                        if k == 11:
                            rank_experts(g + 1)
                        if k == 12:
                            below_top(g + 1)
                        if k == 15:
                            shares(g + 1)

            for n in range(6):
                hi, lo = ((w1_hi, w1_lo), (w3_hi, w3_lo), (w2_hi, w2_lo))[n // 2]
                cols = bass.ts(n % 2, HALF)
                v.wait_ge((sg["raw0"], sg["raw1"])[n % 2], 16 * (n // 2 + 1))
                v.tensor_copy(hi[:, cols], raw[:, n % 2, :]).then_inc(sg["hi"], 1)
                v.wait_ge(sg["hi"], n + 1)
                v.tensor_tensor(lo[:, cols], raw[:, n % 2, :], f(hi[:, cols]), ALU.subtract).then_inc(sg["split"], 1)
            for n in range(2):
                v.wait_ge((sg["raw0"], sg["raw1"])[n], 16 * 4)
                v.tensor_copy(pick[:, bass.ts(n, HALF)], raw[0:2 * E, n, :]).then_inc(sg["split"], 1)
            v.wait_ge(sg["small"], 32)
            layer_norm_stats(v, sg, x2_sb, 0, stats, mv)
            front_norm(0)
            residual(0)
            split_in(0, 0)
            rank_experts(0)
            below_top(0)
            shares(0)
            over_groups(v, step)
            finish(NG - 1, 1)

        @block.gpsimd
        def _(p):
            def scales(g):
                p.wait_ge(sg["mean_var"], g + 1)
                p.tensor_tensor(rstd[:, :], mv[:, 0, :], mv[:, 0, :], ALU.mult).then_inc(sg["rstd_step"], 1)
                p.wait_ge(sg["rstd_step"], rise(g, 0, 4))
                p.tensor_tensor(rstd[:, :], rstd[:, :], mv[:, 1, :], ALU.add).then_inc(sg["rstd_step"], 1)
                p.wait_ge(sg["rstd_step"], rise(g, 1, 4))
                p.tensor_tensor(rstd[:, :], rstd[:, :], c["rms_eps"][:, 0:GB], ALU.add).then_inc(sg["rstd_step"], 1)
                p.wait_ge(sg["rstd_step"], rise(g, 2, 4))
                p.tensor_tensor(rstd[:, :], rstd[:, :], c["minus_half"][:, 0:GB], ALU.pow).then_inc(sg["rstd_step"], 1)

            def step(g, par):
                for k in range(NT):
                    p.wait_ge(sg["h_hi"], rise(g, k, NT))
                    if reached(g, k - RING, NT):
                        p.wait_ge(sg["y_out"], rise(g, k - RING, NT))
                    r = (par * NT + k) % RING
                    p.tensor_tensor(h_lo[:, r, :], h[:, k % 2, :], f(h_hi[:, r, :]), ALU.subtract).then_inc(sg["h_lo"], 1)
                    if k == 2 and has(g + 1):
                        scales(g + 1)

            scales(0)
            over_groups(p, step)


def constants(nc, ctx, io):
    def sb(name, shape, dt=F32):
        return ctx.enter_context(nc.sbuf_tensor(name, shape, dt))

    ident, cols, minus_half = sb("ident", [128, 128]), sb("cols", [128, NCOL]), sb("minus_half", [128, 8])
    ln_eps, rms_eps = sb("ln_eps", [128, GB]), sb("rms_eps", [128, GB])
    loaded = ctx.enter_context(nc.semaphore("const_loaded"))
    with nc.Block() as block:
        @block.sync
        def _(q):
            q.dma_start(ident[:, :], io["ident"]).then_inc(loaded, 16)
            q.dma_start(cols[:, :], io["cols"]).then_inc(loaded, 16)
            q.wait_ge(loaded, 32)

        @block.gpsimd
        def _(p):
            p.memset(minus_half[:, :], -0.5)
            p.memset(ln_eps[:, :], LN_EPS)
            p.memset(rms_eps[:, :], RMS_EPS)

    def col(name):
        i = COL[name] if isinstance(name, str) else len(COLS) + name
        return cols[:, i:i + 1]

    return {"ident": ident, "minus_half": minus_half, "ln_eps": ln_eps, "rms_eps": rms_eps, "col": col}


def program(nc, io):
    with ExitStack() as ctx:
        x_sb = ctx.enter_context(nc.sbuf_tensor("x_sb", [128, B, D], F32))
        c = constants(nc, ctx, io)
        layer0_gnn(nc, io, x_sb, c)
        layer0_ffn(nc, io, x_sb, c)
        layer1_gnn(nc, io, x_sb, c)
        x2_sb = ctx.enter_context(nc.sbuf_tensor("x2_sb", [128, B, D], F32))
        layer1_attention(nc, io, x_sb, x2_sb, c)
        layer1_ffn(nc, io, x_sb, x2_sb, c)


def laid_out(a):
    A = {k: np.asarray(v) for k, v in a.items()}
    rows = lambda m: np.ascontiguousarray(m)
    p = "L0_gnn_"
    w_ih, w_hh = A[p + "w_ih"], A[p + "w_hh"]
    small = [A[p + "conv1_w"][:, :, 0].T]
    small += [w_ih[k * D:(k + 1) * D, :D].T for k in range(3)]
    small += [w_ih[k * D:(k + 1) * D, D:].T for k in range(3)]
    small += [w_hh[k * D:(k + 1) * D].T for k in range(3)]
    bi, bh = A[p + "b_ih"].reshape(3, D), A[p + "b_hh"].reshape(3, D)
    cols = [A[p + n] for n in ("bn1_g", "bn1_b", "bn1_m", "bn1_v", "bn2_g", "bn2_b", "bn2_m", "bn2_v")]
    cols += [bi[0], bi[1], bi[2], bh[0], bh[1], bh[2], A["L0_ffn_gamma"], A["L0_ffn_beta"],
             A["L1_ffn_ln1_w"], A["L1_ffn_ln2_w"]]
    cols += list(A["L0_ffn_b1"].reshape(2 * E, 128))
    out = {
        "x": A["x"], "adj": A["adj"],
        "ident": np.eye(128, dtype=np.float32),
        "cols": rows(np.stack(cols, axis=1)),
        "small0": rows(np.concatenate(small, axis=1)),
        "conv2": rows(A[p + "conv2_w"].transpose(1, 2, 0).reshape(D, TAPS * D)),
        "w_msg": rows(A[p + "w_msg"].T), "b_msg": rows(np.broadcast_to(A[p + "b_msg"], (128, D))),
        "w_se": rows(A[p + "w_se"].T), "b_se": rows(A[p + "b_se"].reshape(3, 1)),
    }
    out.update(more(A, rows))
    return out


def more(A, rows):
    eye = np.eye(E, dtype=np.float32)
    q = "L0_ffn_"
    w1_0 = A[q + "W1"].transpose(1, 0, 2).reshape(D, E * H0)
    w2_0 = A[q + "W2"].reshape(2 * E, 128, D).transpose(1, 0, 2).reshape(128, 2 * E * D)
    freq = 1.0 / 10000.0 ** (np.arange(0, 32, 2, dtype=np.float32) / 32)
    angle = np.outer(np.arange(N, dtype=np.float32), freq)
    angle = np.concatenate([angle, angle], axis=-1).T
    sign = np.concatenate([-np.ones(16, np.float32), np.ones(16, np.float32)])[:, None]
    r = "L1_ffn_"
    swap = (np.arange(128) // 32) * 32 + (np.arange(128) % 32 + 16) % 32
    wq, wk = A[r + "wq"], np.repeat(A[r + "wk"].reshape(2, 32, D), 2, axis=0).reshape(D, D)
    s = "L1_gnn_"
    fill = NT * 128 - HALL
    packed = lambda w: np.concatenate([w.reshape(HALL, D), w.reshape(HALL, D)[:fill]], axis=0)
    pick = np.concatenate([np.repeat(eye, HID, axis=1), np.zeros((E, fill), np.float32)], axis=1)
    w2 = packed(A[r + "w2"].transpose(0, 2, 1)).reshape(NT, 128, D).transpose(1, 0, 2).reshape(128, NT * D)
    return {
        "w1_1": rows(packed(A[r + "w1"]).T), "w3_1": rows(packed(A[r + "w3"]).T), "w2_1": rows(w2),
        "pick_1": rows(np.concatenate([pick, pick], axis=0)), "w_route1": rows(A[r + "router_w"].T),
        "proj0": rows(np.concatenate([A[s + "W_q"].T, A[s + "W_k"].T], axis=1)),
        "w_v0": rows(A[s + "W_v"].T), "w_o0": rows(A[s + "W_o"].T),
        "w_edge": rows(np.broadcast_to(A[s + "W_e"].reshape(8), (128, 8))),
        "proj1": rows(np.concatenate([wq.T, wq[swap].T, wk.T, wk[swap].T], axis=1)),
        "w_v1": rows(A[r + "wv"].T), "w_o1": rows(A[r + "wo"].T),
        "cos": rows(np.tile(np.cos(angle), (4, 1))), "sin": rows(np.tile(np.sin(angle) * sign, (4, 1))),
        "causal": rows(np.triu(np.full((N, N), NEG, np.float32), 1)),
        "w1_0": rows(w1_0), "w2_0": rows(w2_0), "b2_0": rows(np.concatenate([A[q + "b2"]] * 2, axis=0)),
        "pick_0": rows(np.repeat(np.concatenate([eye, eye], axis=0), 128, axis=1)),
        "w_route0": rows(A[q + "Wr"]), "b_route0": rows(np.broadcast_to(A[q + "br"], (128, E))),
        "tri": rows(np.broadcast_to(np.tri(E, k=-1, dtype=np.float32).reshape(E * E), (128, E * E))),
    }


def kernel(**inputs):
    import concourse.bacc as bacc
    from concourse.bass_utils import run_bass_kernel_spmd as run

    arrays = laid_out(inputs)
    nc = bacc.Bacc("TRN2", target_bir_lowering=False, num_devices=1)
    io = {
        n: nc.dram_tensor("in_" + n, a.shape, mybir.dt.from_np(a.dtype), kind="ExternalInput").ap()
        for n, a in arrays.items()}
    io["out"] = nc.dram_tensor("out", (B, N, D), F32, kind="ExternalOutput").ap()
    program(nc, io)
    r = run(nc, [{"in_" + n: a for n, a in arrays.items()}], core_ids=[0])
    return r.results[0]["out"]
```

```python
from contextlib import ExitStack

import numpy as np

import concourse.bass as bass
from concourse import mybir

F32 = mybir.dt.float32
F32R = mybir.dt.float32r
BF16 = mybir.dt.bfloat16
ALU = mybir.AluOpType
ACT = mybir.ActivationFunctionType
AX = mybir.AxisListType

B, N, D = 64, 128, 128
GB = 4
NG = B // GB
W = GB * N
TAPS, PAD = 17, 8
E = 8
H0 = 256
HID = 341
HALL = E * HID
NT = (HALL + 127) // 128
PURE = HID // 128 * E
NEG = -1e30
LN_EPS, RMS_EPS = 1e-5, 1e-6
DOUBLE = 4

COLS = ["bn1_g", "bn1_b", "bn1_m", "bn1_v", "bn2_g", "bn2_b", "bn2_m", "bn2_v",
        "bi_r", "bi_z", "bi_n", "bh_r", "bh_z", "bh_n", "gamma", "beta", "ln1", "ln2"]
COL = {n: i for i, n in enumerate(COLS)}
NCOL = len(COLS) + 2 * E


def over_groups(eng, step):
    step(0, 0)
    step(1, 1)
    with eng.Fori(2, NG - 3, 2) as g:
        step(g, 0)
        step(g + 1, 1)
    step(NG - 2, 0)
    step(NG - 1, 1)


def rise(g, k, per):
    return g * per + (k + 1)


def reached(g, k, per):
    return not isinstance(g, int) or g * per + k >= 0


def has(g):
    return not isinstance(g, int) or 0 <= g < NG


def clear_behind(nc, sg):
    def leave(failed, *_):
        if not failed:
            sems = list(sg.values())
            with nc.Block() as block:
                @block.gpsimd
                def _(p):
                    for sem in sems[0::3]:
                        p.sem_clear(sem)

                @block.scalar
                def _(a):
                    for sem in sems[1::3]:
                        a.sem_clear(sem)

                @block.sync
                def _(q):
                    for sem in sems[2::3]:
                        q.sem_clear(sem)

    return leave


def mm3(t, out, w_hi, w_lo, x_hi, x_lo, start=True, stop=True):
    t.matmul(out, w_hi, x_hi, start=start, stop=False)
    t.matmul(out, w_hi, x_lo, start=False, stop=False)
    return t.matmul(out, w_lo, x_hi, start=False, stop=stop)


def f(ap):
    return ap.bitcast(F32)


def four(ap):
    return ap.rearrange("p (b n) -> p b n", b=GB)


def along(ap, shape):
    return ap.unsqueeze(ap.ndim).to_broadcast(shape)


def layer_norm_stats(v, sg, x_sb, g, stats, mv):
    for b in range(GB):
        i = v.bn_stats(stats[:, b, 0:6], x_sb[:, bass.ds(GB * g + b, 1), :].rearrange("p a d -> p (a d)"))
    i.then_inc(sg["stats"], 1)
    m0, q0, m1, q1, msum, mdif, qsum = (stats[:, :, k] for k in (1, 2, 4, 5, 6, 7, 8))
    v.wait_ge(sg["stats"], g + 1)
    v.tensor_tensor(msum, m0, m1, ALU.add)
    v.tensor_tensor(mdif, m0, m1, ALU.subtract)
    v.tensor_tensor(qsum, q0, q1, ALU.add).then_inc(sg["pairs"], 1)
    v.wait_ge(sg["pairs"], g + 1)
    v.scalar_tensor_tensor(mdif, mdif, 0.25, mdif, ALU.mult, ALU.mult)
    v.tensor_scalar(mv[:, 0, :], msum, 0.5, None, ALU.mult).then_inc(sg["squared"], 1)
    v.wait_ge(sg["squared"], g + 1)
    v.scalar_tensor_tensor(mv[:, 1, :], qsum, 1.0 / D, mdif, ALU.mult, ALU.add).then_inc(sg["mean_var"], 1)


def normalise(v, x_sb, g, mv, rstd, xn):
    for b in range(GB):
        i = v.tensor_scalar(xn[:, b, :], x_sb[:, bass.ds(GB * g + b, 1), :].rearrange("p a d -> p (a d)"),
                            mv[:, 0, b:b + 1], rstd[:, b:b + 1], ALU.subtract, ALU.mult)
    return i


def layer0_gnn(nc, io, x_sb, c):
    with ExitStack() as ctx:
        def sb(name, shape, dt=F32):
            return ctx.enter_context(nc.sbuf_tensor("g0_" + name, shape, dt))

        bank = [ctx.enter_context(nc.psum_tensor(f"g0_bank{i}", [128, W], F32)) for i in range(8)]
        p_back, p_conv, p_s, p_adjT, p_msg, p_r, p_z, p_hn = bank
        p_front, p_dist = p_s, p_s
        p_nmp, p_in = p_adjT, p_msg

        adj = sb("adj", [128, 2, GB, N])
        conv2_raw = sb("conv2_raw", [128, TAPS * D])
        conv2_hi, conv2_lo = sb("conv2_hi", [128, TAPS * D], F32R), sb("conv2_lo", [128, TAPS * D], F32R)
        small_raw = sb("small_raw", [128, 10 * D])
        small_hi, small_lo = sb("small_hi", [128, 10 * D], F32R), sb("small_lo", [128, 10 * D], F32R)
        w_msg, b_msg = sb("w_msg", [128, D]), sb("b_msg", [128, D])
        w_se, b_se = sb("w_se", [128, 3]), sb("b_se", [3, 1])
        half3 = sb("half3", [3, W])
        affine = sb("affine", [128, 16])
        bn1_scale, bn1_shift, bn2_scale, bn2_shift = (affine[:, i:i + 1] for i in range(4))
        half_br, half_bz, half_bhn = (affine[:, i:i + 1] for i in range(4, 7))
        tmp = sb("tmp", [128, 2])
        stats, mv = sb("stats", [128, GB, 9]), sb("mv", [128, 2, GB])
        rstd = sb("rstd", [128, GB])
        xn = sb("xn", [128, GB, D])
        xc = sb("xc", [128, 2, W])
        xcb = sb("xcb", [128, 2, W])
        xc_hi, xc_lo = sb("xc_hi", [128, W], F32R), sb("xc_lo", [128, W], F32R)
        h1 = sb("h1", [128, W])
        h1_hi = sb("h1_hi", [128, GB, N + 2 * PAD], F32R)
        h1_lo = sb("h1_lo", [128, GB, N + 2 * PAD], F32R)
        s3, s3sq = sb("s3", [3, W]), sb("s3sq", [3, W])
        ex, am = sb("ex", [128, W]), sb("am", [128, W])
        msg_pre, msg = sb("msg_pre", [128, W]), sb("msg", [128, W])
        cv = sb("cv", [128, W])
        cv_hi, cv_lo = sb("cv_hi", [128, W], F32R), sb("cv_lo", [128, W], F32R)
        nmp_hi, nmp_lo = sb("nmp_hi", [128, W], F32R), sb("nmp_lo", [128, W], F32R)
        tr, tz = sb("tr", [128, W]), sb("tz", [128, W])
        hn, pre_n, nn = sb("hn", [128, W]), sb("pre_n", [128, W]), sb("nn", [128, W])
        dx, upd = sb("dx", [128, W]), sb("upd", [128, W])

        sg = {n: ctx.enter_context(nc.semaphore("g0_" + n)) for n in """weights conv2_in conv2_head input prep_pool prep_vec split stats pairs squared mean_var var_eps rstd xn
            xT xc xc_hi xc_lo xcb conv1 h1 h1_hi h1_lo s_out s3 s3sq msg_out msg_pre msg adjT am gates_x dist ex
            conv2 cv cv_hi cv_lo nmp nmp_hi nmp_lo gates tr tz hn rn pre_n nn dx zx upd upT added""".split()}
        ctx.push(clear_behind(nc, sg))
        block = ctx.enter_context(nc.Block())
        n_weights = 5

        @block.sync
        def _(q):
            q.dma_start(small_raw[:, :], io["small0"]).then_inc(sg["weights"], 16)
            q.dma_start(w_msg[:, :], io["w_msg"]).then_inc(sg["weights"], 16)
            q.dma_start(b_msg[:, :], io["b_msg"]).then_inc(sg["weights"], 16)
            q.dma_start(w_se[:, :], io["w_se"]).then_inc(sg["weights"], 16)
            q.dma_start(b_se[:, :], io["b_se"]).then_inc(sg["weights"], 16)

            def step(g, par):
                if has(g - 2):
                    q.wait_ge(sg["adjT"], g - 1)
                if has(g - 1):
                    q.wait_ge(sg["input"], rise(g - 1, 31, 32))
                q.dma_start(x_sb[:, bass.ds(GB * g, GB), :],
                            io["x"][bass.ds(GB * g, GB), :, :].rearrange("b n d -> n b d")).then_inc(sg["input"], 16)
                q.dma_start(adj[:, par, :, :],
                            io["adj"][bass.ds(GB * g, GB), :, :].rearrange("b n m -> n b m")).then_inc(sg["input"], 16)

            over_groups(q, step)

        @block.tensor
        def _(t):
            def transpose_in(g):
                t.wait_ge(sg["xn"], g + 1)
                if has(g - 1):
                    t.wait_ge(sg["ex"], g)
                for b in range(GB):
                    i = t.transpose(p_front[:, bass.ts(b, N)], xn[:, b, :], c["ident"][:, :])
                i.then_inc(sg["xT"], 1)

            def transpose_back(g):
                t.wait_ge(sg["upd"], g + 1)
                if has(g - 1):
                    t.wait_ge(sg["added"], g)
                for b in range(GB):
                    i = t.transpose(p_back[:, bass.ts(b, N)], upd[:, bass.ts(b, N)], c["ident"][:, :])
                i.then_inc(sg["upT"], 1)

            def w(k):
                return small_hi[:, bass.ts(k, D)], small_lo[:, bass.ts(k, D)]

            def step(g, par):
                t.wait_ge(sg["xc_hi"], g + 1)
                t.wait_ge(sg["xc_lo"], g + 1)
                if has(g - 1):
                    t.wait_ge(sg["cv"], g)
                mm3(t, p_conv[:, :], *w(0), xc_hi[:, :], xc_lo[:, :]).then_inc(sg["conv1"], 1)
                t.matmul(p_s[0:3, :], w_se[:, :], xc[:, par, :], start=True, stop=True).then_inc(sg["s_out"], 1)
                if has(g - 1):
                    t.wait_ge(sg["nmp_lo"], g)
                t.wait_ge(sg["input"], rise(g, 31, 32))
                for b in range(GB):
                    i = t.transpose(p_adjT[:, bass.ts(b, N)], adj[:, par, b, :], c["ident"][:, :])
                i.then_inc(sg["adjT"], 1)
                if has(g - 1):
                    t.wait_ge(sg["tr"], g)
                mm3(t, p_r[:, :], *w(7), xc_hi[:, :], xc_lo[:, :], stop=False)
                if has(g - 1):
                    t.wait_ge(sg["pre_n"], g)
                for b in range(GB):
                    i = t.matmul(p_msg[:, bass.ts(b, N)], xc[:, par, bass.ts(b, N)], w_msg[:, :], start=True, stop=True)
                i.then_inc(sg["msg_out"], 1)
                t.wait_ge(sg["s3"], g + 1)
                t.wait_ge(sg["s3sq"], g + 1)
                for b in range(GB):
                    cols = bass.ts(b, N)
                    t.matmul(p_dist[:, cols], s3[:, cols], s3[:, cols], start=True, stop=False)
                    t.matmul(p_dist[:, cols], half3[:, cols], s3sq[:, cols], start=False, stop=False)
                    i = t.matmul(p_dist[:, cols], s3sq[:, cols], half3[:, cols], start=False, stop=True)
                i.then_inc(sg["dist"], 1)
                t.wait_ge(sg["h1_hi"], g + 1)
                t.wait_ge(sg["h1_lo"], g + 1)
                if not has(g - 1):
                    t.wait_ge(sg["split"], 2)
                for k in range(TAPS):
                    i = mm3(t, four(p_conv[:, :]), conv2_hi[:, bass.ts(k, D)], conv2_lo[:, bass.ts(k, D)],
                            h1_hi[:, :, k:k + N], h1_lo[:, :, k:k + N], start=k == 0, stop=k == TAPS - 1)
                i.then_inc(sg["conv2"], 1)
                if has(g - 1):
                    t.wait_ge(sg["tz"], g)
                if has(g - 1):
                    t.wait_ge(sg["hn"], g)
                mm3(t, p_z[:, :], *w(8), xc_hi[:, :], xc_lo[:, :], stop=False)
                mm3(t, p_hn[:, :], *w(9), xc_hi[:, :], xc_lo[:, :]).then_inc(sg["gates_x"], 1)
                if has(g - 1):
                    transpose_back(g - 1)
                if has(g + 1):
                    transpose_in(g + 1)
                t.wait_ge(sg["msg"], g + 1)
                t.wait_ge(sg["am"], g + 1)
                for b in range(GB):
                    i = t.matmul(p_nmp[:, bass.ts(b, N)], msg[:, bass.ts(b, N)], am[:, bass.ts(b, N)],
                                 start=True, stop=True)
                i.then_inc(sg["nmp"], 1)
                t.wait_ge(sg["msg_pre"], g + 1)
                t.wait_ge(sg["cv_hi"], g + 1)
                t.wait_ge(sg["cv_lo"], g + 1)
                for k, out in enumerate((p_r, p_z, p_in)):
                    mm3(t, out[:, :], *w(1 + k), cv_hi[:, :], cv_lo[:, :], start=k == 2, stop=False)
                t.wait_ge(sg["nmp_hi"], g + 1)
                t.wait_ge(sg["nmp_lo"], g + 1)
                for k, out in enumerate((p_r, p_z, p_in)):
                    i = mm3(t, out[:, :], *w(4 + k), nmp_hi[:, :], nmp_lo[:, :], start=False)
                i.then_inc(sg["gates"], 1)

            t.wait_ge(sg["split"], 1)
            t.wait_ge(sg["weights"], 16 * n_weights)
            transpose_in(0)
            over_groups(t, step)
            transpose_back(NG - 1)

        @block.scalar
        def _(a):
            def evacuate_in(g, par):
                a.wait_ge(sg["xT"], g + 1)
                if has(g - 2):
                    a.wait_ge(sg["zx"], g - 1)
                if has(g - 2):
                    a.wait_ge(sg["dx"], g - 1)
                a.activation(xc[:, par, :], p_front[:, :], ACT.Copy).then_inc(sg["xc"], 1)
                if has(g - 1):
                    a.wait_ge(sg["gates_x"], g)
                a.activation(xc_hi[:, :], p_front[:, :], ACT.Copy).then_inc(sg["xc_hi"], 1)

            def gates(g):
                a.wait_ge(sg["gates"], g + 1)
                if has(g - 1):
                    a.wait_ge(sg["zx"], g)
                a.activation(tr[:, :], p_r[:, :], ACT.Tanh, bias=half_br, scale=0.5).then_inc(sg["tr"], 1)
                a.activation(tz[:, :], p_z[:, :], ACT.Tanh, bias=half_bz, scale=0.5).then_inc(sg["tz"], 1)

            def new(g):
                a.wait_ge(sg["pre_n"], g + 1)
                if has(g - 1):
                    a.wait_ge(sg["upd"], g)
                a.activation(nn[:, :], pre_n[:, :], ACT.Tanh, bias=c["col"]("bi_n")).then_inc(sg["nn"], 1)

            def step(g, par):
                if has(g - 1):
                    gates(g - 1)
                a.wait_ge(sg["conv1"], g + 1)
                if has(g - 1):
                    a.wait_ge(sg["h1_lo"], g)
                a.activation(h1[:, :], p_conv[:, :], ACT.Relu, bias=bn1_shift, scale=bn1_scale).then_inc(sg["h1"], 1)
                a.wait_ge(sg["s_out"], g + 1)
                a.activation(s3[:, :], p_s[0:3, :], ACT.Identity, bias=b_se[:, :]).then_inc(sg["s3"], 1)
                a.activation(s3sq[:, :], p_s[0:3, :], ACT.Square, bias=b_se[:, :]).then_inc(sg["s3sq"], 1)
                a.wait_ge(sg["h1"], g + 1)
                a.activation(h1_hi[:, :, PAD:PAD + N], four(h1[:, :]), ACT.Copy).then_inc(sg["h1_hi"], 1)
                if has(g - 1):
                    new(g - 1)
                a.wait_ge(sg["msg_pre"], g + 1)
                if has(g - 1):
                    a.wait_ge(sg["nmp"], g)
                a.activation(msg[:, :], msg_pre[:, :], ACT.Relu).then_inc(sg["msg"], 1)
                a.wait_ge(sg["dist"], g + 1)
                if has(g - 1):
                    a.wait_ge(sg["am"], g)
                a.activation(ex[:, :], p_dist[:, :], ACT.Exp, scale=2.0).then_inc(sg["ex"], 1)
                a.wait_ge(sg["cv"], g + 1)
                a.activation(cv_hi[:, :], cv[:, :], ACT.Relu).then_inc(sg["cv_hi"], 1)
                if has(g + 1):
                    evacuate_in(g + 1, 1 - par)
                a.wait_ge(sg["nmp"], g + 1)
                a.activation(nmp_hi[:, :], p_nmp[:, :], ACT.Copy).then_inc(sg["nmp_hi"], 1)

            a.wait_ge(sg["weights"], 16 * n_weights)
            a.dma_start(conv2_raw[:, :], io["conv2"]).then_inc(sg["conv2_in"], 16)
            evacuate_in(0, 0)
            a.wait_ge(sg["conv2_in"], 16)
            a.activation(conv2_hi[:, :], conv2_raw[:, :], ACT.Copy).then_inc(sg["conv2_head"], 1)
            a.wait_ge(sg["prep_vec"], 9)
            a.wait_ge(sg["weights"], 16 * n_weights)
            over_groups(a, step)
            gates(NG - 1)
            new(NG - 1)

        @block.vector
        def _(v):
            def split_in(g, par):
                v.wait_ge(sg["xc"], g + 1)
                v.wait_ge(sg["xc_hi"], g + 1)
                if has(g - 1):
                    v.wait_ge(sg["gates_x"], g)
                v.tensor_tensor(xc_lo[:, :], xc[:, par, :], f(xc_hi[:, :]), ALU.subtract).then_inc(sg["xc_lo"], 1)

            def front_stats(g):
                v.wait_ge(sg["input"], rise(g, 31, 32))
                layer_norm_stats(v, sg, x_sb, g, stats, mv)

            def front_norm(g):
                v.wait_ge(sg["mean_var"], g + 1)
                v.wait_ge(sg["rstd"], g + 1)
                if has(g - 1):
                    v.wait_ge(sg["xT"], g)
                normalise(v, x_sb, g, mv, rstd, xn).then_inc(sg["xn"], 1)

            def gru_gates(g):
                v.wait_ge(sg["gates"], g + 1)
                v.tensor_scalar(hn[:, :], p_hn[:, :], 0.5, half_bhn, ALU.mult, ALU.add).then_inc(sg["hn"], 1)
                v.wait_ge(sg["hn"], g + 1)
                v.wait_ge(sg["tr"], g + 1)
                v.scalar_tensor_tensor(pre_n[:, :], tr[:, :], 1.0, hn[:, :], ALU.add, ALU.mult).then_inc(sg["rn"], 1)
                v.wait_ge(sg["rn"], g + 1)
                v.tensor_tensor(pre_n[:, :], pre_n[:, :], p_in[:, :], ALU.add).then_inc(sg["pre_n"], 1)

            def gru_out(g):
                v.wait_ge(sg["dx"], g + 1)
                v.wait_ge(sg["tz"], g + 1)
                v.scalar_tensor_tensor(dx[:, :], tz[:, :], 1.0, dx[:, :], ALU.add, ALU.mult).then_inc(sg["zx"], 1)
                v.wait_ge(sg["zx"], g + 1)
                v.wait_ge(sg["nn"], g + 1)
                if has(g - 1):
                    v.wait_ge(sg["upT"], g)
                v.scalar_tensor_tensor(upd[:, :], dx[:, :], 0.5, nn[:, :], ALU.mult, ALU.add).then_inc(sg["upd"], 1)

            def add_back(g):
                v.wait_ge(sg["upT"], g + 1)
                xg = x_sb[:, bass.ds(GB * g, GB), :]
                v.tensor_tensor(xg, xg, four(p_back[:, :]), ALU.add).then_inc(sg["added"], 1)

            def step(g, par):
                if has(g - 1):
                    gru_gates(g - 1)
                v.wait_ge(sg["h1_hi"], g + 1)
                v.tensor_tensor(h1_lo[:, :, PAD:PAD + N], four(h1[:, :]), f(h1_hi[:, :, PAD:PAD + N]),
                                ALU.subtract).then_inc(sg["h1_lo"], 1)
                v.wait_ge(sg["msg_out"], g + 1)
                if has(g - 1):
                    v.wait_ge(sg["msg"], g)
                v.tensor_tensor(four(msg_pre[:, :]), four(p_msg[:, :]), b_msg[:, :].unsqueeze(1).to_broadcast([128, GB, D]),
                                ALU.add).then_inc(sg["msg_pre"], 1)
                if has(g - 1):
                    gru_out(g - 1)
                if has(g + 1):
                    front_stats(g + 1)
                v.wait_ge(sg["adjT"], g + 1)
                v.wait_ge(sg["ex"], g + 1)
                if has(g - 1):
                    v.wait_ge(sg["nmp"], g)
                v.tensor_tensor(am[:, :], ex[:, :], p_adjT[:, :], ALU.mult).then_inc(sg["am"], 1)
                if has(g + 1):
                    front_norm(g + 1)
                v.wait_ge(sg["conv2"], g + 1)
                v.wait_ge(sg["xcb"], g + 1)
                v.scalar_tensor_tensor(cv[:, :], p_conv[:, :], bn2_scale, xcb[:, par, :], ALU.mult,
                                       ALU.add).then_inc(sg["cv"], 1)
                if has(g - 1):
                    add_back(g - 1)
                v.wait_ge(sg["cv_hi"], g + 1)
                v.scalar_tensor_tensor(cv_lo[:, :], cv[:, :], 0.0, f(cv_hi[:, :]), ALU.max,
                                       ALU.subtract).then_inc(sg["cv_lo"], 1)
                v.wait_ge(sg["nmp_hi"], g + 1)
                v.tensor_tensor(nmp_lo[:, :], p_nmp[:, :], f(nmp_hi[:, :]), ALU.subtract).then_inc(sg["nmp_lo"], 1)
                if has(g + 1):
                    split_in(g + 1, 1 - par)

            v.memset(h1_hi[:, :, :].bitcast(F32), 0.0)
            v.memset(h1_lo[:, :, :].bitcast(F32), 0.0)
            v.memset(half3[:, :], -0.5).then_inc(sg["prep_vec"], 1)
            v.wait_ge(sg["prep_pool"], 2)
            v.tensor_tensor(bn1_scale, c["col"]("bn1_g"), tmp[:, 0:1], ALU.mult).then_inc(sg["prep_vec"], 1)
            v.tensor_tensor(bn2_scale, c["col"]("bn2_g"), tmp[:, 1:2], ALU.mult).then_inc(sg["prep_vec"], 1)
            v.wait_ge(sg["prep_vec"], 3)
            v.tensor_tensor(bn1_shift, c["col"]("bn1_m"), bn1_scale, ALU.mult)
            v.tensor_tensor(bn2_shift, c["col"]("bn2_m"), bn2_scale, ALU.mult).then_inc(sg["prep_vec"], 1)
            v.wait_ge(sg["prep_vec"], 4)
            v.tensor_tensor(bn1_shift, c["col"]("bn1_b"), bn1_shift, ALU.subtract)
            v.tensor_tensor(bn2_shift, c["col"]("bn2_b"), bn2_shift, ALU.subtract).then_inc(sg["prep_vec"], 1)
            v.tensor_tensor(half_br, c["col"]("bi_r"), c["col"]("bh_r"), ALU.add)
            v.tensor_tensor(half_bz, c["col"]("bi_z"), c["col"]("bh_z"), ALU.add).then_inc(sg["prep_vec"], 1)
            v.tensor_scalar(half_bhn, c["col"]("bh_n"), 0.5, None, ALU.mult).then_inc(sg["prep_vec"], 1)
            v.wait_ge(sg["prep_vec"], 7)
            v.tensor_scalar(half_br, half_br, 0.5, None, ALU.mult).then_inc(sg["prep_vec"], 1)
            v.tensor_scalar(half_bz, half_bz, 0.5, None, ALU.mult).then_inc(sg["prep_vec"], 1)
            front_stats(0)
            v.wait_ge(sg["weights"], 16 * n_weights)
            v.tensor_copy(small_hi[:, :], small_raw[:, :]).then_inc(sg["prep_vec"], 1)
            v.wait_ge(sg["prep_vec"], 10)
            front_norm(0)
            v.tensor_tensor(small_lo[:, :], small_raw[:, :], f(small_hi[:, :]), ALU.subtract).then_inc(sg["split"], 1)
            split_in(0, 0)
            v.wait_ge(sg["conv2_head"], 1)
            v.tensor_tensor(conv2_lo[:, :], conv2_raw[:, :], f(conv2_hi[:, :]), ALU.subtract).then_inc(sg["split"], 1)
            over_groups(v, step)
            gru_gates(NG - 1)
            gru_out(NG - 1)
            add_back(NG - 1)

        @block.gpsimd
        def _(p):
            def front(g):
                p.wait_ge(sg["mean_var"], g + 1)
                p.tensor_tensor(rstd[:, :], mv[:, 1, :], c["ln_eps"][:, 0:GB], ALU.add).then_inc(sg["var_eps"], 1)
                p.wait_ge(sg["var_eps"], g + 1)
                p.tensor_tensor(rstd[:, :], rstd[:, :], c["minus_half"][:, 0:GB], ALU.pow).then_inc(sg["rstd"], 1)

            def shifted(g, par):
                p.wait_ge(sg["xc"], g + 1)
                if has(g - 2):
                    p.wait_ge(sg["cv"], g - 1)
                p.tensor_tensor(xcb[:, par, :], xc[:, par, :], bn2_shift.to_broadcast([128, W]), ALU.add).then_inc(sg["xcb"], 1)

            def gru_diff(g, par):
                p.wait_ge(sg["nn"], g + 1)
                if has(g - 1):
                    p.wait_ge(sg["upd"], g)
                p.tensor_tensor(dx[:, :], xc[:, par, :], nn[:, :], ALU.subtract).then_inc(sg["dx"], 1)

            def step(g, par):
                if has(g - 1):
                    gru_diff(g - 1, 1 - par)
                if has(g + 1):
                    front(g + 1)
                    shifted(g + 1, 1 - par)

            p.tensor_scalar(tmp[:, 0:1], c["col"]("bn1_v"), LN_EPS, None, ALU.add)
            p.tensor_scalar(tmp[:, 1:2], c["col"]("bn2_v"), LN_EPS, None, ALU.add).then_inc(sg["prep_pool"], 1)
            p.wait_ge(sg["prep_pool"], 1)
            p.tensor_tensor(tmp[:, :], tmp[:, :], c["minus_half"][:, 0:2], ALU.pow).then_inc(sg["prep_pool"], 1)
            p.wait_ge(sg["prep_vec"], 5)
            front(0)
            shifted(0, 0)
            over_groups(p, step)
            gru_diff(NG - 1, 1)


def ranks(v, sem, g, base, per, logits, gt, eq, rank, tri):
    mine = logits.unsqueeze(3).to_broadcast([128, GB, E, E])
    other = logits.unsqueeze(2).to_broadcast([128, GB, E, E])
    v.tensor_tensor(gt, other, mine, ALU.is_gt)
    v.tensor_tensor(eq, other, mine, ALU.is_equal).then_inc(sem, 1)
    v.wait_ge(sem, rise(g, base, per))
    v.tensor_tensor(eq, eq, tri, ALU.mult).then_inc(sem, 1)
    v.wait_ge(sem, rise(g, base + 1, per))
    v.tensor_tensor(gt, gt, eq, ALU.add).then_inc(sem, 1)
    v.wait_ge(sem, rise(g, base + 2, per))
    v.tensor_reduce(rank, gt, AX.X, ALU.add).then_inc(sem, 1)


def layer0_ffn(nc, io, x_sb, c):
    with ExitStack() as ctx:
        def sb(name, shape, dt=F32):
            return ctx.enter_context(nc.sbuf_tensor("f0_" + name, shape, dt))

        bank = [ctx.enter_context(nc.psum_tensor(f"f0_bank{i}", [128, W], F32)) for i in range(8)]
        p_h, p_wb, p_y, p_front, p_back = bank[0:2], bank[2:4], bank[4:6], bank[6], bank[7]

        C = 2 * E
        LAG = 6
        RING = 8
        w1_raw, w2_raw = sb("w1_raw", [128, C * 128]), sb("w2_raw", [128, C * 128])
        w1_hi, w1_lo = sb("w1_hi", [128, C * 128], F32R), sb("w1_lo", [128, C * 128], F32R)
        w2_hi, w2_lo = sb("w2_hi", [128, C * 128], F32R), sb("w2_lo", [128, C * 128], F32R)
        b2_raw = sb("b2_raw", [2 * E, D])
        b2_hi, b2_lo = sb("b2_hi", [2 * E, D], F32R), sb("b2_lo", [2 * E, D], F32R)
        pick_raw, pick = sb("pick_raw", [2 * E, E * 128]), sb("pick", [2 * E, E * 128], F32R)
        w_route, b_route, tri = sb("w_route", [128, E]), sb("b_route", [128, E]), sb("tri", [128, E * E])
        stats, mv, rstd = sb("stats", [128, GB, 9]), sb("mv", [128, 2, GB]), sb("rstd", [128, 2, GB])
        xn = sb("xn", [128, GB, D])
        xc = sb("xc", [128, W])
        xc_hi, xc_lo = sb("xc_hi", [128, 2, W], F32R), sb("xc_lo", [128, 2, W], F32R)
        logits = sb("logits", [128, GB, E])
        gt, eq = sb("gt", [128, GB, E, E]), sb("eq", [128, GB, E, E])
        rank, first, second = sb("rank", [128, GB, E]), sb("first", [128, GB, E]), sb("second", [128, GB, E])
        dif, both, prod = sb("dif", [128, GB, E]), sb("both", [128, GB, E]), sb("prod", [128, GB, E])
        gap, tanh_gap = sb("gap", [128, GB]), sb("tanh_gap", [128, GB])
        w_cat = sb("w_cat", [128, GB, 2 * E], F32R)
        wT = sb("wT", [2 * E, 2, W], F32R)
        h, hw = sb("h", [128, 4, W]), sb("hw", [128, 4, W])
        h_hi, h_lo = sb("h_hi", [128, RING, W], F32R), sb("h_lo", [128, RING, W], F32R)
        y = sb("y", [128, W])

        sg = {n: ctx.enter_context(nc.semaphore("f0_" + n)) for n in """weights w1 w2 b2_head hi split stats pairs squared mean_var rstd_step xn xT xc xc_hi xc_lo
            logits_out logits route gap tanh_gap w_cat wT_out wT wb h_out h hw h_hi h_lo h_lo_v y_out y yT added""".split()}
        ctx.push(clear_behind(nc, sg))
        block = ctx.enter_context(nc.Block())
        RSTD = DOUBLE
        ROUTE = 10

        def remainder_ready(eng, g, k):
            if k % 4 == 3:
                if reached(g, k // 4, C // 4):
                    eng.wait_ge(sg["h_lo_v"], rise(g, k // 4, C // 4))
            elif reached(g, k // 4 * 3 + k % 4, C // 4 * 3):
                eng.wait_ge(sg["h_lo"], rise(g, k // 4 * 3 + k % 4, C // 4 * 3))

        @block.sync
        def _(q):
            for dst, src in ((b2_raw, io["b2_0"]), (pick_raw, io["pick_0"]),
                             (w_route, io["w_route0"]), (b_route, io["b_route0"]), (tri, io["tri"])):
                q.dma_start(dst[:, :], src).then_inc(sg["weights"], 16)
            q.dma_start(w1_raw[:, :], io["w1_0"]).then_inc(sg["w1"], 16)
            q.dma_start(w2_raw[:, :], io["w2_0"]).then_inc(sg["w2"], 16)

        @block.tensor
        def _(t):
            def transpose_in(g):
                t.wait_ge(sg["xn"], g + 1)
                if has(g - 1):
                    t.wait_ge(sg["wT"], g)
                for b in range(GB):
                    i = t.transpose(p_front[:, bass.ts(b, N)], xn[:, b, :], c["ident"][:, :])
                i.then_inc(sg["xT"], 1)

            def route(g):
                t.wait_ge(sg["xc"], g + 1)
                t.wait_ge(sg["xc_hi"], g + 1)
                for b in range(GB):
                    i = t.matmul(p_front[:, b * E:(b + 1) * E], xc[:, bass.ts(b, N)], w_route[:, :], start=True, stop=True)
                i.then_inc(sg["logits_out"], 1)

            def weights_in(g):
                t.wait_ge(sg["w_cat"], g + 1)
                t.wait_ge(sg["logits"], g + 1)
                for b in range(GB):
                    i = t.transpose(p_front[0:2 * E, bass.ts(b, N)], f(w_cat[:, b, :]), c["ident"][:, :])
                i.then_inc(sg["wT_out"], 1)

            def transpose_back(g):
                t.wait_ge(sg["y"], g + 1)
                if has(g - 1):
                    t.wait_ge(sg["added"], g)
                for b in range(GB):
                    i = t.transpose(p_back[:, bass.ts(b, N)], y[:, bass.ts(b, N)], c["ident"][:, :])
                i.then_inc(sg["yT"], 1)

            def second(g, par, k):
                out = p_y[par][:, :]
                if k == 0:
                    if has(g - 2):
                        t.wait_ge(sg["y"], g - 1)
                    if not has(g - 1):
                        t.wait_ge(sg["split"], 3)
                    t.matmul(out, b2_hi[:, :], wT[:, par, :], start=True, stop=False)
                    t.matmul(out, b2_lo[:, :], wT[:, par, :], start=False, stop=False)
                t.wait_ge(sg["h_hi"], rise(g, k, C))
                remainder_ready(t, g, k)
                i = mm3(t, out, w2_hi[:, bass.ts(k, 128)], w2_lo[:, bass.ts(k, 128)],
                        h_hi[:, k % RING, :], h_lo[:, k % RING, :], start=False, stop=k == C - 1)
                i.then_inc(sg["y_out"], 1)

            def step(g, par):
                for k in range(C):
                    if k == 0:
                        t.wait_ge(sg["xc_hi"], g + 1)
                        t.wait_ge(sg["xc_lo"], g + 1)
                    if reached(g, k - 2, C):
                        t.wait_ge(sg["h"], rise(g, k - 2, C))
                    mm3(t, p_h[k % 2][:, :], w1_hi[:, bass.ts(k, 128)], w1_lo[:, bass.ts(k, 128)],
                        xc_hi[:, par, :], xc_lo[:, par, :]).then_inc(sg["h_out"], 1)
                    if k == 0:
                        if not has(g - 1):
                            weights_in(0)
                        t.wait_ge(sg["wT"], g + 1)
                    if k % 2 == 0:
                        e = k // 2
                        if reached(g, k - 3, C):
                            t.wait_ge(sg["hw"], rise(g, k - 3, C))
                        t.matmul(p_wb[e % 2][:, :], pick[:, bass.ts(e, 128)], wT[:, par, :],
                                 start=True, stop=True).then_inc(sg["wb"], 1)
                    if k >= LAG:
                        second(g, par, k - LAG)
                    elif has(g - 1):
                        second(g - 1, 1 - par, k - LAG + C)
                    if k == 3 and has(g + 1):
                        transpose_in(g + 1)
                    if k == 6 and has(g + 1):
                        route(g + 1)
                    if k == 8 and has(g - 1):
                        transpose_back(g - 1)
                    if k == 13 and has(g + 1):
                        weights_in(g + 1)

            transpose_in(0)
            t.wait_ge(sg["weights"], 16 * 5)
            route(0)
            t.wait_ge(sg["split"], 1)
            over_groups(t, step)
            for k in range(C - LAG, C):
                second(NG - 1, 1, k)
            transpose_back(NG - 1)

        @block.scalar
        def _(a):
            def evacuate_in(g, par):
                a.wait_ge(sg["xT"], g + 1)
                if has(g - 1):
                    a.wait_ge(sg["logits_out"], g)
                a.activation(xc[:, :], p_front[:, :], ACT.Identity, bias=c["col"]("beta"), scale=c["col"]("gamma")).then_inc(sg["xc"], 1)
                if reached(g, -C - 1, C):
                    a.wait_ge(sg["h_out"], rise(g, -C - 1, C))
                a.activation(xc_hi[:, par, :], p_front[:, :], ACT.Identity, bias=c["col"]("beta"),
                             scale=c["col"]("gamma")).then_inc(sg["xc_hi"], 1)

            def share(g):
                a.wait_ge(sg["gap"], g + 1)
                a.activation(tanh_gap[:, :], gap[:, :], ACT.Tanh, scale=0.5).then_inc(sg["tanh_gap"], 1)

            def weights_in(g, par):
                a.wait_ge(sg["wT_out"], g + 1)
                if reached(g, -2 * C, C):
                    a.wait_ge(sg["y_out"], rise(g, -2 * C, C))
                if reached(g, -E - 1, E):
                    a.wait_ge(sg["wb"], rise(g, -E - 1, E))
                a.activation(wT[:, par, :], p_front[0:2 * E, :], ACT.Copy).then_inc(sg["wT"], 1)

            def evacuate_y(g, par):
                a.wait_ge(sg["y_out"], rise(g, C - 1, C))
                if has(g - 1):
                    a.wait_ge(sg["yT"], g)
                a.activation(y[:, :], p_y[par][:, :], ACT.Copy).then_inc(sg["y"], 1)

            def head(g, k):
                a.wait_ge(sg["hw"], rise(g, k, C))
                if reached(g, k - RING, C):
                    a.wait_ge(sg["y_out"], rise(g, k - RING, C))
                a.activation(h_hi[:, k % RING, :], hw[:, k % 4, :], ACT.Copy).then_inc(sg["h_hi"], 1)

            def step(g, par):
                for k in range(C):
                    a.wait_ge(sg["h_out"], rise(g, k, C))
                    if reached(g, k - 4, C):
                        a.wait_ge(sg["hw"], rise(g, k - 4, C))
                    a.activation(h[:, k % 4, :], p_h[k % 2][:, :], ACT.Gelu, bias=c["col"](k)).then_inc(sg["h"], 1)
                    if k == 0 and not has(g - 1):
                        weights_in(0, 0)
                    if k >= 2 or has(g - 1):
                        head(g, k - 2)
                    if k == 4 and has(g + 1):
                        evacuate_in(g + 1, 1 - par)
                    if k == 6 and has(g - 1):
                        evacuate_y(g - 1, 1 - par)
                    if k == 10 and has(g + 1):
                        share(g + 1)
                    if k == 14 and has(g + 1):
                        weights_in(g + 1, 1 - par)

            evacuate_in(0, 0)
            a.wait_ge(sg["w1"], 16)
            a.activation(w1_hi[:, :], w1_raw[:, :], ACT.Copy).then_inc(sg["hi"], 1)
            share(0)
            a.wait_ge(sg["w2"], 16)
            a.activation(w2_hi[:, :], w2_raw[:, :], ACT.Copy).then_inc(sg["hi"], 1)
            over_groups(a, step)
            head(NG, -2)
            head(NG, -1)
            evacuate_y(NG - 1, 1)

        @block.vector
        def _(v):
            def front_norm(g):
                v.wait_ge(sg["rstd_step"], rise(g, RSTD - 1, RSTD))
                if has(g - 1):
                    v.wait_ge(sg["xT"], g)
                normalise(v, x_sb, g, mv, rstd[:, 1, :], xn).then_inc(sg["xn"], 1)

            def split_in(g, par):
                v.wait_ge(sg["xc"], g + 1)
                v.wait_ge(sg["xc_hi"], g + 1)
                v.tensor_tensor(xc_lo[:, par, :], xc[:, :], f(xc_hi[:, par, :]), ALU.subtract).then_inc(sg["xc_lo"], 1)

            def rank_experts(g):
                v.wait_ge(sg["logits_out"], g + 1)
                v.tensor_tensor(logits[:, :, :], p_front[:, 0:GB * E].rearrange("p (b e) -> p b e", b=GB),
                                b_route[:, :].unsqueeze(1).to_broadcast([128, GB, E]), ALU.add).then_inc(sg["logits"], 1)
                v.wait_ge(sg["logits"], g + 1)
                ranks(v, sg["route"], g, 0, ROUTE, logits[:, :, :], gt[:, :, :, :], eq[:, :, :, :],
                      rank[:, :, :], tri[:, :].rearrange("p (e j) -> p e j", e=E).unsqueeze(1).to_broadcast([128, GB, E, E]))

            def pick_two(g):
                v.wait_ge(sg["route"], rise(g, 3, ROUTE))
                v.tensor_scalar(first[:, :, :], rank[:, :, :], 0.0, None, ALU.is_equal)
                v.tensor_scalar(second[:, :, :], rank[:, :, :], 1.0, None, ALU.is_equal).then_inc(sg["route"], 1)
                v.wait_ge(sg["route"], rise(g, 4, ROUTE))
                v.tensor_tensor(dif[:, :, :], first[:, :, :], second[:, :, :], ALU.subtract)
                v.tensor_tensor(both[:, :, :], first[:, :, :], second[:, :, :], ALU.add).then_inc(sg["route"], 1)
                v.wait_ge(sg["route"], rise(g, 5, ROUTE))
                v.tensor_tensor(prod[:, :, :], logits[:, :, :], dif[:, :, :], ALU.mult).then_inc(sg["route"], 1)
                v.wait_ge(sg["route"], rise(g, 6, ROUTE))
                v.tensor_reduce(gap[:, :], prod[:, :, :], AX.X, ALU.add).then_inc(sg["gap"], 1)

            def shares(g):
                v.wait_ge(sg["tanh_gap"], g + 1)
                v.tensor_tensor(prod[:, :, :], dif[:, :, :], tanh_gap[:, :].unsqueeze(2).to_broadcast([128, GB, E]),
                                ALU.mult).then_inc(sg["route"], 1)
                v.wait_ge(sg["route"], rise(g, 7, ROUTE))
                v.tensor_tensor(prod[:, :, :], prod[:, :, :], both[:, :, :], ALU.add).then_inc(sg["route"], 1)
                v.wait_ge(sg["route"], rise(g, 8, ROUTE))
                if has(g - 1):
                    v.wait_ge(sg["wT_out"], g)
                v.tensor_scalar(w_cat[:, :, 0:E], prod[:, :, :], 0.5, None, ALU.mult).then_inc(sg["route"], 1)
                v.wait_ge(sg["route"], rise(g, 9, ROUTE))
                v.scalar_tensor_tensor(w_cat[:, :, E:2 * E], prod[:, :, :], 0.5, f(w_cat[:, :, 0:E]), ALU.mult,
                                       ALU.subtract).then_inc(sg["w_cat"], 1)

            def add_back(g):
                v.wait_ge(sg["yT"], g + 1)
                xg = x_sb[:, bass.ds(GB * g, GB), :]
                v.tensor_tensor(xg, xg, four(p_back[:, :]), ALU.add).then_inc(sg["added"], 1)

            def remainder(g, k):
                if k % 4 == 3:
                    v.wait_ge(sg["h_hi"], rise(g, k, C))
                    if reached(g, k - RING, C):
                        v.wait_ge(sg["y_out"], rise(g, k - RING, C))
                    v.tensor_tensor(h_lo[:, k % RING, :], hw[:, k % 4, :], f(h_hi[:, k % RING, :]),
                                    ALU.subtract).then_inc(sg["h_lo_v"], 1)

            def step(g, par):
                for k in range(C):
                    v.wait_ge(sg["h"], rise(g, k, C))
                    v.wait_ge(sg["wb"], rise(g, k // 2, E))
                    remainder_ready(v, g, k - 4)
                    v.tensor_tensor(hw[:, k % 4, :], h[:, k % 4, :], p_wb[k // 2 % 2][:, :], ALU.mult).then_inc(sg["hw"], 1)
                    if k >= 3 or has(g - 1):
                        remainder(g, k - 3)
                    if has(g + 1):
                        if k == 0:
                            front_norm(g + 1)
                        if k == 6:
                            split_in(g + 1, 1 - par)
                        if k == 7:
                            rank_experts(g + 1)
                        if k == 8:
                            pick_two(g + 1)
                        if k == 11:
                            shares(g + 1)
                    if k == 10 and has(g - 1):
                        add_back(g - 1)
                    if k == 12 and has(g + 2):
                        layer_norm_stats(v, sg, x_sb, g + 2, stats, mv)

            layer_norm_stats(v, sg, x_sb, 0, stats, mv)
            front_norm(0)
            v.wait_ge(sg["weights"], 16 * 5)
            v.tensor_copy(pick[:, :], pick_raw[:, :])
            v.tensor_copy(b2_hi[:, :], b2_raw[:, :]).then_inc(sg["b2_head"], 1)
            split_in(0, 0)
            rank_experts(0)
            pick_two(0)
            v.wait_ge(sg["hi"], 1)
            v.tensor_tensor(w1_lo[:, :], w1_raw[:, :], f(w1_hi[:, :]), ALU.subtract).then_inc(sg["split"], 1)
            shares(0)
            v.wait_ge(sg["hi"], 2)
            v.tensor_tensor(w2_lo[:, :], w2_raw[:, :], f(w2_hi[:, :]), ALU.subtract).then_inc(sg["split"], 1)
            v.wait_ge(sg["b2_head"], 1)
            v.tensor_tensor(b2_lo[:, :], b2_raw[:, :], f(b2_hi[:, :]), ALU.subtract).then_inc(sg["split"], 1)
            layer_norm_stats(v, sg, x_sb, 1, stats, mv)
            over_groups(v, step)
            for k in range(-3, 0):
                remainder(NG, k)
            add_back(NG - 1)

        @block.gpsimd
        def _(p):
            def front(g):
                double_norm_scale(p, sg, g, mv, rstd, c, c["ln_eps"])

            def remainder(g, k):
                p.wait_ge(sg["h_hi"], rise(g, k, C))
                if reached(g, k - RING, C):
                    p.wait_ge(sg["y_out"], rise(g, k - RING, C))
                p.tensor_tensor(h_lo[:, k % RING, :], hw[:, k % 4, :], f(h_hi[:, k % RING, :]),
                                ALU.subtract).then_inc(sg["h_lo"], 1)

            def step(g, par):
                for k in range(C):
                    if k % 4 != 3:
                        remainder(g, k)
                    if k == 12 and has(g + 2):
                        front(g + 2)

            front(0)
            front(1)
            over_groups(p, step)


def double_norm_scale(p, sg, g, mv, rstd, c, eps2):
    tt = p.tensor_tensor
    step = sg["rstd_step"]
    p.wait_ge(sg["mean_var"], g + 1)
    tt(rstd[:, 0, :], mv[:, 1, :], c["ln_eps"][:, 0:GB], ALU.add).then_inc(step, 1)
    p.wait_ge(step, rise(g, 0, DOUBLE))
    tt(rstd[:, 1, :], rstd[:, 0, :], eps2[:, 0:GB], ALU.mult).then_inc(step, 1)
    p.wait_ge(step, rise(g, 1, DOUBLE))
    tt(rstd[:, 1, :], rstd[:, 1, :], mv[:, 1, :], ALU.add).then_inc(step, 1)
    p.wait_ge(step, rise(g, 2, DOUBLE))
    tt(rstd[:, :, :], rstd[:, :, :], c["minus_half"][:, 0:2 * GB].rearrange("p (n b) -> p n b", n=2),
       ALU.pow).then_inc(step, 1)


def attention(nc, io, x_sb, x2_sb, c):
    rope = x2_sb is not None
    pre = "a1_" if rope else "a0_"
    H = 4 if rope else 8
    HD = D // H
    HALVES = H // 4
    U = GB * HALVES
    T_LAG, PV_LAG = (1, 2) if rope else (2, 3)
    EDGES = 4
    with ExitStack() as ctx:
        def sb(name, shape, dt=F32):
            return ctx.enter_context(nc.sbuf_tensor(pre + name, shape, dt))

        bank = [ctx.enter_context(nc.psum_tensor(f"{pre}bank{i}", [128, W], F32)) for i in range(8)]
        p_s, p_t, p_o, p_front, p_x = bank[0:2], bank[2:4], bank[4:6], bank[6], bank[7]

        NPROJ = 4 if rope else 2
        VH = 2 if rope else 8
        proj_raw = sb("proj_raw", [128, NPROJ * D])
        proj_hi, proj_lo = sb("proj_hi", [128, NPROJ * D], F32R), sb("proj_lo", [128, NPROJ * D], F32R)
        w_v, w_o = sb("w_v", [128, VH * HD]), sb("w_o", [128, D])
        ident_bf = sb("ident_bf", [128, 128], BF16)
        stats, mv, rstd = sb("stats", [128, GB, 9]), sb("mv", [128, 2, GB]), sb("rstd", [128, 2, GB])
        xn = sb("xn", [128, GB, D])
        xc = sb("xc", [128, 2, W])
        xc_hi, xc_lo = sb("xc_hi", [128, 2, W], F32R), sb("xc_lo", [128, 2, W], F32R)
        q_hi, q_lo = sb("q_hi", [128, 2, W], F32R), sb("q_lo", [128, 2, W], F32R)
        k_split = sb("k_split", [128, 2, W], F32R)
        k_hi, k_lo = k_split[:, 0, :], k_split[:, 1, :]
        k_blocks = sb("k_blocks", [128, 2, 2, H, GB, N], F32R)
        v_ones = sb("v_ones", [128, 2, GB, VH, HD + 1])
        top = sb("top", [128, 2, 4])
        probs, probsT = sb("probs", [128, 2, W]), sb("probsT", [128, 2, W])
        inv = sb("inv", [128, 2, 2 * H])
        yn, yT = sb("yn", [128, GB, D]), sb("yT", [128, W])
        if rope:
            cos, sin = sb("cos", [128, N]), sb("sin", [128, N])
            causal_raw, causal = sb("causal_raw", [128, N]), sb("causal", [128, N], BF16)
            rot_a, rot_b, rot = sb("rot_a", [128, 2, W]), sb("rot_b", [128, 2, W]), sb("rot", [128, 2, W])
        else:
            w_edge = sb("w_edge", [128, H])
            adj = sb("adj", [128, 2, GB, N])
            masked = sb("masked", [128, 2, GB, N], BF16)
            edge, scores = sb("edge", [128, EDGES, W]), sb("scores", [128, 2, W])

        sg = {n: ctx.enter_context(nc.semaphore(pre + n)) for n in """weights zeroed_v zeroed_p hi split input stats pairs squared mean_var rstd_step xn xT xc
            xc_hi xc_lo proj proj_a proj_b rot q_hi q_lo k_hi k_lo kb v_out v masked edge s_out scores top exp
            pT_out pT_v pT_a pv inv yn yT_out yT o_out added base""".split()}
        ctx.push(clear_behind(nc, sg))
        block = ctx.enter_context(nc.Block())
        loads = [(proj_raw, io["proj1"] if rope else io["proj0"]), (w_v, io["w_v1"] if rope else io["w_v0"]),
                 (w_o, io["w_o1"] if rope else io["w_o0"])]
        loads += [(cos, io["cos"]), (sin, io["sin"]), (causal_raw, io["causal"])] if rope else [(w_edge, io["w_edge"])]
        RSTD = DOUBLE if rope else 2
        SCALE = float(np.float32(1.0 / np.sqrt(np.float32(HD))))
        if rope:
            PE_PLAN = [[("front", 0), ("front", 1)], [("front", 2), ("front", 3)], [("front", 4), ("back", 0)],
                       [("in", 0), ("back", 1)]]
            ACT_Q, ACT_K, ACT_V, ACT_Y, ACT_IN = 2, 1, 3, 3, 0
            DVE_Q, DVE_K, DVE_NORM, DVE_ADD, DVE_HALF = 1, 0, 2, 3, 3
        else:
            PE_PLAN = [[("front", 0)], [], [("front", 1)], [], [("front", 2), ("back", 0)], [], [("in", 0), ("back", 1)], []]
            ACT_Q, ACT_K, ACT_V, ACT_Y, ACT_IN = 1, 3, 5, 5, 7
            DVE_Q, DVE_K, DVE_MASK, DVE_NORM, DVE_ADD, DVE_HALF = 1, 3, 6, 5, 7, 7

        def on_act(u):
            return not rope and u % 2 == 1

        def turned(eng, g, u):
            if rope and reached(g, u, U):
                eng.wait_ge(sg["pT_v"], rise(g, u, U))
            if not rope and reached(g, u // 2, U // 2):
                eng.wait_ge(sg["pT_a"] if on_act(u) else sg["pT_v"], rise(g, u // 2, U // 2))

        KB = 16 * H

        @block.sync
        def _(s):
            for dst, src in loads:
                s.dma_start(dst[:, :], src).then_inc(sg["weights"], 16)

            def load(g, par):
                if not rope:
                    if has(g - 2):
                        s.wait_ge(sg["masked"], g - 1)
                    if reached(g, -U - 1, U):
                        s.wait_ge(sg["edge"], rise(g, -U - 1, U))
                    s.dma_start(adj[:, par, :, :],
                                io["adj"][bass.ds(GB * g, GB), :, :].rearrange("b n m -> n b m")).then_inc(sg["input"], 16)

            def blocks(g, par):
                s.wait_ge(sg["k_hi"], g + 1)
                s.wait_ge(sg["k_lo"], g + 1)
                if reached(g, -U - 1, U):
                    s.wait_ge(sg["s_out"], rise(g, -U - 1, U))
                if not has(g - 2):
                    s.wait_ge(sg["zeroed_v"], 1)
                    s.wait_ge(sg["zeroed_p"], g + 1)
                if has(g - 1):
                    s.wait_ge(sg["kb"], rise(g - 1, KB - 1, KB))
                for h in range(H):
                    rows = slice(HD * h, HD * h + HD)
                    s.dma_start(f(k_blocks[rows, par, :, h, :, :]),
                                f(k_split[rows, :, :]).rearrange("p s (b n) -> p s b n", b=GB)).then_inc(sg["kb"], 16)

            def step(g, par):
                if has(g + 1):
                    if not rope:
                        s.wait_ge(sg["input"], rise(g, 15, 16))
                    load(g + 1, 1 - par)
                    blocks(g + 1, 1 - par)

            load(0, 0)
            blocks(0, 0)
            over_groups(s, step)

        @block.tensor
        def _(t):
            def transpose_in(g):
                t.wait_ge(sg["xn"], g + 1)
                if has(g - 1):
                    t.wait_ge(sg["v"], g)
                for b in range(GB):
                    i = t.transpose(p_front[:, bass.ts(b, N)], xn[:, b, :], c["ident"][:, :])
                i.then_inc(sg["xT"], 1)

            def project(g, par, n):
                if n == 0:
                    t.wait_ge(sg["xc_hi"], g + 1)
                    t.wait_ge(sg["xc_lo"], g + 1)
                elif not rope:
                    t.wait_ge(sg["q_lo"], g + 1)
                elif n == 1:
                    if has(g - 3):
                        t.wait_ge(sg["added"], g - 2)
                    if has(g - 1):
                        t.wait_ge(sg["proj_b"], rise(g - 1, 1, 2))
                elif n == 2:
                    t.wait_ge(sg["proj_a"], rise(g, 0, 2))
                else:
                    t.wait_ge(sg["proj_b"], rise(g, 0, 2))
                out = p_x if rope and n % 2 else p_front
                w = (n + 2) % 4 if rope else n
                mm3(t, out[:, :], proj_hi[:, bass.ts(w, D)], proj_lo[:, bass.ts(w, D)],
                    xc_hi[:, par, :], xc_lo[:, par, :]).then_inc(sg["proj"], 1)

            def values(g, par):
                if rope:
                    t.wait_ge(sg["proj_a"], rise(g, 1, 2))
                else:
                    t.wait_ge(sg["k_lo"], g + 1)
                width = VH * HD
                for b in range(GB):
                    i = t.matmul(p_front[:, b * width:(b + 1) * width], xc[:, par, bass.ts(b, N)], w_v[:, :],
                                 start=True, stop=True)
                i.then_inc(sg["v_out"], 1)

            def score(g, par, u):
                b, half = divmod(u, HALVES)
                out = p_s[u % 2][:, :]
                if u == 0:
                    t.wait_ge(sg["q_hi"], g + 1)
                    t.wait_ge(sg["q_lo"], g + 1)
                    t.wait_ge(sg["kb"], rise(g, KB - 1, KB))
                    if not rope:
                        t.wait_ge(sg["masked"], g + 1)
                if reached(g, u - 2, U):
                    t.wait_ge(sg["exp"] if rope else sg["scores"], rise(g, u - 2, U))
                mask = causal[:, :] if rope else masked[:, par, b, :]
                t.matmul(four(out), ident_bf[:, :], mask.unsqueeze(1).to_broadcast([128, 4, N]), start=True, stop=False)
                heads, nodes = slice(4 * half, 4 * half + 4), bass.ts(b, N)
                mm3(t, four(out), q_hi[:, par, nodes], q_lo[:, par, nodes], k_blocks[:, par, 0, heads, b, :],
                    k_blocks[:, par, 1, heads, b, :], start=False).then_inc(sg["s_out"], 1)

            def turn(g, u):
                t.wait_ge(sg["exp"], rise(g, u, U))
                turned(t, g, u - 2)
                for h in range(4):
                    i = t.transpose(p_t[u % 2][:, bass.ts(h, N)], probs[:, u % 2, bass.ts(h, N)], c["ident"][:, :])
                i.then_inc(sg["pT_out"], 1)

            def weigh(g, par, u):
                b, half = divmod(u, HALVES)
                if u == 0:
                    t.wait_ge(sg["v"], g + 1)
                if u % (U // 2) == 0 and has(g - 1):
                    t.wait_ge(sg["yn"], rise(g - 1, u // (U // 2), 2))
                turned(t, g, u)
                for h in range(4):
                    head = 4 * half + h
                    o = ((b % 2) * H + head) * (HD + 1)
                    i = t.matmul(p_o[b // 2][:, o:o + HD + 1], probsT[:, u % 2, bass.ts(h, N)],
                                 v_ones[:, par, b, head * VH // H, :], start=True, stop=True)
                i.then_inc(sg["pv"], 1)

            def turn_y(g):
                t.wait_ge(sg["yn"], rise(g, 1, 2))
                if has(g - 1):
                    t.wait_ge(sg["added"], g)
                if rope and has(g + 2):
                    t.wait_ge(sg["proj_b"], rise(g + 2, 1, 2))
                for b in range(GB):
                    i = t.transpose(p_x[:, bass.ts(b, N)], yn[:, b, :], c["ident"][:, :])
                i.then_inc(sg["yT_out"], 1)

            def out_product(g):
                t.wait_ge(sg["yT"], g + 1)
                for b in range(GB):
                    i = t.matmul(p_x[:, bass.ts(b, N)], yT[:, bass.ts(b, N)], w_o[:, :], start=True, stop=True)
                i.then_inc(sg["o_out"], 1)

            def front(g, par, n):
                if n < NPROJ:
                    project(g, par, n)
                else:
                    values(g, par)

            def step(g, par):
                for u in range(U):
                    score(g, par, u)
                    if u >= T_LAG:
                        turn(g, u - T_LAG)
                    elif has(g - 1):
                        turn(g - 1, u - T_LAG + U)
                    if u >= PV_LAG:
                        weigh(g, par, u - PV_LAG)
                    elif has(g - 1):
                        weigh(g - 1, 1 - par, u - PV_LAG + U)
                    for side, n in PE_PLAN[u]:
                        if side == "back" and has(g - 1):
                            (turn_y, out_product)[n](g - 1)
                        if side == "front" and has(g + 1):
                            front(g + 1, 1 - par, n)
                        if side == "in" and has(g + 2):
                            transpose_in(g + 2)

            transpose_in(0)
            t.wait_ge(sg["weights"], 16 * len(loads))
            t.wait_ge(sg["split"], 1)
            for n in range(NPROJ + 1):
                front(0, 0, n)
            transpose_in(1)
            over_groups(t, step)
            for j in range(PV_LAG):
                if j < T_LAG:
                    turn(NG - 1, U - T_LAG + j)
                weigh(NG - 1, 1, U - PV_LAG + j)
            turn_y(NG - 1)
            out_product(NG - 1)

        @block.scalar
        def _(a):
            def evacuate_in(g, par):
                a.wait_ge(sg["xT"], g + 1)
                if rope:
                    a.activation(xc[:, par, :], p_front[:, :], ACT.Copy, scale=c["col"]("ln1")).then_inc(sg["xc"], 1)
                    a.activation(xc_hi[:, par, :], p_front[:, :], ACT.Copy, scale=c["col"]("ln1")).then_inc(sg["xc_hi"], 1)
                else:
                    a.activation(xc[:, par, :], p_front[:, :], ACT.Copy).then_inc(sg["xc"], 1)
                    a.activation(xc_hi[:, par, :], p_front[:, :], ACT.Copy).then_inc(sg["xc_hi"], 1)

            def q_head(g, par):
                if reached(g, -U - 1, U):
                    a.wait_ge(sg["s_out"], rise(g, -U - 1, U))
                if rope:
                    a.wait_ge(sg["rot"], rise(g, 1, 2))
                    a.activation(q_hi[:, par, :], rot[:, 1, :], ACT.Copy).then_inc(sg["q_hi"], 1)
                else:
                    a.wait_ge(sg["proj"], rise(g, 0, 2))
                    a.activation(q_hi[:, par, :], p_front[:, :], ACT.Copy, scale=SCALE).then_inc(sg["q_hi"], 1)

            def k_head(g):
                if has(g - 1):
                    a.wait_ge(sg["kb"], rise(g - 1, KB - 1, KB))
                if rope:
                    a.wait_ge(sg["rot"], rise(g, 0, 2))
                    a.activation(k_hi, rot[:, 0, :], ACT.Copy).then_inc(sg["k_hi"], 1)
                else:
                    a.wait_ge(sg["proj"], rise(g, 1, 2))
                    a.activation(k_hi, p_front[:, :], ACT.Copy).then_inc(sg["k_hi"], 1)

            def values(g, par):
                a.wait_ge(sg["v_out"], g + 1)
                if reached(g, -U - 1, U):
                    a.wait_ge(sg["pv"], rise(g, -U - 1, U))
                a.activation(v_ones[:, par, :, :, 0:HD],
                             p_front[:, 0:GB * VH * HD].rearrange("p (b h d) -> p b h d", b=GB, h=VH),
                             ACT.Copy).then_inc(sg["v"], 1)

            def exponent(g, u):
                a.wait_ge(sg["top"], rise(g, u, U))
                if reached(g, u - 2, U):
                    a.wait_ge(sg["pT_out"], rise(g, u - 2, U))
                src = p_s[u % 2][:, :] if rope else scores[:, u % 2, :]
                for h in range(4):
                    i = a.activation(probs[:, u % 2, bass.ts(h, N)], src[:, bass.ts(h, N)], ACT.Exp,
                                     bias=top[:, u % 2, h:h + 1])
                i.then_inc(sg["exp"], 1)

            def evacuate_turned(g, u):
                a.wait_ge(sg["pT_out"], rise(g, u, U))
                if reached(g, u - 2, U):
                    a.wait_ge(sg["pv"], rise(g, u - 2, U))
                a.activation(probsT[:, u % 2, :], p_t[u % 2][:, :], ACT.Copy).then_inc(sg["pT_a"], 1)

            def y_in(g):
                a.wait_ge(sg["yT_out"], g + 1)
                if has(g - 1):
                    a.wait_ge(sg["o_out"], g)
                a.activation(yT[:, :], p_x[:, :], ACT.Copy).then_inc(sg["yT"], 1)

            def step(g, par):
                for u in range(U):
                    if on_act(u - T_LAG):
                        if u >= T_LAG:
                            evacuate_turned(g, u - T_LAG)
                        elif has(g - 1):
                            evacuate_turned(g - 1, u - T_LAG + U)
                    if has(g + 1):
                        if rope and u == ACT_IN:
                            evacuate_in(g + 1, 1 - par)
                        if not rope and u == ACT_Q:
                            q_head(g + 1, 1 - par)
                        if u == ACT_K:
                            k_head(g + 1)
                        if u == ACT_V:
                            values(g + 1, 1 - par)
                    if not rope and has(g + 2) and u == ACT_IN:
                        evacuate_in(g + 2, par)
                    if has(g - 1) and u == ACT_Y:
                        y_in(g - 1)
                    exponent(g, u)
                    if rope and has(g + 1) and u == ACT_Q:
                        q_head(g + 1, 1 - par)

            evacuate_in(0, 0)
            for part in ("kq" if rope else "qk"):
                if part == "k":
                    k_head(0)
                else:
                    q_head(0, 0)
            values(0, 0)
            if not rope:
                evacuate_in(1, 1)
            over_groups(a, step)
            for u in range(U - T_LAG, U):
                if on_act(u):
                    evacuate_turned(NG - 1, u)
            y_in(NG - 1)

        @block.vector
        def _(v):
            def front_norm(g):
                v.wait_ge(sg["rstd_step"], rise(g, RSTD - 1, RSTD))
                if has(g - 1):
                    v.wait_ge(sg["xT"], g)
                normalise(v, x_sb, g, mv, rstd[:, 1 if rope else 0, :], xn).then_inc(sg["xn"], 1)

            def residual(g):
                normalise(v, x_sb, g, mv, rstd[:, 0, :], x2_sb[:, bass.ds(GB * g, GB), :]).then_inc(sg["base"], 1)

            def front_q(g, par):
                if rope:
                    rotate(g, 1)
                else:
                    v.wait_ge(sg["q_hi"], g + 1)
                    v.scalar_tensor_tensor(q_lo[:, par, :], p_front[:, :], SCALE, f(q_hi[:, par, :]), ALU.mult,
                                           ALU.subtract).then_inc(sg["q_lo"], 1)

            def front_k(g):
                if rope:
                    rotate(g, 0)
                else:
                    v.wait_ge(sg["k_hi"], g + 1)
                    v.tensor_tensor(k_lo, p_front[:, :], f(k_hi), ALU.subtract).then_inc(sg["k_lo"], 1)

            def rotate(g, n):
                v.wait_ge(sg["proj"], rise(g, 2 * n, 4))
                if has(g - 1):
                    v.wait_ge(sg["rot"], rise(g - 1, 1, 2))
                scale = SCALE if n else 1.0
                v.scalar_tensor_tensor(four(rot_a[:, n, :]), four(p_front[:, :]), scale,
                                       cos[:, :].unsqueeze(1).to_broadcast([128, GB, N]), ALU.mult, ALU.mult).then_inc(sg["proj_a"], 1)
                v.wait_ge(sg["proj"], rise(g, 2 * n + 1, 4))
                v.scalar_tensor_tensor(four(rot_b[:, n, :]), four(p_x[:, :]), scale,
                                       sin[:, :].unsqueeze(1).to_broadcast([128, GB, N]), ALU.mult, ALU.mult).then_inc(sg["proj_b"], 1)

            def mask(g, par):
                v.wait_ge(sg["input"], rise(g, 15, 16))
                if reached(g, -U - 1, U):
                    v.wait_ge(sg["s_out"], rise(g, -U - 1, U))
                v.tensor_scalar(masked[:, par, :, :], adj[:, par, :, :], 0.0, NEG, ALU.is_equal,
                                ALU.mult).then_inc(sg["masked"], 1)

            def unit(g, u):
                v.wait_ge(sg["s_out"], rise(g, u, U))
                if reached(g, u - 2, U):
                    v.wait_ge(sg["exp"], rise(g, u - 2, U))
                src = p_s[u % 2]
                if not rope:
                    v.wait_ge(sg["edge"], rise(g, u, U))
                    v.tensor_tensor(scores[:, u % 2, :], p_s[u % 2][:, :], edge[:, u % EDGES, :], ALU.add).then_inc(sg["scores"], 1)
                    v.wait_ge(sg["scores"], rise(g, u, U))
                    src = scores[:, u % 2, :]
                v.tensor_reduce(top[:, u % 2, :], four(src[:, :]), AX.X, ALU.max, negate=True).then_inc(sg["top"], 1)

            def evacuate_turned(g, u):
                v.wait_ge(sg["pT_out"], rise(g, u, U))
                if reached(g, u - 2, U):
                    v.wait_ge(sg["pv"], rise(g, u - 2, U))
                v.tensor_copy(probsT[:, u % 2, :], p_t[u % 2][:, :]).then_inc(sg["pT_v"], 1)

            def divide(g, n):
                v.wait_ge(sg["pv"], rise(g, (n + 1) * (U // 2) - 1, U))
                if has(g - 1):
                    v.wait_ge(sg["yT_out"], g)
                out = p_o[n][:, 0:2 * H * (HD + 1)].rearrange("p (h d) -> p h d", d=HD + 1)
                v.reciprocal(inv[:, n, :], out[:, :, HD]).then_inc(sg["inv"], 1)
                v.wait_ge(sg["inv"], rise(g, n, 2))
                v.tensor_tensor(yn[:, 2 * n:2 * n + 2, :].rearrange("p b (h d) -> p (b h) d", h=H),
                                out[:, :, 0:HD], inv[:, n, :].unsqueeze(2).to_broadcast([128, 2 * H, HD]),
                                ALU.mult).then_inc(sg["yn"], 1)

            def add_back(g):
                v.wait_ge(sg["o_out"], g + 1)
                xg = (x2_sb if rope else x_sb)[:, bass.ds(GB * g, GB), :]
                if rope:
                    v.wait_ge(sg["base"], g + 1)
                v.tensor_tensor(xg, xg, four(p_x[:, :]), ALU.add).then_inc(sg["added"], 1)

            def step(g, par):
                for u in range(U):
                    unit(g, u)
                    if not on_act(u - T_LAG):
                        if u >= T_LAG:
                            evacuate_turned(g, u - T_LAG)
                        elif has(g - 1):
                            evacuate_turned(g - 1, u - T_LAG + U)
                    if has(g + 1):
                        if u == DVE_Q:
                            front_q(g + 1, 1 - par)
                        if u == DVE_K:
                            front_k(g + 1)
                        if not rope and u == DVE_MASK:
                            mask(g + 1, 1 - par)
                    if has(g - 1) and u == PV_LAG - 1:
                        divide(g - 1, 1)
                    if u == DVE_HALF:
                        divide(g, 0)
                    if has(g + 2):
                        if u == 0:
                            layer_norm_stats(v, sg, x_sb, g + 2, stats, mv)
                        if u == DVE_NORM:
                            front_norm(g + 2)
                    if has(g - 1) and u == DVE_ADD:
                        add_back(g - 1)
                    if rope and has(g + 2) and u == DVE_NORM:
                        residual(g + 2)

            layer_norm_stats(v, sg, x_sb, 0, stats, mv)
            v.memset(v_ones[:, :, :, :, HD:HD + 1], 1.0)
            front_norm(0)
            v.wait_ge(sg["weights"], 16 * len(loads))
            v.tensor_copy(proj_hi[:, :], proj_raw[:, :]).then_inc(sg["hi"], 1)
            v.wait_ge(sg["hi"], 1)
            v.tensor_tensor(proj_lo[:, :], proj_raw[:, :], f(proj_hi[:, :]), ALU.subtract).then_inc(sg["split"], 1)
            v.tensor_copy(ident_bf[:, :], c["ident"][:, :])
            if rope:
                v.tensor_copy(causal[:, :], causal_raw[:, :])
                residual(0)
            else:
                mask(0, 0)
            v.memset(f(k_blocks[:, 0, 0, :, :, :]), 0.0).then_inc(sg["zeroed_v"], 1)
            for part in ("kq" if rope else "qk"):
                if part == "k":
                    front_k(0)
                else:
                    front_q(0, 0)
            layer_norm_stats(v, sg, x_sb, 1, stats, mv)
            front_norm(1)
            if rope:
                residual(1)
            over_groups(v, step)
            for u in range(U - T_LAG, U):
                if not on_act(u):
                    evacuate_turned(NG - 1, u)
            divide(NG - 1, 1)
            add_back(NG - 1)

        @block.gpsimd
        def _(p):
            def scales(g):
                if rope:
                    double_norm_scale(p, sg, g, mv, rstd, c, c["rms_eps"])
                else:
                    p.wait_ge(sg["mean_var"], g + 1)
                    p.tensor_tensor(rstd[:, 0, :], mv[:, 1, :], c["ln_eps"][:, 0:GB], ALU.add).then_inc(sg["rstd_step"], 1)
                    p.wait_ge(sg["rstd_step"], rise(g, 0, RSTD))
                    p.tensor_tensor(rstd[:, 0, :], rstd[:, 0, :], c["minus_half"][:, 0:GB], ALU.pow).then_inc(sg["rstd_step"], 1)

            def split_in(g, par):
                p.wait_ge(sg["xc"], g + 1)
                p.wait_ge(sg["xc_hi"], g + 1)
                p.tensor_tensor(xc_lo[:, par, :], xc[:, par, :], f(xc_hi[:, par, :]), ALU.subtract).then_inc(sg["xc_lo"], 1)

            def edge_bias(g, par, u):
                b, half = divmod(u, HALVES)
                if u == 0:
                    p.wait_ge(sg["input"], rise(g, 15, 16))
                if reached(g, u - EDGES, U):
                    p.wait_ge(sg["scores"], rise(g, u - EDGES, U))
                p.tensor_tensor(four(edge[:, u % EDGES, :]), adj[:, par, b, :].unsqueeze(1).to_broadcast([128, 4, N]),
                                w_edge[:, 4 * half:4 * half + 4].unsqueeze(2).to_broadcast([128, 4, N]),
                                ALU.mult).then_inc(sg["edge"], 1)

            def rotated(g, par, n):
                p.wait_ge(sg["proj_b"], rise(g, n, 2))
                if has(g - 1):
                    p.wait_ge(sg["q_lo"] if n else sg["k_lo"], g)
                    p.wait_ge(sg["q_hi"] if n else sg["k_hi"], g)
                p.tensor_tensor(rot[:, n, :], rot_a[:, n, :], rot_b[:, n, :], ALU.add).then_inc(sg["rot"], 1)
                hi, lo, s_hi, s_lo = ((q_hi[:, par, :], q_lo[:, par, :], sg["q_hi"], sg["q_lo"]) if n else
                                      (k_hi, k_lo, sg["k_hi"], sg["k_lo"]))
                p.wait_ge(s_hi, g + 1)
                p.tensor_tensor(lo, rot[:, n, :], f(hi), ALU.subtract).then_inc(s_lo, 1)

            def step(g, par):
                for u in range(U):
                    if not rope:
                        edge_bias(g, par, u)
                    if has(g + 1) and u == 0:
                        split_in(g + 1, 1 - par)
                    if rope and has(g + 1) and u in (DVE_Q, DVE_K):
                        rotated(g + 1, 1 - par, int(u == DVE_Q))
                    if has(g + 2) and u == (0 if rope else 3):
                        scales(g + 2)

            scales(0)
            split_in(0, 0)
            p.memset(f(k_blocks[:, 0, 1, :, :, :]), 0.0).then_inc(sg["zeroed_p"], 1)
            if not rope:
                p.wait_ge(sg["weights"], 16 * len(loads))
            if rope:
                rotated(0, 0, 0)
                rotated(0, 0, 1)
            p.memset(f(k_blocks[:, 1, :, :, :, :]), 0.0).then_inc(sg["zeroed_p"], 1)
            scales(1)
            over_groups(p, step)


def layer1_gnn(nc, io, x_sb, c):
    attention(nc, io, x_sb, None, c)


def layer1_attention(nc, io, x_sb, x2_sb, c):
    attention(nc, io, x_sb, x2_sb, c)


def layer1_ffn(nc, io, x_sb, x2_sb, c):
    with ExitStack() as ctx:
        def sb(name, shape, dt=F32):
            return ctx.enter_context(nc.sbuf_tensor("f1_" + name, shape, dt))

        bank = [ctx.enter_context(nc.psum_tensor(f"f1_bank{i}", [128, W], F32)) for i in range(8)]
        p_gate, p_up, p_wb, p_y, p_front = bank[0:2], bank[2:4], bank[4:6], bank[6], bank[7]

        NWB = E + NT - PURE
        PICK = NWB * 128
        LAG = 4
        RING = 4
        HALF = NT * 128 // 2
        first, last = slice(0, HALF), slice(HALF, 2 * HALF)
        raw = sb("raw", [128, 2, HALF])
        w1_hi, w1_lo = sb("w1_hi", [128, NT * 128], F32R), sb("w1_lo", [128, NT * 128], F32R)
        w3_hi, w3_lo = sb("w3_hi", [128, NT * 128], F32R), sb("w3_lo", [128, NT * 128], F32R)
        w2_hi, w2_lo = sb("w2_hi", [128, NT * 128], F32R), sb("w2_lo", [128, NT * 128], F32R)
        pick = sb("pick", [2 * E, NWB * 128], F32R)
        w_route, tri = sb("w_route", [128, E]), sb("tri", [128, E * E])
        stats, mv, rstd = sb("stats", [128, GB, 9]), sb("mv", [128, 2, GB]), sb("rstd", [128, GB])
        xn, xc = sb("xn", [128, GB, D]), sb("xc", [128, W])
        xc_hi, xc_lo = sb("xc_hi", [128, 2, W], F32R), sb("xc_lo", [128, 2, W], F32R)
        logits = sb("logits", [128, GB, E])
        gt, eq = sb("gt", [128, GB, E, E]), sb("eq", [128, GB, E, E])
        rank, chosen = sb("rank", [128, GB, E]), sb("chosen", [128, GB, E])
        ex, share = sb("ex", [128, GB, E]), sb("share", [128, GB, E])
        top, total, kept = sb("top", [128, GB]), sb("total", [128, GB]), sb("kept", [128, GB])
        w_cat, wT = sb("w_cat", [128, GB, 2 * E], F32R), sb("wT", [2 * E, 2, W], F32R)
        act, h = sb("act", [128, 4, W]), sb("h", [128, 4, W])
        h_hi, h_lo = sb("h_hi", [128, RING, W], F32R), sb("h_lo", [128, RING, W], F32R)
        y = sb("y", [128, W])

        sg = {n: ctx.enter_context(nc.semaphore("f1_" + n)) for n in """small w1a w3a w2a w1b w3b w2b pick_in pick hi lo_vec lo_pool stats pairs squared mean_var rstd_step xn xT xc xc_hi
            xc_lo logits_out logits route shifted ex w_head w_cat wT_out wT gate up wb act gated h h_hi h_lo y_out y yT
            result stored residual""".split()}
        block = ctx.enter_context(nc.Block())
        ROUTE = 11

        def weight_tile(k):
            return k * E // PURE if k < PURE else E + k - PURE

        @block.sync
        def _(q):
            q.dma_start(w_route[:, :], io["w_route1"]).then_inc(sg["small"], 16)
            q.dma_start(tri[:, :], io["tri"]).then_inc(sg["small"], 16)
            q.dma_start(act[0:2 * E, :, :].rearrange("p a n -> p (a n)")[:, 0:PICK], io["pick_1"]).then_inc(sg["pick_in"], 16)
            q.dma_start(raw[:, 0, :], io["w1_1"][:, first]).then_inc(sg["w1a"], 16)
            q.dma_start(raw[:, 1, :], io["w3_1"][:, first]).then_inc(sg["w3a"], 16)
            q.wait_ge(sg["lo_vec"], 1)
            q.dma_start(raw[:, 0, :], io["w2_1"][:, first]).then_inc(sg["w2a"], 16)
            q.wait_ge(sg["lo_vec"], 2)
            q.dma_start(raw[:, 1, :], io["w3_1"][:, last]).then_inc(sg["w3b"], 16)
            q.wait_ge(sg["lo_pool"], 1)
            q.dma_start(raw[:, 0, :], io["w1_1"][:, last]).then_inc(sg["w1b"], 16)
            q.wait_ge(sg["lo_vec"], 3)
            q.dma_start(raw[:, 1, :], io["w2_1"][:, last]).then_inc(sg["w2b"], 16)

            def step(g, par):
                q.wait_ge(sg["result"], g + 1)
                if has(g - 1):
                    q.wait_ge(sg["stored"], rise(g - 1, 15, 16))
                q.dma_start(io["out"][bass.ds(GB * g, GB), :, :].rearrange("b n d -> n b d"),
                            x2_sb[:, bass.ds(GB * g, GB), :]).then_inc(sg["stored"], 16)

            over_groups(q, step)
            q.wait_ge(sg["stored"], 16 * NG)

        @block.tensor
        def _(t):
            def transpose_in(g):
                t.wait_ge(sg["xn"], g + 1)
                if has(g - 1):
                    t.wait_ge(sg["wT"], g)
                if has(g - 2):
                    t.wait_ge(sg["result"], g - 1)
                for b in range(GB):
                    i = t.transpose(p_front[:, bass.ts(b, N)], xn[:, b, :], c["ident"][:, :])
                i.then_inc(sg["xT"], 1)

            def route(g):
                t.wait_ge(sg["xc"], g + 1)
                t.wait_ge(sg["xc_hi"], g + 1)
                for b in range(GB):
                    i = t.matmul(p_front[:, b * E:(b + 1) * E], xc[:, bass.ts(b, N)], w_route[:, :], start=True, stop=True)
                i.then_inc(sg["logits_out"], 1)

            def weights_in(g):
                t.wait_ge(sg["w_cat"], g + 1)
                t.wait_ge(sg["logits"], g + 1)
                if has(g - 2):
                    t.wait_ge(sg["result"], g - 1)
                for b in range(GB):
                    i = t.transpose(p_front[0:2 * E, bass.ts(b, N)], f(w_cat[:, b, :]), c["ident"][:, :])
                i.then_inc(sg["wT_out"], 1)

            def transpose_back(g):
                t.wait_ge(sg["y"], g + 1)
                if has(g + 1):
                    t.wait_ge(sg["wT"], g + 2)
                for b in range(GB):
                    i = t.transpose(p_front[:, bass.ts(b, N)], y[:, bass.ts(b, N)], c["ident"][:, :])
                i.then_inc(sg["yT"], 1)

            def out_product(g, par, k):
                if k == 0:
                    if has(g - 1):
                        t.wait_ge(sg["y"], g)
                    else:
                        t.wait_ge(sg["lo_pool"], 1)
                if k == NT // 2 and not has(g - 1):
                    t.wait_ge(sg["lo_vec"], 5)
                t.wait_ge(sg["h_hi"], rise(g, k, NT))
                t.wait_ge(sg["h_lo"], rise(g, k, NT))
                r = (par * NT + k) % RING
                mm3(t, p_y[:, :], w2_hi[:, bass.ts(k, 128)], w2_lo[:, bass.ts(k, 128)],
                    h_hi[:, r, :], h_lo[:, r, :], start=k == 0, stop=k == NT - 1).then_inc(sg["y_out"], 1)

            def step(g, par):
                for k in range(NT):
                    if k == 0:
                        t.wait_ge(sg["xc_hi"], g + 1)
                        t.wait_ge(sg["xc_lo"], g + 1)
                        if not has(g - 1):
                            t.wait_ge(sg["lo_vec"], 2)
                    if k == NT // 2 and not has(g - 1):
                        t.wait_ge(sg["lo_vec"], 4)
                    cols = bass.ts(k, 128)
                    if reached(g, k - 2, NT):
                        t.wait_ge(sg["act"], rise(g, k - 2, NT))
                    mm3(t, p_gate[k % 2][:, :], w1_hi[:, cols], w1_lo[:, cols],
                        xc_hi[:, par, :], xc_lo[:, par, :]).then_inc(sg["gate"], 1)
                    if reached(g, k - 2, NT):
                        t.wait_ge(sg["gated"], rise(g, k - 2, NT))
                    mm3(t, p_up[k % 2][:, :], w3_hi[:, cols], w3_lo[:, cols],
                        xc_hi[:, par, :], xc_lo[:, par, :]).then_inc(sg["up"], 1)
                    if k == 0:
                        if not has(g - 1):
                            weights_in(0)
                        t.wait_ge(sg["wT"], g + 1)
                    if k == 0 or weight_tile(k) != weight_tile(k - 1):
                        n = weight_tile(k)
                        reader = k - 2 if k == 0 or k > PURE else k - 3
                        if reached(g, reader, NT):
                            t.wait_ge(sg["h"], rise(g, reader, NT))
                        t.matmul(p_wb[n % 2][:, :], pick[:, bass.ts(n, 128)], wT[:, par, :],
                                 start=True, stop=True).then_inc(sg["wb"], 1)
                    if k >= LAG:
                        out_product(g, par, k - LAG)
                    elif has(g - 1):
                        out_product(g - 1, 1 - par, k - LAG + NT)
                    if k == 4 and has(g - 1):
                        transpose_back(g - 1)
                    if has(g + 1):
                        if k == 7:
                            transpose_in(g + 1)
                        if k == 10:
                            route(g + 1)
                        if k == 18:
                            weights_in(g + 1)

            transpose_in(0)
            t.wait_ge(sg["small"], 32)
            route(0)
            t.wait_ge(sg["pick"], 1)
            over_groups(t, step)
            for k in range(NT - LAG, NT):
                out_product(NG - 1, 1, k)
            transpose_back(NG - 1)

        @block.scalar
        def _(a):
            def evacuate_in(g, par):
                a.wait_ge(sg["xT"], g + 1)
                if has(g - 1):
                    a.wait_ge(sg["logits_out"], g)
                a.activation(xc[:, :], p_front[:, :], ACT.Copy, scale=c["col"]("ln2")).then_inc(sg["xc"], 1)
                if reached(g, -NT - 1, NT):
                    a.wait_ge(sg["up"], rise(g, -NT - 1, NT))
                a.activation(xc_hi[:, par, :], p_front[:, :], ACT.Copy, scale=c["col"]("ln2")).then_inc(sg["xc_hi"], 1)

            def exponent(g):
                a.wait_ge(sg["shifted"], rise(g, 0, 1))
                if has(g - 1):
                    a.wait_ge(sg["w_cat"], g)
                a.activation(ex[:, :, :], logits[:, :, :], ACT.Exp).then_inc(sg["ex"], 1)

            def weights_in(g, par):
                a.wait_ge(sg["wT_out"], g + 1)
                if reached(g, -NWB - 1, NWB):
                    a.wait_ge(sg["wb"], rise(g, -NWB - 1, NWB))
                a.activation(wT[:, par, :], p_front[0:2 * E, :], ACT.Copy).then_inc(sg["wT"], 1)

            def evacuate_y(g):
                a.wait_ge(sg["y_out"], rise(g, NT - 1, NT))
                if has(g - 1):
                    a.wait_ge(sg["yT"], g)
                a.activation(y[:, :], p_y[:, :], ACT.Copy).then_inc(sg["y"], 1)

            def head(g, par, k):
                a.wait_ge(sg["h"], rise(g, k, NT))
                if reached(g, k - RING, NT):
                    a.wait_ge(sg["y_out"], rise(g, k - RING, NT))
                a.activation(h_hi[:, (par * NT + k) % RING, :], h[:, (2 * par + k) % 4, :], ACT.Copy).then_inc(sg["h_hi"], 1)

            def weight_head(name, hi, slot, cols):
                a.wait_ge(sg[name], 16)
                a.activation(hi[:, cols], raw[:, slot, :], ACT.Copy).then_inc(sg["hi"], 1)

            def step(g, par):
                for k in range(NT):
                    a.wait_ge(sg["gate"], rise(g, k, NT))
                    if reached(g, k - 4, NT):
                        a.wait_ge(sg["h"], rise(g, k - 4, NT))
                    a.activation(act[:, (2 * par + k) % 4, :], p_gate[k % 2][:, :], ACT.Silu).then_inc(sg["act"], 1)
                    if k == 0 and not has(g - 1):
                        weights_in(0, 0)
                        weight_head("w3b", w3_hi, 1, last)
                    if k >= 2 or has(g - 1):
                        head(g, par, k - 2)
                    if k == 2 and not has(g - 1):
                        weight_head("w1b", w1_hi, 0, last)
                    if k == 5 and not has(g - 1):
                        weight_head("w2b", w2_hi, 1, last)
                    if k == 3 and has(g - 1):
                        evacuate_y(g - 1)
                    if has(g + 1):
                        if k == 8:
                            evacuate_in(g + 1, 1 - par)
                        if k == 14:
                            exponent(g + 1)
                        if k == 19:
                            weights_in(g + 1, 1 - par)

            weight_head("w1a", w1_hi, 0, first)
            evacuate_in(0, 0)
            weight_head("w3a", w3_hi, 1, first)
            weight_head("w2a", w2_hi, 0, first)
            exponent(0)
            over_groups(a, step)
            head(NG, 0, -2)
            head(NG, 0, -1)
            evacuate_y(NG - 1)

        @block.vector
        def _(v):
            def front_norm(g):
                v.wait_ge(sg["rstd_step"], rise(g, 3, 4))
                if has(g - 1):
                    v.wait_ge(sg["xT"], g)
                for b in range(GB):
                    i = v.tensor_scalar(xn[:, b, :], x2_sb[:, bass.ds(GB * g + b, 1), :].rearrange("p a d -> p (a d)"),
                                        rstd[:, b:b + 1], None, ALU.mult)
                i.then_inc(sg["xn"], 1)

            def residual(g):
                xg = x2_sb[:, bass.ds(GB * g, GB), :]
                v.wait_ge(sg["xn"], g + 1)
                v.tensor_tensor(xg, xg, x_sb[:, bass.ds(GB * g, GB), :], ALU.add).then_inc(sg["residual"], 1)

            def split_in(g, par):
                v.wait_ge(sg["xc"], g + 1)
                v.wait_ge(sg["xc_hi"], g + 1)
                v.tensor_tensor(xc_lo[:, par, :], xc[:, :], f(xc_hi[:, par, :]), ALU.subtract).then_inc(sg["xc_lo"], 1)

            def rank_experts(g):
                v.wait_ge(sg["logits_out"], g + 1)
                v.tensor_copy(logits[:, :, :], p_front[:, 0:GB * E].rearrange("p (b e) -> p b e", b=GB)).then_inc(sg["logits"], 1)
                v.wait_ge(sg["logits"], g + 1)
                ranks(v, sg["route"], g, 0, ROUTE, logits[:, :, :], gt[:, :, :, :], eq[:, :, :, :],
                      rank[:, :, :], tri[:, :].rearrange("p (e j) -> p e j", e=E).unsqueeze(1).to_broadcast([128, GB, E, E]))

            def below_top(g):
                v.tensor_reduce(top[:, :], logits[:, :, :], AX.X, ALU.max, negate=True).then_inc(sg["route"], 1)
                v.wait_ge(sg["route"], rise(g, 4, ROUTE))
                v.tensor_tensor(logits[:, :, :], logits[:, :, :], along(top[:, :], [128, GB, E]), ALU.add).then_inc(sg["shifted"], 1)

            def shares(g):
                v.wait_ge(sg["ex"], g + 1)
                v.tensor_reduce(total[:, :], ex[:, :, :], AX.X, ALU.add)
                v.tensor_scalar(chosen[:, :, :], rank[:, :, :], 2.0, None, ALU.is_lt).then_inc(sg["route"], 1)
                v.wait_ge(sg["route"], rise(g, 5, ROUTE))
                v.tensor_tensor(share[:, :, :], ex[:, :, :], chosen[:, :, :], ALU.mult).then_inc(sg["route"], 1)
                v.wait_ge(sg["route"], rise(g, 6, ROUTE))
                v.tensor_reduce(kept[:, :], share[:, :, :], AX.X, ALU.add).then_inc(sg["route"], 1)
                v.wait_ge(sg["route"], rise(g, 7, ROUTE))
                v.scalar_tensor_tensor(kept[:, :], total[:, :], 1e-9, kept[:, :], ALU.mult, ALU.add).then_inc(sg["route"], 1)
                v.wait_ge(sg["route"], rise(g, 8, ROUTE))
                v.reciprocal(kept[:, :], kept[:, :]).then_inc(sg["route"], 1)
                v.wait_ge(sg["route"], rise(g, 9, ROUTE))
                v.tensor_tensor(share[:, :, :], share[:, :, :], along(kept[:, :], [128, GB, E]), ALU.mult).then_inc(sg["route"], 1)
                v.wait_ge(sg["route"], rise(g, 10, ROUTE))
                if has(g - 1):
                    v.wait_ge(sg["wT_out"], g)
                v.tensor_copy(w_cat[:, :, 0:E], share[:, :, :]).then_inc(sg["w_head"], 1)
                v.wait_ge(sg["w_head"], g + 1)
                v.tensor_tensor(w_cat[:, :, E:2 * E], share[:, :, :], f(w_cat[:, :, 0:E]), ALU.subtract).then_inc(sg["w_cat"], 1)

            def finish(g):
                v.wait_ge(sg["yT"], g + 1)
                v.wait_ge(sg["residual"], g + 1)
                xg = x2_sb[:, bass.ds(GB * g, GB), :]
                v.tensor_tensor(xg, xg, four(p_front[:, :]), ALU.add).then_inc(sg["result"], 1)

            def weight_rest(n, lo, hi, slot, cols):
                v.wait_ge(sg["hi"], n)
                v.tensor_tensor(lo[:, cols], raw[:, slot, :], f(hi[:, cols]), ALU.subtract).then_inc(sg["lo_vec"], 1)

            def step(g, par):
                for k in range(NT):
                    v.wait_ge(sg["act"], rise(g, k, NT))
                    v.wait_ge(sg["up"], rise(g, k, NT))
                    r = (2 * par + k) % 4
                    v.tensor_tensor(act[:, r, :], act[:, r, :], p_up[k % 2][:, :], ALU.mult).then_inc(sg["gated"], 1)
                    v.wait_ge(sg["gated"], rise(g, k, NT))
                    v.wait_ge(sg["wb"], rise(g, weight_tile(k), NWB))
                    if reached(g, k - 4, NT):
                        v.wait_ge(sg["h_lo"], rise(g, k - 4, NT))
                    v.tensor_tensor(h[:, r, :], act[:, r, :], p_wb[weight_tile(k) % 2][:, :], ALU.mult).then_inc(sg["h"], 1)
                    if k == 1 and not has(g - 1):
                        weight_rest(4, w3_lo, w3_hi, 1, last)
                    if k == 3 and not has(g - 1):
                        weight_rest(5, w1_lo, w1_hi, 0, last)
                    if k == 6 and not has(g - 1):
                        weight_rest(6, w2_lo, w2_hi, 1, last)
                    if k == 5 and has(g - 1):
                        finish(g - 1)
                    if has(g + 1):
                        if k == 1:
                            layer_norm_stats(v, sg, x2_sb, g + 1, stats, mv)
                        if k == 4:
                            front_norm(g + 1)
                        if k == 6:
                            residual(g + 1)
                        if k == 9:
                            split_in(g + 1, 1 - par)
                        if k == 11:
                            rank_experts(g + 1)
                        if k == 12:
                            below_top(g + 1)
                        if k == 15:
                            shares(g + 1)

            layer_norm_stats(v, sg, x2_sb, 0, stats, mv)
            v.wait_ge(sg["pick_in"], 16)
            v.tensor_copy(pick[:, :], act[0:2 * E, :, :].rearrange("p a n -> p (a n)")[:, 0:PICK]).then_inc(sg["pick"], 1)
            front_norm(0)
            residual(0)
            weight_rest(1, w1_lo, w1_hi, 0, first)
            split_in(0, 0)
            v.wait_ge(sg["small"], 32)
            rank_experts(0)
            below_top(0)
            weight_rest(2, w3_lo, w3_hi, 1, first)
            shares(0)
            over_groups(v, step)
            finish(NG - 1)

        @block.gpsimd
        def _(p):
            def scales(g):
                p.wait_ge(sg["mean_var"], g + 1)
                p.tensor_tensor(rstd[:, :], mv[:, 0, :], mv[:, 0, :], ALU.mult).then_inc(sg["rstd_step"], 1)
                p.wait_ge(sg["rstd_step"], rise(g, 0, 4))
                p.tensor_tensor(rstd[:, :], rstd[:, :], mv[:, 1, :], ALU.add).then_inc(sg["rstd_step"], 1)
                p.wait_ge(sg["rstd_step"], rise(g, 1, 4))
                p.tensor_tensor(rstd[:, :], rstd[:, :], c["rms_eps"][:, 0:GB], ALU.add).then_inc(sg["rstd_step"], 1)
                p.wait_ge(sg["rstd_step"], rise(g, 2, 4))
                p.tensor_tensor(rstd[:, :], rstd[:, :], c["minus_half"][:, 0:GB], ALU.pow).then_inc(sg["rstd_step"], 1)

            def step(g, par):
                for k in range(NT):
                    p.wait_ge(sg["h_hi"], rise(g, k, NT))
                    if reached(g, k - RING, NT):
                        p.wait_ge(sg["y_out"], rise(g, k - RING, NT))
                    r = (par * NT + k) % RING
                    p.tensor_tensor(h_lo[:, r, :], h[:, r, :], f(h_hi[:, r, :]), ALU.subtract).then_inc(sg["h_lo"], 1)
                    if k == 2 and has(g + 1):
                        scales(g + 1)

            scales(0)
            p.wait_ge(sg["hi"], 3)
            p.tensor_tensor(w2_lo[:, first], raw[:, 0, :], f(w2_hi[:, first]), ALU.subtract).then_inc(sg["lo_pool"], 1)
            over_groups(p, step)


def constants(nc, ctx, io):
    def sb(name, shape, dt=F32):
        return ctx.enter_context(nc.sbuf_tensor(name, shape, dt))

    ident, cols, minus_half = sb("ident", [128, 128]), sb("cols", [128, NCOL]), sb("minus_half", [128, 8])
    ln_eps, rms_eps = sb("ln_eps", [128, GB]), sb("rms_eps", [128, GB])
    loaded = ctx.enter_context(nc.semaphore("const_loaded"))
    with nc.Block() as block:
        @block.sync
        def _(q):
            q.dma_start(ident[:, :], io["ident"]).then_inc(loaded, 16)
            q.dma_start(cols[:, :], io["cols"]).then_inc(loaded, 16)
            q.wait_ge(loaded, 32)

        @block.gpsimd
        def _(p):
            p.memset(minus_half[:, :], -0.5)
            p.memset(ln_eps[:, :], LN_EPS)
            p.memset(rms_eps[:, :], RMS_EPS)

    def col(name):
        i = COL[name] if isinstance(name, str) else len(COLS) + name
        return cols[:, i:i + 1]

    return {"ident": ident, "minus_half": minus_half, "ln_eps": ln_eps, "rms_eps": rms_eps, "col": col}


def program(nc, io):
    with ExitStack() as ctx:
        x_sb = ctx.enter_context(nc.sbuf_tensor("x_sb", [128, B, D], F32))
        c = constants(nc, ctx, io)
        layer0_gnn(nc, io, x_sb, c)
        layer0_ffn(nc, io, x_sb, c)
        layer1_gnn(nc, io, x_sb, c)
        x2_sb = ctx.enter_context(nc.sbuf_tensor("x2_sb", [128, B, D], F32))
        layer1_attention(nc, io, x_sb, x2_sb, c)
        layer1_ffn(nc, io, x_sb, x2_sb, c)


def laid_out(a):
    A = {k: np.asarray(v) for k, v in a.items()}
    rows = lambda m: np.ascontiguousarray(m)
    p = "L0_gnn_"
    w_ih, w_hh = A[p + "w_ih"], A[p + "w_hh"]
    small = [A[p + "conv1_w"][:, :, 0].T]
    small += [w_ih[k * D:(k + 1) * D, :D].T for k in range(3)]
    small += [w_ih[k * D:(k + 1) * D, D:].T for k in range(3)]
    small += [w_hh[k * D:(k + 1) * D].T for k in range(3)]
    bi, bh = A[p + "b_ih"].reshape(3, D), A[p + "b_hh"].reshape(3, D)
    cols = [A[p + n] for n in ("bn1_g", "bn1_b", "bn1_m", "bn1_v", "bn2_g", "bn2_b", "bn2_m", "bn2_v")]
    cols += [bi[0], bi[1], bi[2], bh[0], bh[1], bh[2], A["L0_ffn_gamma"], A["L0_ffn_beta"],
             A["L1_ffn_ln1_w"], A["L1_ffn_ln2_w"]]
    cols += list(A["L0_ffn_b1"].reshape(2 * E, 128))
    out = {
        "x": A["x"], "adj": A["adj"],
        "ident": np.eye(128, dtype=np.float32),
        "cols": rows(np.stack(cols, axis=1)),
        "small0": rows(np.concatenate(small, axis=1)),
        "conv2": rows(A[p + "conv2_w"].transpose(1, 2, 0).reshape(D, TAPS * D)),
        "w_msg": rows(A[p + "w_msg"].T), "b_msg": rows(np.broadcast_to(A[p + "b_msg"], (128, D))),
        "w_se": rows(A[p + "w_se"].T), "b_se": rows(A[p + "b_se"].reshape(3, 1)),
    }
    out.update(more(A, rows))
    return out


def more(A, rows):
    eye = np.eye(E, dtype=np.float32)
    q = "L0_ffn_"
    w1_0 = A[q + "W1"].transpose(1, 0, 2).reshape(D, E * H0)
    w2_0 = A[q + "W2"].reshape(2 * E, 128, D).transpose(1, 0, 2).reshape(128, 2 * E * D)
    freq = 1.0 / 10000.0 ** (np.arange(0, 32, 2, dtype=np.float32) / 32)
    angle = np.outer(np.arange(N, dtype=np.float32), freq)
    angle = np.concatenate([angle, angle], axis=-1).T
    sign = np.concatenate([-np.ones(16, np.float32), np.ones(16, np.float32)])[:, None]
    r = "L1_ffn_"
    swap = (np.arange(128) // 32) * 32 + (np.arange(128) % 32 + 16) % 32
    wq, wk = A[r + "wq"], np.repeat(A[r + "wk"].reshape(2, 32, D), 2, axis=0).reshape(D, D)
    s = "L1_gnn_"
    pure, rest = HID // 128 * 128, HID % 128
    order = np.concatenate([np.arange(pure) + HID * e for e in range(E)] +
                           [np.arange(rest) + HID * e + pure for e in range(E)] + [np.arange(NT * 128 - HALL)])
    packed = lambda w: w.reshape(HALL, D)[order]
    pick = np.concatenate([np.repeat(eye, 128, axis=1), np.repeat(eye, rest, axis=1),
                           np.zeros((E, NT * 128 - HALL), np.float32)], axis=1)
    w2 = packed(A[r + "w2"].transpose(0, 2, 1)).reshape(NT, 128, D).transpose(1, 0, 2).reshape(128, NT * D)
    return {
        "w1_1": rows(packed(A[r + "w1"]).T), "w3_1": rows(packed(A[r + "w3"]).T), "w2_1": rows(w2),
        "pick_1": rows(np.concatenate([pick, pick], axis=0)), "w_route1": rows(A[r + "router_w"].T),
        "proj0": rows(np.concatenate([A[s + "W_q"].T, A[s + "W_k"].T], axis=1)),
        "w_v0": rows(A[s + "W_v"].T), "w_o0": rows(A[s + "W_o"].T),
        "w_edge": rows(np.broadcast_to(A[s + "W_e"].reshape(8), (128, 8))),
        "proj1": rows(np.concatenate([wq.T, wq[swap].T, wk.T, wk[swap].T], axis=1)),
        "w_v1": rows(A[r + "wv"].T), "w_o1": rows(A[r + "wo"].T),
        "cos": rows(np.tile(np.cos(angle), (4, 1))), "sin": rows(np.tile(np.sin(angle) * sign, (4, 1))),
        "causal": rows(np.triu(np.full((N, N), NEG, np.float32), 1)),
        "w1_0": rows(w1_0), "w2_0": rows(w2_0), "b2_0": rows(np.concatenate([A[q + "b2"]] * 2, axis=0)),
        "pick_0": rows(np.repeat(np.concatenate([eye, eye], axis=0), 128, axis=1)),
        "w_route0": rows(A[q + "Wr"]), "b_route0": rows(np.broadcast_to(A[q + "br"], (128, E))),
        "tri": rows(np.broadcast_to(np.tri(E, k=-1, dtype=np.float32).reshape(E * E), (128, E * E))),
    }


def kernel(**inputs):
    import concourse.bacc as bacc
    from concourse.bass_utils import run_bass_kernel_spmd as run

    arrays = laid_out(inputs)
    nc = bacc.Bacc("TRN2", target_bir_lowering=False, num_devices=1)
    io = {
        n: nc.dram_tensor("in_" + n, a.shape, mybir.dt.from_np(a.dtype), kind="ExternalInput").ap()
        for n, a in arrays.items()}
    io["out"] = nc.dram_tensor("out", (B, N, D), F32, kind="ExternalOutput").ap()
    program(nc, io)
    r = run(nc, [{"in_" + n: a for n, a in arrays.items()}], core_ids=[0])
    return r.results[0]["out"]
```
